# Optimizing a Trainium2 kernel written in Bass

```python
import numpy as np
import jax
import jax.numpy as jnp

def _softmax(x, axis=-1):
    return jax.nn.softmax(x, axis=axis)

def _gelu(x):
    return jax.nn.gelu(x, approximate=True)

def _silu(x):
    return jax.nn.silu(x)

def _sigmoid(x):
    return jax.nn.sigmoid(x)

def _layernorm(x, axis=-1, eps=1e-05):
    m = jnp.mean(x, axis=axis, keepdims=True)
    v = jnp.var(x, axis=axis, keepdims=True)
    return (x - m) / jnp.sqrt(v + eps)

def _scatter_add(tgt, idx, src, axis=0):
    return tgt.at[idx].add(src)

def _segment_sum(src, seg, n):
    return jax.ops.segment_sum(src, seg, n)
kernel_name = 'mk_gps_d1_gnn_r32_3998d0'

def setup_inputs(seed: int=0):
    np.random.seed(seed)
    _w = jnp.asarray

    def _rec_inputs():
        import jax
        import jax.numpy as jnp
        _gk = jax.random.key(seed)
        x = -0.003407 + 1.001 * jax.random.normal(jax.random.fold_in(_gk, 1), (3125, 256), jnp.float32)
        src = jax.random.randint(jax.random.fold_in(_gk, 2), (50000,), 0, 3125, jnp.int32)
        dst = jnp.minimum((3125 * jax.random.uniform(jax.random.fold_in(_gk, 3), (50000,)) ** 2.0).astype(jnp.int32), 99999)
        _o = jnp.argsort(dst, stable=True)
        src = src[_o]
        dst = dst[_o]
        edge_weight1 = jax.random.uniform(jax.random.fold_in(_gk, 12), (50000, 1), jnp.float32, 0.0, 1)
        return (x, src, dst, edge_weight1)
    x, src, dst, edge_weight1 = _rec_inputs()

    def _L0_gnn_setup():
        import jax, jax.numpy as jnp
        import numpy as np
        BS = 512
        EMBED = 256
        NHEAD = 8
        HDIM = EMBED // NHEAD
        E = BS * BS

        def _xavier(key, shape):
            lim = float(np.sqrt(6.0 / (shape[0] + shape[1])))
            return jax.random.uniform(key, shape, jnp.float32, -lim, lim)
        key = jax.random.key(seed)
        ks = jax.random.split(key, 6)
        feats = jax.random.normal(ks[0], (BS, EMBED), jnp.float32)
        dst = jnp.repeat(jnp.arange(BS), BS)
        src = jnp.tile(jnp.arange(BS), BS)
        edge_index = jnp.stack([src, dst], axis=1).astype(jnp.int32)
        edge_attr = jnp.zeros((E, 1), jnp.float32)
        return {'feats': feats, 'edge_index': edge_index, 'edge_attr': edge_attr, 'Wq': _xavier(ks[1], (EMBED, EMBED)), 'bq': jnp.zeros((EMBED,), jnp.float32), 'Wk': _xavier(ks[2], (EMBED, EMBED)), 'bk': jnp.zeros((EMBED,), jnp.float32), 'Wv': _xavier(ks[3], (EMBED, EMBED)), 'bv': jnp.zeros((EMBED,), jnp.float32), 'Wo': _xavier(ks[4], (EMBED, EMBED)), 'bo': jnp.zeros((EMBED,), jnp.float32)}
    _L0_gnn_all = _L0_gnn_setup()
    _L0_gnn_in = {k: v for k, v in _L0_gnn_all.items() if k in ('Wq', 'bq', 'Wk', 'bk', 'Wv', 'bv', 'Wo', 'bo')}
    del _L0_gnn_all

    def _L0_mix_setup():
        import jax, jax.numpy as jnp
        import numpy as np
        DIM = 256
        HEADS = 4
        DIM_HEAD = 32
        NUM_MEM = 4
        HIDDEN = HEADS * DIM_HEAD
        SCALE = DIM_HEAD ** (-0.5)

        def rmsnorm(x, g):
            n = jnp.linalg.norm(x, axis=-1, keepdims=True)
            return x / jnp.maximum(n, 1e-12) * g * x.shape[-1] ** 0.5
        key = jax.random.key(seed)
        ks = jax.random.split(key, 8)
        B, N = (4, 512)
        return {'x': jax.random.normal(ks[0], (B, N, DIM), jnp.float32), 't': jax.random.normal(ks[1], (B,), jnp.float32), 'w_qkv': jax.random.normal(ks[2], (DIM, 3 * HIDDEN), jnp.float32) * 0.02, 'mem_kv': jax.random.normal(ks[3], (2, HEADS, DIM_HEAD, NUM_MEM), jnp.float32), 'w_out': jax.random.normal(ks[4], (HIDDEN, DIM), jnp.float32) * 0.02, 'b_out': jnp.zeros((DIM,), jnp.float32), 'g_out': jnp.ones((DIM,), jnp.float32), 'g_pre': jnp.ones((DIM,), jnp.float32)}
    _L0_mix_all = _L0_mix_setup()
    _L0_mix_in = {k: v for k, v in _L0_mix_all.items() if k in ('t', 'w_qkv', 'mem_kv', 'w_out', 'b_out', 'g_out', 'g_pre')}
    del _L0_mix_all

    def _L0_ffn_setup():
        import math
        import jax, jax.numpy as jnp
        import numpy as np
        CAPACITY_FACTOR = 1.25
        key = jax.random.key(seed)
        ks = jax.random.split(key, 5)
        B, L, D, F, E = (8, 256, 256, 1024, 8)
        h = jax.random.normal(ks[0], (B, L, D), dtype=jnp.float32)
        gate_w = jax.random.normal(ks[1], (D, E), dtype=jnp.float32) * 0.02
        gate_b = jnp.zeros((E,), dtype=jnp.float32)
        w1 = jax.random.normal(ks[2], (E, D, F), dtype=jnp.float32) * (1.0 / math.sqrt(D))
        b1 = jnp.zeros((E, F), dtype=jnp.float32)
        w2 = jax.random.normal(ks[3], (E, F, D), dtype=jnp.float32) * (1.0 / math.sqrt(F))
        b2 = jnp.zeros((E, D), dtype=jnp.float32)
        return {'h': h, 'gate_w': gate_w, 'gate_b': gate_b, 'w1': w1, 'b1': b1, 'w2': w2, 'b2': b2}
    _L0_ffn_all = _L0_ffn_setup()
    _L0_ffn_in = {k: v for k, v in _L0_ffn_all.items() if k in ('gate_w', 'gate_b', 'w1', 'b1', 'w2', 'b2')}
    del _L0_ffn_all
    return {'x': x, 'src': src, 'dst': dst, 'edge_weight1': edge_weight1, 'L0_gnn_Wq': _L0_gnn_in['Wq'], 'L0_gnn_bq': _L0_gnn_in['bq'], 'L0_gnn_Wk': _L0_gnn_in['Wk'], 'L0_gnn_bk': _L0_gnn_in['bk'], 'L0_gnn_Wv': _L0_gnn_in['Wv'], 'L0_gnn_bv': _L0_gnn_in['bv'], 'L0_gnn_Wo': _L0_gnn_in['Wo'], 'L0_gnn_bo': _L0_gnn_in['bo'], 'L0_mix_t': _L0_mix_in['t'], 'L0_mix_w_qkv': _L0_mix_in['w_qkv'], 'L0_mix_mem_kv': _L0_mix_in['mem_kv'], 'L0_mix_w_out': _L0_mix_in['w_out'], 'L0_mix_b_out': _L0_mix_in['b_out'], 'L0_mix_g_out': _L0_mix_in['g_out'], 'L0_mix_g_pre': _L0_mix_in['g_pre'], 'L0_ffn_gate_w': _L0_ffn_in['gate_w'], 'L0_ffn_gate_b': _L0_ffn_in['gate_b'], 'L0_ffn_w1': _L0_ffn_in['w1'], 'L0_ffn_b1': _L0_ffn_in['b1'], 'L0_ffn_w2': _L0_ffn_in['w2'], 'L0_ffn_b2': _L0_ffn_in['b2']}

def reference(x, src, dst, edge_weight1, L0_gnn_Wq, L0_gnn_bq, L0_gnn_Wk, L0_gnn_bk, L0_gnn_Wv, L0_gnn_bv, L0_gnn_Wo, L0_gnn_bo, L0_mix_t, L0_mix_w_qkv, L0_mix_mem_kv, L0_mix_w_out, L0_mix_b_out, L0_mix_g_out, L0_mix_g_pre, L0_ffn_gate_w, L0_ffn_gate_b, L0_ffn_w1, L0_ffn_b1, L0_ffn_w2, L0_ffn_b2):
    import jax
    import jax.numpy as jnp

    def _L0_gnn_ref(feats, edge_index, edge_attr, Wq, bq, Wk, bk, Wv, bv, Wo, bo):
        import jax, jax.numpy as jnp
        import numpy as np
        BS = 512
        EMBED = 256
        NHEAD = 8
        HDIM = EMBED // NHEAD
        E = BS * BS

        def _xavier(key, shape):
            lim = float(np.sqrt(6.0 / (shape[0] + shape[1])))
            return jax.random.uniform(key, shape, jnp.float32, -lim, lim)
        bs = feats.shape[0]
        scale = 1.0 / np.sqrt(HDIM)
        q = (feats @ Wq.T + bq).reshape(bs, NHEAD, HDIM).transpose(1, 0, 2)
        k = (feats @ Wk.T + bk).reshape(bs, NHEAD, HDIM).transpose(1, 0, 2)
        v = (feats @ Wv.T + bv).reshape(bs, NHEAD, HDIM).transpose(1, 0, 2)
        r, c = (edge_index[:, 0], edge_index[:, 1])
        qe = q[:, c, :]
        ke = k[:, r, :]
        ve = v[:, r, :]
        sim = jnp.einsum('hed,hed->eh', qe, ke) * scale
        m = jax.ops.segment_max(sim, c, num_segments=bs)
        p = jnp.exp(sim - m[c])
        s = jax.ops.segment_sum(p, c, num_segments=bs)
        attn = p / s[c]
        out_e = attn.T[..., None] * ve
        out_e = out_e.transpose(1, 0, 2).reshape(-1, NHEAD * HDIM)
        agg = jax.ops.segment_sum(out_e, c, num_segments=bs)
        return agg @ Wo.T + bo

    def _L0_mix_ref(x, t, w_qkv, mem_kv, w_out, b_out, g_out, g_pre):
        import jax, jax.numpy as jnp
        import numpy as np
        DIM = 256
        HEADS = 4
        DIM_HEAD = 32
        NUM_MEM = 4
        HIDDEN = HEADS * DIM_HEAD
        SCALE = DIM_HEAD ** (-0.5)

        def rmsnorm(x, g):
            n = jnp.linalg.norm(x, axis=-1, keepdims=True)
            return x / jnp.maximum(n, 1e-12) * g * x.shape[-1] ** 0.5
        b, n, c = x.shape
        xn = rmsnorm(x, g_pre)
        qkv = xn @ w_qkv
        q, k, v = jnp.split(qkv, 3, axis=-1)

        def to_heads(z):
            return z.reshape(b, n, HEADS, DIM_HEAD).transpose(0, 2, 3, 1)
        q, k, v = map(to_heads, (q, k, v))
        mk = jnp.broadcast_to(mem_kv[0], (b, HEADS, DIM_HEAD, NUM_MEM))
        mv = jnp.broadcast_to(mem_kv[1], (b, HEADS, DIM_HEAD, NUM_MEM))
        k = jnp.concatenate([mk, k], axis=-1)
        v = jnp.concatenate([mv, v], axis=-1)
        q = jax.nn.softmax(q, axis=-2) * SCALE
        k = jax.nn.softmax(k, axis=-1)
        context = jnp.einsum('bhdn,bhen->bhde', k, v)
        out = jnp.einsum('bhde,bhdn->bhen', context, q)
        out = out.transpose(0, 3, 1, 2).reshape(b, n, HIDDEN)
        out = rmsnorm(out @ w_out + b_out, g_out)
        return out + x

    def _L0_ffn_ref(h, gate_w, gate_b, w1, b1, w2, b2):
        import math
        import jax, jax.numpy as jnp
        import numpy as np
        CAPACITY_FACTOR = 1.25
        B, L, D = h.shape
        E = gate_w.shape[1]
        T = B * L
        C = max(1, math.ceil(CAPACITY_FACTOR * T / E))
        x = h.reshape(T, D)
        logits = x @ gate_w + gate_b
        probs = jax.nn.softmax(logits, axis=-1)
        idx = jnp.argmax(probs, axis=-1)
        prb = jnp.take_along_axis(probs, idx[:, None], axis=1)[:, 0]
        one_hot = jax.nn.one_hot(idx, E, dtype=jnp.float32)
        pos = (jnp.cumsum(one_hot, axis=0) * one_hot).sum(-1).astype(jnp.int32) - 1
        kept = pos < C
        pos_safe = jnp.where(kept, pos, C)
        buf = jnp.zeros((E, C, D), dtype=h.dtype).at[idx, pos_safe].set(x, mode='drop')
        hmid = jax.nn.relu(jnp.einsum('ecd,edf->ecf', buf, w1) + b1[:, None, :])
        ybuf = jnp.einsum('ecf,efd->ecd', hmid, w2) + b2[:, None, :]
        pos_g = jnp.minimum(pos, C - 1)
        y_tok = ybuf[idx, pos_g] * (prb * kept)[:, None]
        y = y_tok.reshape(B, L, D)
        y = jnp.nan_to_num(y, nan=0.0, posinf=10000.0, neginf=-10000.0)
        return y
    edge_index_t = jnp.stack([src, dst], axis=1)
    xn = _layernorm(x, axis=-1)
    x = x + _L0_gnn_ref(xn, edge_index_t, edge_weight1, L0_gnn_Wq, L0_gnn_bq, L0_gnn_Wk, L0_gnn_bk, L0_gnn_Wv, L0_gnn_bv, L0_gnn_Wo, L0_gnn_bo) + _L0_mix_ref(xn[None], L0_mix_t, L0_mix_w_qkv, L0_mix_mem_kv, L0_mix_w_out, L0_mix_b_out, L0_mix_g_out, L0_mix_g_pre)[0]
    x = x + _L0_ffn_ref(_layernorm(x, axis=-1)[None], L0_ffn_gate_w, L0_ffn_gate_b, L0_ffn_w1, L0_ffn_b1, L0_ffn_w2, L0_ffn_b2)[0]
    return x

_drawn_inputs = setup_inputs


def setup_inputs(seed=0):
    import zlib

    import numpy as np

    out = dict(_drawn_inputs(seed))
    spreads = {'L0_gnn_bq': (0.0, 0.473),
     'L0_gnn_bk': (0.0, 0.8),
     'L0_gnn_bv': (0.0, 0.1),
     'L0_gnn_bo': (0.0, 0.1),
     'L0_mix_b_out': (0.0, 0.1),
     'L0_mix_g_out': (1.0, 0.2),
     'L0_mix_g_pre': (1.0, 0.6),
     'L0_ffn_gate_b': (0.0, 0.1),
     'L0_ffn_b1': (0.0, 0.8),
     'L0_ffn_b2': (0.0, 0.8)}
    factors = {'L0_mix_w_qkv': 8.0, 'L0_mix_mem_kv': 8.0, 'L0_mix_w_out': 8.0}
    for name, (base, spread) in spreads.items():
        noise = np.random.default_rng([zlib.crc32(name.encode()), seed]).standard_normal(out[name].shape)
        drawn = base * np.exp(spread * noise) if base else spread * noise
        out[name] = jnp.asarray(drawn.astype(out[name].dtype))
    for name, factor in factors.items():
        out[name] = (out[name] * factor).astype(out[name].dtype)
    return out
```

```python
import numpy as np
import concourse.bass as bass
from concourse import mybir
from contextlib import ExitStack

F32 = mybir.dt.float32
I32 = mybir.dt.int32
U32 = mybir.dt.uint32
BF16 = mybir.dt.bfloat16
ALU = mybir.AluOpType
ACT = mybir.ActivationFunctionType
X = mybir.AxisListType.X
PE_ONLY = [mybir.EngineType.PE]
DVE_ONLY = [mybir.EngineType.DVE]

N, D, E = 3125, 256, 50000
TT, NT = 125, 25
H, HD = 8, 32
MH, MD, MEM, HID = 4, 32, 4, 128
QKV = 3 * HID
WALL = 3 * D + QKV
EX, FF = 8, 1024
CAP = -(-5 * N // (4 * EX))
U = 16
EROWS = -(-(E // 128 + 1) // 8) * 8
STEPS = 416
CH = STEPS // U
TG, TP = 4, STEPS // 4
RG, RP = 4, EROWS // 4
SB = 16
SL = STEPS * 128 // SB
PAD_NODE = 4000.0
BIG = 1.0e30
RESET = 1.0e38
EPS = 1e-5
assert EROWS * 128 >= E and EROWS - 1 + NT <= STEPS and CAP == 489 and SL * SB == STEPS * 128


def spread(ap, axis, n):
    a = ap.unsqueeze(axis)
    shape = list(a.shape)
    shape[axis] = n
    return a.to_broadcast(shape)


def flat(ap):
    return ap.rearrange("p a b -> p (a b)")


def at(t, i):
    if isinstance(i, int):
        return t[:, i]
    a = t[:, bass.ds(i, 1)]
    return a.squeeze(1)


def wait(eng, sem, value):
    if isinstance(value, int) and value <= 0:
        return
    eng.wait_ge(sem, value)


class Steps:

    def __init__(self, sem):
        self.eng, self.sem, self.c = None, sem, 0

    def on(self, eng):
        self.eng = eng
        return self

    def then(self, ins):
        ins.then_inc(self.sem, 1)
        self.c += 1

    def settle(self):
        self.eng.wait_ge(self.sem, self.c)

    def link(self, ins):
        self.then(ins)
        self.settle()


def mean_and_var(dve, st, stats, mean, var, tmp):
    st.then(dve.tensor_tensor(mean, stats[:, :, 1], stats[:, :, 4], ALU.add))
    st.then(dve.tensor_tensor(tmp, stats[:, :, 1], stats[:, :, 4], ALU.subtract))
    st.link(dve.tensor_tensor(var, stats[:, :, 2], stats[:, :, 5], ALU.add))
    st.then(dve.tensor_scalar(mean, mean, 0.5, None, ALU.mult))
    st.then(dve.tensor_scalar(var, var, 1.0 / D, EPS, ALU.mult, ALU.add))
    st.link(dve.tensor_tensor(tmp, tmp, tmp, ALU.mult))
    return dve.scalar_tensor_tensor(out=var, in0=tmp, scalar=0.25, in1=var, op0=ALU.mult, op1=ALU.add)


def edge_tables(nc, m, io):
    with ExitStack() as ctx:
        def sb(n, s, d=F32):
            return ctx.enter_context(nc.sbuf_tensor(n, s, d))
        padd = sb("padd", [1, EROWS * 128 - E], I32)
        pads = sb("pads", [1, EROWS * 128 - E], I32)
        last_i = sb("last_i", [RP, RG, 2 * 128], I32)
        last_f = sb("last_f", [RP, RG])
        thr = sb("thr", [RP, NT - 1])
        junk = sb("junk", [RP, NT - 1])
        wend = sb("wend", [RP, RG])
        wfound = sb("wfound", [RP, RG])
        pen2 = sb("pen2", [128, STEPS])
        iota_i = sb("iota_i", [RP, STEPS])
        before = sb("before", [RP, RG, STEPS])
        ones = sb("ones_t", [RP, 1])
        step_no = sb("step_no", [TP, TG])
        row_no = sb("row_no", [TP, TG])
        row_i = sb("row_i", [TP, TG], I32)
        row_ib = sb("row_ib", [TP, TG], I32)
        win0 = sb("win0", [TP, TG])
        got = sb("got", [TP, TG, 2 * 128], I32)
        dst_f = sb("dst_f", [TP, TG, 128])
        src_f = sb("src_f", [TP, TG, 128])
        key = sb("key", [TP, TG, 128])
        loc16 = sb("loc16", [TP, TG, 128], BF16)
        drow = sb("drow", [1, STEPS])
        front = sb("front", [1, 1])
        back = sb("back", [1, 1])
        psl = ctx.enter_context(nc.psum_tensor("psl", [128, TG, 128], F32))
        pss = ctx.enter_context(nc.psum_tensor("pss", [128, TG, 128], F32))
        psr = ctx.enter_context(nc.psum_tensor("psr", [128, 512], F32))
        pst = ctx.enter_context(nc.psum_tensor("pst", [128, 512], F32))
        S = m.sem
        with nc.Block() as block:
            @block.sync
            def _(sp):
                full = E // 128
                e2 = m.edges.rearrange("r (c e) -> r c e", c=2)
                ef = E - full * 128
                for c, a in ((0, io.dst), (1, io.src)):
                    sp.dma_start(e2[0:full, c, :], a[0:full * 128].rearrange("(r e) -> r e", e=128)).then_inc(S.edges_in, 16)
                    sp.dma_start(e2[full:full + 1, c, 0:ef], a[full * 128:E].rearrange("(r e) -> r e", r=1)).then_inc(S.edges_in, 16)
                sp.wait_ge(S.tbl_const, 5)
                for c, p in ((0, padd), (1, pads)):
                    sp.dma_start(e2[full:full + 1, c, ef:128], p[:, 0:128 - ef]).then_inc(S.edges_in, 16)
                    rest = EROWS - full - 1
                    sp.dma_start(e2[full + 1:EROWS, c, :], p[:, 0:rest * 128].rearrange("o (r e) -> o r e", r=rest)).then_inc(S.edges_in, 16)
                sp.dma_start(m.key[0:1].rearrange("(a n) -> a n", a=1), front[:, :]).then_inc(S.keys_out, 16)
                sp.dma_start(m.key[1 + STEPS * 128:2 + STEPS * 128].rearrange("(a n) -> a n", a=1), back[:, :]).then_inc(S.keys_out, 16)
                sp.wait_ge(S.edges_in, 128)
                sp.dma_start(last_i[:, :, :], m.edges.rearrange("(g p) c -> p g c", p=RP)).then_inc(S.last_in, 16)
                sp.wait_ge(S.keys_made, 1)
                for g in range(TG):
                    o = 1 + g * TP * 128
                    sp.dma_start(m.key[o:o + TP * 128].rearrange("(p e) -> p e", p=TP), key[:, g, :]).then_inc(S.keys_out, 16)
                sp.dma_start(m.loc.rearrange("(g p) e -> p g e", p=TP), loc16[:, :, :]).then_inc(S.keys_out, 16)
                sp.wait_ge(S.keys_out, 16 * (3 + TG))

            @block.gpsimd
            def _(pool):
                pool.memset(padd[:], int(PAD_NODE)).then_inc(S.tbl_const, 1)
                pool.memset(pads[:], 0).then_inc(S.tbl_const, 1)
                pool.memset(front[:], -1.0).then_inc(S.tbl_const, 1)
                pool.memset(back[:], 1.0e6).then_inc(S.tbl_const, 1)
                pool.memset(m.src_e[:, CH, :], 0).then_inc(S.tbl_const, 1)
                pool.iota(thr[:, :], pattern=[[TT, NT - 1]], base=TT, channel_multiplier=0, allow_small_or_imprecise_dtypes=True).then_inc(S.tbl_iota, 1)
                pool.iota(iota_i[:, :], pattern=[[1, STEPS]], base=0, channel_multiplier=0, allow_small_or_imprecise_dtypes=True).then_inc(S.tbl_iota, 1)
                pool.iota(wend[:, :], pattern=[[RP, RG]], base=0, channel_multiplier=1, allow_small_or_imprecise_dtypes=True).then_inc(S.tbl_iota, 1)
                pool.iota(step_no[:, :], pattern=[[TP, TG]], base=0, channel_multiplier=1, allow_small_or_imprecise_dtypes=True).then_inc(S.tbl_iota, 1)
                pool.memset(ones[:], 1.0).then_inc(S.tbl_iota, 1)
                pool.memset(m.ident[:], 0.0).then_inc(S.ident_zero, 1)
                pool.wait_ge(S.ident_zero, 1)
                pool.affine_select(out=m.ident[:, :], in_=m.ident[:, :], compare_op=ALU.not_equal, fill=1.0, base=0,
                                   pattern=[[-1, 128]], channel_multiplier=1).then_inc(S.ident_made, 1)
                pool.iota(m.iota_w[:, :], pattern=[[1, TT]], base=0, channel_multiplier=0, allow_small_or_imprecise_dtypes=True).then_inc(S.ident_made, 1)
                pool.iota(m.iota_p[:, :], pattern=[[0, 1]], base=0, channel_multiplier=1, allow_small_or_imprecise_dtypes=True).then_inc(S.ident_made, 1)
                pool.wait_ge(S.rows_known, 1)
                pool.wait_ge(S.edges_in, 128)
                for g in range(TG):
                    pool.indirect_dma_start(got[:, g, :], None, m.edges,
                                            bass.IndirectOffsetOnAxis(ap=row_i[:, g:g + 1].bitcast(U32), axis=0)).then_inc(S.rows_in[g], 16)

            @block.vector
            def _(dve):
                st = m.dve_steps.on(dve)
                dve.wait_ge(S.last_in, 16)
                dve.wait_ge(S.tbl_iota, 5)
                st.link(dve.tensor_copy(last_f[:, :], last_i[:, :, 127]))
                for g in range(RG):
                    st.link(dve.tensor_scalar(junk[:, :], thr[:, :], last_f[:, g:g + 1], 0.0, ALU.is_le, ALU.add,
                                              accum_out=wfound[:, g:g + 1]))
                st.link(dve.tensor_tensor(wend[:, :], wend[:, :], wfound[:, :], ALU.add))
                for g in range(RG):
                    last = dve.tensor_scalar(before[:, g, :], iota_i[:, :], wend[:, g:g + 1], None, ALU.is_gt)
                    st.then(last)
                st.settle()
                dve.sem_inc(S.before_made, 1)
                dve.wait_ge(S.rows_counted, 1)
                st.link(dve.tensor_copy(row_no[:, :], psr[0:TP, 0:TG]))
                dve.tensor_copy(row_i[:, :], row_no[:, :]).then_inc(S.rows_known, 1)
                st.link(dve.tensor_tensor(win0[:, :], step_no[:, :], row_no[:, :], ALU.subtract))
                st.link(dve.tensor_scalar(win0[:, :], win0[:, :], float(TT), None, ALU.mult))
                st.link(dve.tensor_tensor(drow[:, :], iota_i[0:1, :], pst[0:1, 0:STEPS], ALU.subtract))
                st.then(dve.tensor_copy(m.win_of.rearrange("p a b -> p (a b)"), drow[:, :]))
                for g in range(TG):
                    dve.wait_ge(S.rows_in[g], 16)
                    st.then(dve.tensor_copy(src_f[:, g, :], got[:, g, 128:256]))
                    st.link(dve.tensor_copy(dst_f[:, g, :], got[:, g, 0:128]))
                    st.link(dve.tensor_scalar(dst_f[:, g, :], dst_f[:, g, :], win0[:, g:g + 1], None, ALU.subtract))
                    st.then(dve.tensor_scalar(key[:, g, :], dst_f[:, g, :], 0.0, float(TT - 1), ALU.max, ALU.min))
                    st.link(dve.tensor_scalar(dst_f[:, g, :], dst_f[:, g, :], -1.0, float(TT), ALU.max, ALU.min))
                    st.then(dve.tensor_scalar(key[:, g, :], key[:, g, :], win0[:, g:g + 1], None, ALU.add))
                    st.then(dve.tensor_copy(loc16[:, g, :], dst_f[:, g, :]))
                st.settle()
                dve.sem_inc(S.keys_made, 1)
                dve.wait_ge(S.tbl_turned, 1)
                dve.wait_ge(S.tbl_const, 5)
                le = m.loc_e.rearrange("p a b -> p (a b)")
                pe_ = m.pen_e.rearrange("p a b -> p (a b)")
                for g in range(TG):
                    st.then(dve.tensor_copy(le[:, g * TP:(g + 1) * TP], psl[:, g, 0:TP]))
                    st.then(dve.tensor_copy(m.src_e.rearrange("p a b -> p (a b)")[:, g * TP:(g + 1) * TP], pss[:, g, 0:TP]))
                st.settle()
                st.then(dve.tensor_scalar(pe_, le, 0.0, -BIG, ALU.is_lt, ALU.mult))
                st.link(dve.tensor_scalar(pen2[:, :], le, float(TT) - 0.5, -BIG, ALU.is_gt, ALU.mult))
                st.link(dve.tensor_tensor(pe_, pe_, pen2[:, :], ALU.add))

            @block.tensor
            def _(pe):
                pe.wait_ge(S.before_made, 1)
                for j in range(TG):
                    for g in range(RG):
                        pe.matmul(psr[0:TP, j:j + 1], before[:, g, j * TP:(j + 1) * TP], ones[:, :], start=(g == 0), stop=(g == RG - 1))
                for g in range(RG):
                    last = pe.matmul(pst[0:1, 0:STEPS], ones[:, :], before[:, g, :], start=(g == 0), stop=(g == RG - 1))
                last.then_inc(S.rows_counted, 1)
                pe.wait_ge(S.keys_made, 1)
                pe.wait_ge(S.ident_made, 3)
                for g in range(TG):
                    pe.transpose(psl[:, g, 0:TP], dst_f[:, g, :], m.ident[0:TP, 0:TP])
                    last = pe.transpose(pss[:, g, 0:TP], src_f[:, g, :], m.ident[0:TP, 0:TP])
                last.then_inc(S.tbl_turned, 1)


def project(nc, m, io):
    LG = 5
    with ExitStack() as ctx:
        def sb(n, s, d=F32):
            return ctx.enter_context(nc.sbuf_tensor(n, s, d))
        wnat = sb("wnat", [128, 4, 2, D])
        wall = sb("wall", [128, 2, WALL])
        gpre = sb("gpre", [128, 2])
        bqkv = sb("bqkv", [TT, 3 * D])
        bo = sb("bo", [TT, D])
        stats = sb("stats", [TT, NT, 6])
        mean = sb("mean", [TT, NT])
        var = sb("var", [TT, NT])
        rstd = sb("rstd", [TT, NT])
        ss = sb("ss", [TT, NT])
        rms = sb("rms", [TT, NT])
        sq = sb("sq", [TT, 2, D])
        xr = sb("xr", [TT, 2, D])
        xnT = sb("xnT", [128, 2, 2, TT])
        kst = sb("kst", [TT, 2, D])
        vst = sb("vst", [TT, 2, D])
        zero = sb("zero", [128, 4 * D])
        pt = [ctx.enter_context(nc.psum_tensor(f"pt{i}", [128, 512], F32)) for i in range(2)]
        pa = [ctx.enter_context(nc.psum_tensor(f"pa{i}", [TT, 512], F32)) for i in range(2)]
        pb = [ctx.enter_context(nc.psum_tensor(f"pb{i}", [TT, 512], F32)) for i in range(2)]
        pc = [ctx.enter_context(nc.psum_tensor(f"pc{i}", [TT, 512], F32)) for i in range(2)]
        S = m.sem
        xt = io.x.rearrange("(t p) d -> p t d", p=TT)

        def tiles(eng, body):
            body(0, 0, 0, False)
            body(1, 1, 0, False)
            body(2, 0, 1, False)
            with eng.Fori(2, 12) as k:
                body(2 * k - 1, 1, k - 1, False)
                body(2 * k, 0, k, False)
            body(23, 1, 11, False)
            body(24, 0, 12, True)

        with nc.Block() as block:
            @block.sync
            def _(sp):
                for g in range(NT // LG):
                    sp.dma_start(m.base[:, g * LG:(g + 1) * LG, :], xt[:, g * LG:(g + 1) * LG, :]).then_inc(S.x_in[g], 16)
                for w, a in enumerate((io.Wq, io.Wk, io.Wv, io.Wo)):
                    sp.dma_start(wnat[:, w, :, :], a.rearrange("(c p) i -> p c i", p=128)).then_inc(S.w_in, 16)
                sp.dma_start(wall[:, :, 3 * D:WALL], io.w_qkv.rearrange("(c p) n -> p c n", p=128)).then_inc(S.w_in, 16)
                sp.dma_start(gpre[:, :], io.g_pre.rearrange("(c p) -> p c", p=128), allow_slow_non_contiguous=True).then_inc(S.w_in, 16)
                for i, b in enumerate((io.bq, io.bk, io.bv)):
                    sp.dma_start(bqkv[:, i * D:(i + 1) * D], b.partition_broadcast(TT)).then_inc(S.b_in, 16)
                sp.dma_start(bo[:, :], io.bo.partition_broadcast(TT)).then_inc(S.bo_in, 16)
                sp.wait_ge(S.zero_made, 1)
                rows = EX * CAP
                for r in range(0, rows, 512):
                    p = min(512, rows - r) // 4
                    sp.dma_start(m.slots[r:r + 4 * p, :].rearrange("(p a) d -> p (a d)", a=4), zero[0:p, :]).then_inc(S.zero_out, 16)

                def body(t, par, turn, last):
                    sp.wait_ge(S.qkv_out, t + 1)
                    rows = bass.ds(t * TT, TT)
                    sp.dma_start(m.k_d[rows, :], kst[:, par, :]).then_inc(S.kv_stored[par], 16)
                    sp.dma_start(m.v_d[rows, :], vst[:, par, :]).then_inc(S.kv_stored[par], 16)
                tiles(sp, body)
                sp.wait_ge(S.kv_stored[0], 13 * 32)
                sp.wait_ge(S.kv_stored[1], 12 * 32)
                sp.wait_ge(S.zero_out, 16 * (-(-rows // 512)))

            @block.gpsimd
            def _(pool):
                pool.memset(zero[:], 0.0).then_inc(S.zero_made, 1)
                pool.memset(m.mixv[:, :, HID:HID + 1], 1.0).then_inc(S.mixv_one, 1)
                pool.wait_ge(S.bo_in, 16)

                def body(t, par, turn, last):
                    pool.wait_ge(S.squared, t + 1)
                    pool.nop(nofuse=True)
                    if not (isinstance(t, int) and t < 2):
                        pool.wait_ge(S.xn_turned, t - 1)
                        pool.nop(nofuse=True)
                    pool.tensor_copy(xr[:, par, :], at(m.xn, t)).then_inc(S.xr_made, 1)
                    pool.tensor_tensor(at(m.base, t), at(m.base, t), at(m.xn, t), ALU.add).then_inc(S.base_x, 1)
                    pool.wait_ge(S.base_x, t + 1)
                    pool.nop(nofuse=True)
                    pool.tensor_tensor(at(m.base, t), at(m.base, t), bo[:, :], ALU.add)
                tiles(pool, body)

            @block.vector
            def _(dve):
                st = m.dve_steps.on(dve)
                for g in range(NT // LG):
                    dve.wait_ge(S.x_in[g], 16)
                    r = slice(g * LG, (g + 1) * LG)
                    for t in range(g * LG, (g + 1) * LG):
                        st.then(dve.bn_stats(stats[:, t, :], m.base[:, t, :]))
                    st.settle()
                    mean_and_var(dve, st, stats[:, r, :], mean[:, r], var[:, r], rms[:, r]).then_inc(S.var_made, 1)
                    dve.wait_ge(S.std_made, g + 1)
                    st.link(dve.reciprocal(rstd[:, r], rstd[:, r]))
                    for t in range(g * LG, (g + 1) * LG):
                        dve.tensor_scalar(m.xn[:, t, :], m.base[:, t, :], mean[:, t:t + 1], rstd[:, t:t + 1], ALU.subtract,
                                          ALU.mult).then_inc(S.xn_made, 1)
                    if g == 0:
                        dve.wait_ge(S.w_in, 96)
                        for c in range(2):
                            dve.tensor_scalar(wall[:, c, 3 * D:WALL], wall[:, c, 3 * D:WALL], gpre[:, c:c + 1], None,
                                              ALU.mult).then_inc(S.w_ready, 1)
                    dve.wait_ge(S.squared, (g + 1) * LG)
                    dve.tensor_scalar(ss[:, r], ss[:, r], 1e-24, None, ALU.max).then_inc(S.ss_made, 1)
                    dve.wait_ge(S.norm_made, g + 1)
                    st.link(dve.reciprocal(rms[:, r], rms[:, r]))
                    dve.tensor_scalar(rms[:, r], rms[:, r], float(D) ** 0.5, None, ALU.mult).then_inc(S.rms_made, 1)
                dve.wait_ge(S.b_in, 48)

                def body(t, par, turn, last):
                    dve.wait_ge(S.projected, t + 1)
                    wait(dve, S.kv_stored[par], 32 * turn)
                    dve.tensor_tensor(at(m.q, t), pa[par][:, 0:D], bqkv[:, 0:D], ALU.add)
                    dve.tensor_tensor(kst[:, par, :], pa[par][:, D:2 * D], bqkv[:, D:2 * D], ALU.add)
                    dve.tensor_tensor(vst[:, par, :], pb[par][:, 0:D], bqkv[:, 2 * D:3 * D], ALU.add).then_inc(S.qkv_out, 1)
                tiles(dve, body)

            @block.scalar
            def _(act):
                for w in range(4):
                    act.wait_ge(S.w_turned, w + 1)
                    src = pt[w % 2][:, :].rearrange("p (i o) -> p i o", i=2)
                    dst = wall[:, :, w * D:(w + 1) * D] if w < 3 else m.woT[:, :, :]
                    act.activation(dst, src, ACT.Copy).then_inc(S.w_evac, 1)
                for g in range(NT // LG):
                    act.wait_ge(S.var_made, g + 1)
                    act.activation(rstd[:, g * LG:(g + 1) * LG], var[:, g * LG:(g + 1) * LG], ACT.Sqrt).then_inc(S.std_made, 1)
                    for t in range(g * LG, (g + 1) * LG):
                        act.wait_ge(S.xn_made, t + 1)
                        wait(act, S.squared, t - 1)
                        act.activation(sq[:, t % 2, :], m.xn[:, t, :], ACT.Square, accum_out=ss[:, t:t + 1]).then_inc(S.squared, 1)
                    act.wait_ge(S.ss_made, g + 1)
                    act.activation(rms[:, g * LG:(g + 1) * LG], ss[:, g * LG:(g + 1) * LG], ACT.Sqrt).then_inc(S.norm_made, 1)

                def turn_out(t, par):
                    act.wait_ge(S.xn_turned, t + 1)
                    wait(act, S.projected, t - 1)
                    act.activation(xnT[:, par, :, :], pt[par][:, 0:2 * TT].rearrange("p (c n) -> p c n", c=2), ACT.Copy).then_inc(S.xnT_made, 1)

                def body(t, par, turn, last):
                    if not last:
                        turn_out(t + 1, 1 - par)
                    act.wait_ge(S.projected, t + 1)
                    if isinstance(t, int) and t == 0:
                        act.wait_ge(S.rms_made, NT // LG)
                    r = at(rms.rearrange("p (t o) -> p t o", o=1), t)
                    act.activation(at(m.mixq, t), pc[par][:, 0:HID], ACT.Copy, scale=r)
                    act.activation(at(m.mixk, t), pc[par][:, HID:2 * HID], ACT.Copy, scale=r)
                    act.activation(at(m.mixv, t)[:, 0:HID], pc[par][:, 2 * HID:3 * HID], ACT.Copy, scale=r).then_inc(S.mix_out, 1)
                turn_out(0, 0)
                tiles(act, body)

            @block.tensor
            def _(pe):
                pe.wait_ge(S.w_in, 96)
                for w in range(4):
                    wait(pe, S.w_evac, w - 1)
                    for i in range(2):
                        for o in range(2):
                            last = pe.transpose(pt[w % 2][:, i * D + o * 128:i * D + (o + 1) * 128],
                                                wnat[:, w, o, i * 128:(i + 1) * 128], m.ident[:, :])
                    last.then_inc(S.w_turned, 1)
                pe.wait_ge(S.w_evac, 4)

                def turn_in(t, par):
                    pe.wait_ge(S.xr_made, t + 1)
                    wait(pe, S.xnT_made, t - 1)
                    for c in range(2):
                        last = pe.transpose(pt[par][:, c * TT:(c + 1) * TT], xr[:, par, c * 128:(c + 1) * 128], m.ident[0:TT, 0:TT])
                    last.then_inc(S.xn_turned, 1)

                def body(t, par, turn, last):
                    if not last:
                        turn_in(t + 1, 1 - par)
                    pe.wait_ge(S.xnT_made, t + 1)
                    wait(pe, S.qkv_out, t - 1)
                    wait(pe, S.mix_out, t - 1)
                    for dst, a, b in ((pa, 0, 2 * D), (pb, 2 * D, 3 * D), (pc, 3 * D, WALL)):
                        for c in range(2):
                            mm = pe.matmul(dst[par][:, 0:b - a], xnT[:, par, c, :], wall[:, c, a:b], start=(c == 0), stop=(c == 1))
                    mm.then_inc(S.projected, 1)
                turn_in(0, 0)
                pe.wait_ge(S.w_ready, 2)
                tiles(pe, body)


def linear_attention(nc, m, io):
    with ExitStack() as ctx:
        def sb(n, s, d=F32):
            return ctx.enter_context(nc.sbuf_tensor(n, s, d))

        def ps(n, s):
            return ctx.enter_context(nc.psum_tensor(n, s, F32))
        qmax = sb("qmax", [TT, NT * MH])
        kpart = sb("kpart", [TT, HID])
        kmax = sb("kmax", [128, 2])
        mk = sb("mk", [128, MEM])
        mvm = sb("mvm", [128, MEM])
        kmrow = sb("kmrow", [1, HID])
        ones = sb("ones_m", [1, TT])
        memk = sb("memk", [MEM, HID])
        memv = sb("memv", [MEM, HID + 1])
        wo = sb("w_out_sb", [128, D])
        cd = sb("cd", [128, HID])
        cdT = sb("cdT", [128, HID])
        csum = sb("csum", [128, 1])
        wc = sb("wc", [128, D])
        bout = sb("bout", [TT, D])
        gout = sb("gout", [TT, D])
        qr = sb("qr", [TT, 2, HID])
        qT = sb("qT", [128, 2, TT])
        ysq = sb("ysq", [TT, 2, D])
        yss = sb("yss", [TT, NT])
        p1, p2, p3 = ps("p1", [128, 512]), ps("p2", [128, 512]), ps("p3", [128, 512])
        pq = [ps(f"pq{i}", [128, 512]) for i in range(2)]
        py = [ps(f"py{i}", [TT, 512]) for i in range(2)]
        S = m.sem
        y = m.xn
        qv = m.mixq.rearrange("p t (h d) -> p (t h) d", h=MH)
        qf = m.mixq.rearrange("p t c -> p (t c)")
        kf = m.mixk.rearrange("p t c -> p (t c)")
        with nc.Block() as block:
            @block.sync
            def _(sp):
                mem = io.mem_kv.rearrange("a h d m -> a (h d) m")
                sp.dma_start(mk[:, :], mem[0]).then_inc(S.mem_in, 16)
                sp.dma_start(mvm[:, :], mem[1]).then_inc(S.mem_in, 16)
                sp.dma_start(wo[:, :], io.w_out).then_inc(S.mem_in, 16)
                sp.dma_start(bout[:, :], io.b_out.partition_broadcast(TT)).then_inc(S.mem_in, 16)
                sp.dma_start(gout[:, :], io.g_out.partition_broadcast(TT)).then_inc(S.mem_in, 16)

            @block.gpsimd
            def _(pool):
                pool.memset(ones[:], 1.0).then_inc(S.la_const, 1)
                pool.memset(memv[:], 1.0).then_inc(S.la_const, 1)
                pool.memset(cd[:], 0.0).then_inc(S.la_const, 1)

                def stage(t, par):
                    if not (isinstance(t, int) and t < 2):
                        pool.wait_ge(S.q_turned, t - 1)
                        pool.nop(nofuse=True)
                    pool.tensor_copy(qr[:, par, :], at(m.mixq, t)).then_inc(S.qr_made, 1)
                pool.wait_ge(S.q_soft, 1)
                for t in range(3):
                    stage(t, t % 2)
                with pool.Fori(2, 13) as k:
                    stage(2 * k - 1, 1)
                    stage(2 * k, 0)
                with pool.Fori(0, NT) as t:
                    pool.wait_ge(S.y_scaled, t + 1)
                    pool.nop(nofuse=True)
                    pool.tensor_tensor(at(m.base, t), at(m.base, t), at(y, t), ALU.add)

            @block.vector
            def _(dve):
                st = m.dve_steps.on(dve)
                dve.tensor_reduce(kpart[:, :], m.mixk.rearrange("p t c -> p c t"), X, ALU.max).then_inc(S.kmax1, 1)
                st.link(dve.tensor_reduce(qmax[:, :], qv, X, ALU.max))
                dve.tensor_tensor(qv, qv, spread(qmax[:, :], 2, MD), ALU.subtract).then_inc(S.q_shifted, 1)
                dve.wait_ge(S.mem_in, 80)
                st.then(dve.tensor_reduce(kmax[:, 0:1], mk[:, :], X, ALU.max))
                dve.wait_ge(S.kmax_turned, 1)
                st.link(dve.tensor_reduce(kmax[:, 1:2], p1[:, 0:TT], X, ALU.max))
                st.link(dve.tensor_tensor(kmax[:, 0:1], kmax[:, 0:1], kmax[:, 1:2], ALU.max))
                dve.tensor_scalar(mk[:, :], mk[:, :], kmax[:, 0:1], None, ALU.subtract).then_inc(S.kmax2, 1)
                dve.wait_ge(S.kmax_row, 1)
                dve.tensor_copy(kmrow[:, :], p2[0:1, 0:HID]).then_inc(S.kmax3, 1)
                dve.wait_ge(S.kmax_wide, 1)
                dve.tensor_tensor(m.mixk[:, :, :], m.mixk[:, :, :], spread(p3[0:TT, 0:HID], 1, NT), ALU.subtract).then_inc(S.k_shifted, 1)
                dve.wait_ge(S.mem_turned, 1)
                dve.wait_ge(S.la_const, 3)
                dve.tensor_copy(memk[:, :], p2[0:MEM, 128:256])
                dve.tensor_copy(memv[:, 0:HID], p2[0:MEM, 256:384]).then_inc(S.mem_ready, 1)
                dve.wait_ge(S.q_exp, 1)
                st.link(dve.tensor_reduce(qmax[:, :], qv, X, ALU.add))
                st.link(dve.reciprocal(qmax[:, :], qmax[:, :]))
                dve.tensor_tensor(qv, qv, spread(qmax[:, :], 2, MD), ALU.mult).then_inc(S.q_soft, 1)
                st.then(dve.tensor_scalar(gout[:, :], gout[:, :], float(D) ** 0.5, None, ALU.mult))
                dve.wait_ge(S.ctx_made, 1)
                st.link(dve.reciprocal(csum[:, :], p1[:, 128 + HID:129 + HID]))
                for h in range(MH):
                    r = slice(h * MD, (h + 1) * MD)
                    last = dve.tensor_scalar(cd[r, r], p1[r, 128 + h * MD:128 + (h + 1) * MD], csum[r, 0:1], float(MD) ** -0.5, ALU.mult, ALU.mult)
                last.then_inc(S.cd_made, 1)
                dve.wait_ge(S.cd_turned, 1)
                dve.tensor_copy(cdT[:, :], p3[:, 0:HID]).then_inc(S.cdT_made, 1)
                dve.wait_ge(S.wc_prod, 1)
                dve.tensor_copy(wc[:, :], p3[:, 128:128 + D]).then_inc(S.wc_made, 1)

                def body(t, par):
                    dve.wait_ge(S.y_prod, t + 1)
                    dve.tensor_tensor(at(y, t), py[par][:, 0:D], bout[:, :], ALU.add).then_inc(S.y_made, 1)
                for t in range(3):
                    body(t, t % 2)
                with dve.Fori(2, 13) as k:
                    body(2 * k - 1, 1)
                    body(2 * k, 0)
                dve.wait_ge(S.y_squared, NT)
                dve.tensor_scalar(yss[:, :], yss[:, :], 1e-24, None, ALU.max).then_inc(S.yss_made, 1)
                dve.wait_ge(S.ynorm_made, 1)
                st.link(dve.reciprocal(yss[:, :], yss[:, :]))
                with dve.Fori(0, NT) as t:
                    dve.scalar_tensor_tensor(out=at(y, t), in0=at(y, t), scalar=at(yss.rearrange("p (t o) -> p t o", o=1), t),
                                             in1=gout[:, :], op0=ALU.mult, op1=ALU.mult).then_inc(S.y_scaled, 1)

            @block.scalar
            def _(act):
                act.wait_ge(S.q_shifted, 1)
                act.activation(qf, qf, ACT.Exp).then_inc(S.q_exp, 1)
                act.wait_ge(S.kmax2, 1)
                act.activation(mk[:, :], mk[:, :], ACT.Exp).then_inc(S.mk_exp, 1)
                act.wait_ge(S.k_shifted, 1)
                act.activation(kf, kf, ACT.Exp).then_inc(S.k_exp, 1)

                def body(t, par):
                    act.wait_ge(S.q_turned, t + 1)
                    wait(act, S.y_prod, t - 1)
                    act.activation(qT[:, par, :], pq[par][:, 0:TT], ACT.Copy).then_inc(S.qT_made, 1)

                def square(t, par):
                    act.wait_ge(S.y_made, t + 1)
                    wait(act, S.y_squared, t - 1)
                    act.activation(ysq[:, par, :], at(y, t), ACT.Square, accum_out=at(yss.rearrange("p (t o) -> p t o", o=1), t)).then_inc(S.y_squared, 1)
                body(0, 0)
                for t in range(1, 4):
                    body(t, t % 2)
                    square(t - 1, (t - 1) % 2)
                with act.Fori(2, 12) as k:
                    body(2 * k, 0)
                    square(2 * k - 1, 1)
                    body(2 * k + 1, 1)
                    square(2 * k, 0)
                body(24, 0)
                square(23, 1)
                square(24, 0)
                act.wait_ge(S.yss_made, 1)
                act.activation(yss[:, :], yss[:, :], ACT.Sqrt).then_inc(S.ynorm_made, 1)

            @block.tensor
            def _(pe):
                pe.wait_ge(S.kmax1, 1)
                pe.transpose(p1[:, 0:TT], kpart[:, :], m.ident[0:TT, 0:TT]).then_inc(S.kmax_turned, 1)
                pe.wait_ge(S.kmax2, 1)
                pe.transpose(p2[0:1, 0:HID], kmax[:, 0:1], m.ident[:, :]).then_inc(S.kmax_row, 1)
                pe.wait_ge(S.kmax3, 1)
                pe.wait_ge(S.la_const, 1)
                pe.matmul(p3[0:TT, 0:HID], ones[:, :], kmrow[:, :], start=True, stop=True).then_inc(S.kmax_wide, 1)
                pe.wait_ge(S.mk_exp, 1)
                pe.transpose(p2[0:MEM, 128:256], mk[:, :], m.ident[:, :])
                pe.transpose(p2[0:MEM, 256:384], mvm[:, :], m.ident[:, :]).then_inc(S.mem_turned, 1)
                pe.wait_ge(S.k_exp, 1)
                for t in range(NT):
                    pe.matmul(p1[:, 128:129 + HID], m.mixk[:, t, :], m.mixv[:, t, :], start=(t == 0), stop=False)
                pe.wait_ge(S.mem_ready, 1)
                pe.matmul(p1[:, 128:129 + HID], memk[:, :], memv[:, :], start=False, stop=True).then_inc(S.ctx_made, 1)
                pe.wait_ge(S.cd_made, 1)
                pe.transpose(p3[:, 0:HID], cd[:, :], m.ident[:, :]).then_inc(S.cd_turned, 1)
                pe.wait_ge(S.cdT_made, 1)
                pe.matmul(p3[:, 128:128 + D], cdT[:, :], wo[:, :], start=True, stop=True).then_inc(S.wc_prod, 1)
                pe.wait_ge(S.wc_made, 1)

                def turn(t, par):
                    pe.wait_ge(S.qr_made, t + 1)
                    wait(pe, S.qT_made, t - 1)
                    pe.transpose(pq[par][:, 0:TT], qr[:, par, :], m.ident[0:TT, 0:TT]).then_inc(S.q_turned, 1)

                def prod(t, par):
                    pe.wait_ge(S.qT_made, t + 1)
                    wait(pe, S.y_made, t - 1)
                    pe.matmul(py[par][:, 0:D], qT[:, par, :], wc[:, :], start=True, stop=True).then_inc(S.y_prod, 1)
                turn(0, 0)
                for t in range(1, 4):
                    turn(t, t % 2)
                    prod(t - 1, (t - 1) % 2)
                with pe.Fori(2, 12) as k:
                    turn(2 * k, 0)
                    prod(2 * k - 1, 1)
                    turn(2 * k + 1, 1)
                    prod(2 * k, 0)
                turn(24, 0)
                prod(23, 1)
                prod(24, 0)


def gather_chunks(pool, m, rows, table_ready, consumed, per_chunk):
    for u in range(U):
        pool.indirect_dma_start(m.slot[:, u, :], None, rows,
                                bass.IndirectOffsetOnAxis(ap=m.src_e[:, 0, u:u + 1].bitcast(U32), axis=0)).then_inc(m.sem.arrived[u], 16)
    with pool.Fori(1, CH) as k:
        for u in range(U):
            if u % (U // 2) == 0:
                pool.wait_ge(table_ready, 2 * k - 1 + u // (U // 2))
                pool.nop(nofuse=True)
            if u % 4 == 0:
                pool.wait_ge(consumed, per_chunk * k + (u + 4) * per_chunk // U - per_chunk)
                pool.nop(nofuse=True)
            pool.indirect_dma_start(m.slot[:, u, :], None, rows,
                                    bass.IndirectOffsetOnAxis(ap=m.idx[:, u:u + 1].bitcast(U32), axis=0)).then_inc(m.sem.arrived[u], 16)


def stage_indices(act, m, k, consumed, per_chunk, table_ready):
    for hf in range(2):
        r = slice(hf * U // 2, (hf + 1) * U // 2)
        act.wait_ge(consumed, per_chunk * k + (hf + 1) * per_chunk // 2)
        act.activation(m.idx[:, r], at(m.src_e, k + 1)[:, r], ACT.Copy).then_inc(table_ready, 1)


def scores(nc, m):
    with ExitStack() as ctx:
        def sb(n, s, d=F32):
            return ctx.enter_context(nc.sbuf_tensor(n, s, d))
        locrow = sb("locrow", [TT, U * 128], BF16)
        hotT = sb("hotT", [TT, U, 128])
        prod = sb("prod", [128, 2, 2, D])
        sc = sb("sc", [128, H, U])
        sp_ = sb("sc_pen", [128, H, U])
        scT = sb("scT", [128, 128])
        pq = [ctx.enter_context(nc.psum_tensor(f"spq{i}", [128, 512], F32)) for i in range(4)]
        pt = ctx.enter_context(nc.psum_tensor("spt", [128, 512], F32))
        S = m.sem
        loc_c = m.loc.rearrange("(k i) e -> k (i e)", i=U)
        s_c = m.s_d.rearrange("h (k i) e -> k h i e", i=U)

        def chunks(eng, body):
            body(0)
            with eng.Fori(1, CH) as k:
                body(k)

        with nc.Block() as block:
            @block.sync
            def _(sp):
                def body(k):
                    wait(sp, S.hotT_made, k)
                    sp.dma_start(locrow[:, :], loc_c[bass.ds(k, 1), :].to_broadcast([TT, U * 128])).then_inc(S.loc_in, 16)
                    if isinstance(k, int):
                        return
                    store(k - 1)

                def store(k):
                    sp.wait_ge(S.scT_made, k + 1)
                    sp.dma_start(s_c[bass.ds(k, 1)].squeeze(0), scT[:, :]).then_inc(S.s_stored, 16)
                chunks(sp, body)
                store(CH - 1)
                sp.wait_ge(S.s_stored, 16 * CH)

            @block.gpsimd
            def _(pool):
                gather_chunks(pool, m, m.k_d, S.idx1, S.prod_made, U // 2)

            @block.scalar
            def _(act):
                def body(k):
                    if not (isinstance(k, int) and k == CH - 1):
                        stage_indices(act, m, k, S.prod_made, U // 2, S.idx1)
                    act.wait_ge(S.sc_turned, k + 1)
                    wait(act, S.s_stored, 16 * k)
                    act.activation(scT[:, :], pt[:, 0:128], ACT.Copy).then_inc(S.scT_made, 1)
                body(0)
                with act.Fori(1, CH - 1) as k:
                    body(k)
                body(CH - 1)

            @block.vector
            def _(dve):
                def body(k):
                    dve.wait_ge(S.loc_in, 16 * k + 16)
                    wait(dve, S.q_spread, 8 * k)
                    dve.tensor_scalar(flat(hotT[:, :, :]), locrow[:, :], m.iota_p[0:TT, 0:1], None, ALU.is_equal).then_inc(S.hotT_made, 1)
                    for j in range(U // 2):
                        dve.wait_ge(S.arrived[2 * j], 16 * k + 16)
                        dve.wait_ge(S.arrived[2 * j + 1], 16 * k + 16)
                        dve.wait_ge(S.q_spread, 8 * k + j + 1)
                        wait(dve, S.reduced, 8 * k + j - 1)
                        dve.tensor_tensor(flat(prod[:, j % 2, :, :]), pq[j % 4][:, :], flat(m.slot[:, 2 * j:2 * j + 2, :]),
                                          ALU.mult).then_inc(S.prod_made, 1)
                        if j:
                            reduce(k, j - 1)
                    reduce(k, U // 2 - 1)
                    dve.wait_ge(S.reduced, 8 * k + 8)
                    wait(dve, S.sc_turned, k)
                    dve.tensor_tensor(sp_[:, :, :], sc[:, :, :], spread(at(m.pen_e, k), 1, H), ALU.add).then_inc(S.sc_made, 1)

                def reduce(k, j):
                    dve.wait_ge(S.prod_made, 8 * k + j + 1)
                    wait(dve, S.sc_made, k)
                    dve.tensor_reduce(sc[:, :, 2 * j:2 * j + 2].rearrange("p h i -> p i h"),
                                      prod[:, j % 2, :, :].rearrange("p i (h d) -> p i h d", h=H), X, ALU.add).then_inc(S.reduced, 1)
                chunks(dve, body)

            @block.tensor
            def _(pe):
                def body(k):
                    wins = nc.values_load_multi_w_load_instructions(flat(m.win_of[0:1, bass.ds(k, 1), :]), engines=PE_ONLY,
                                                                    min_val=0, max_val=NT - 1)[1]
                    pe.wait_ge(S.hotT_made, k + 1)
                    for u in range(U):
                        if u % 2 == 0:
                            wait(pe, S.prod_made, 8 * k + u // 2 - 3)
                        mm = pe.matmul(pq[(u // 2) % 4][:, (u % 2) * D:(u % 2 + 1) * D], hotT[:, u, :], at(m.q, wins[u]),
                                       start=True, stop=True)
                        if u % 2:
                            mm.then_inc(S.q_spread, 1)
                    pe.wait_ge(S.sc_made, k + 1)
                    wait(pe, S.scT_made, k)
                    pe.transpose(pt[:, 0:128], sp_[:, :, :].rearrange("p h i -> p (h i)"), m.ident[:, :]).then_inc(S.sc_turned, 1)
                chunks(pe, body)


def segment_softmax(nc, m):
    with ExitStack() as ctx:
        def sb(n, s, d=F32):
            return ctx.enter_context(nc.sbuf_tensor(n, s, d))
        s = sb("seg_s", [128, SL])
        key = sb("seg_key", [128, SL + 2])
        fwd = sb("seg_fwd", [128, SL])
        bwd = sb("seg_bwd", [128, SL])
        ends = sb("seg_ends", [128, 8])
        row = sb("seg_row", [1, 4, 130])
        one = sb("seg_one", [1, 1])
        pr = ctx.enter_context(nc.psum_tensor("seg_pr", [128, 512], F32))
        pc = ctx.enter_context(nc.psum_tensor("seg_pc", [128, 512], F32))
        S = m.sem
        mx = key[:, 0:SL]
        kd = m.key.rearrange("(b n) -> b n", n=SL)
        kd1 = m.key[0:SB * SL].rearrange("(b n) -> b n", n=SL)
        with nc.Block() as block:
            @block.sync
            def _(sp):
                for h in range(H):
                    r = slice(h * SB, (h + 1) * SB)
                    sp.dma_start(key[r, 0:SL], kd1).then_inc(S.key_in, 16)
                    sp.dma_start(key[r, SL:SL + 2], kd[1:SB + 1, 0:2]).then_inc(S.key_in, 16)
                sp.dma_start(s[:, :], m.s_d.rearrange("h (b i) e -> (h b) (i e)", b=SB)).then_inc(S.s_in, 16)
                sp.wait_ge(S.p_made, 1)
                sp.dma_start(m.p_d.rearrange("h (b i) e -> (h b) (i e)", b=SB), s[:, :]).then_inc(S.p_stored, 16)
                sp.wait_ge(S.p_stored, 16)

            @block.gpsimd
            def _(pool):
                pool.memset(one[:], 1.0).then_inc(S.seg_const, 1)
                pool.memset(row[:], -RESET).then_inc(S.seg_const, 1)
                pool.memset(flat(m.agg[:, 0:13, :]), 0.0)
                pool.memset(flat(m.agg[:, 13:NT, :]), 0.0)

            @block.vector
            def _(dve):
                st = m.dve_steps.on(dve)
                dve.wait_ge(S.key_in, 16 * 2 * H)
                st.then(dve.tensor_tensor(fwd[:, :], key[:, 1:SL + 1], key[:, 0:SL], ALU.not_equal))
                st.link(dve.tensor_tensor(bwd[:, :], key[:, 1:SL + 1], key[:, 2:SL + 2], ALU.not_equal))
                st.then(dve.tensor_scalar(fwd[:, :], fwd[:, :], -RESET, None, ALU.mult))
                st.link(dve.tensor_scalar(bwd[:, :], bwd[:, :], -RESET, None, ALU.mult))
                st.then(dve.tensor_reduce(ends[:, 1:2], fwd[:, :], X, ALU.min))
                st.then(dve.tensor_reduce(ends[:, 3:4], bwd[:, :], X, ALU.min))
                dve.wait_ge(S.s_in, 16)
                dve.wait_ge(S.seg_const, 2)
                st.link(dve.tensor_tensor_scan(mx, fwd[:, :], s[:, :], -RESET, ALU.add, ALU.max))
                st.link(dve.tensor_copy(ends[:, 0:1], mx[:, SL - 1:SL]))
                dve.sem_inc(S.ends_made, 1)
                dve.wait_ge(S.ends_turned, 1)
                st.link(dve.tensor_copy(row[:, 0:2, 1:129], pr[0:1, 0:256].rearrange("p (a b) -> p a b", a=2)))
                st.link(dve.tensor_tensor_scan(row[:, 2, 1:129], row[:, 1, 1:129], row[:, 0, 1:129], -RESET, ALU.add, ALU.max))
                dve.sem_inc(S.carry_made, 1)
                dve.wait_ge(S.carry_turned, 1)
                st.link(dve.tensor_copy(ends[:, 4:5], pc[:, 0:1]))
                st.link(dve.tensor_tensor_scan(mx, fwd[:, :], s[:, :], ends[:, 4:5], ALU.add, ALU.max))
                st.link(dve.tensor_tensor_scan(fwd[:, ::-1], bwd[:, ::-1], mx[:, ::-1], -RESET, ALU.add, ALU.max))
                st.link(dve.tensor_copy(ends[:, 2:3], fwd[:, 0:1]))
                dve.sem_inc(S.ends_made, 1)
                dve.wait_ge(S.ends_turned, 2)
                st.link(dve.tensor_copy(row[:, 0:2, 1:129], pr[0:1, 256:512].rearrange("p (a b) -> p a b", a=2)))
                st.link(dve.tensor_tensor_scan(row[:, 3, 1:129][:, ::-1], row[:, 1, 1:129][:, ::-1], row[:, 0, 1:129][:, ::-1],
                                               -RESET, ALU.add, ALU.max))
                dve.sem_inc(S.carry_made, 1)
                dve.wait_ge(S.carry_turned, 2)
                st.link(dve.tensor_copy(ends[:, 5:6], pc[:, 1:2]))
                st.link(dve.tensor_tensor_scan(fwd[:, ::-1], bwd[:, ::-1], mx[:, ::-1], ends[:, 5:6], ALU.add, ALU.max))
                st.link(dve.tensor_tensor(s[:, :], s[:, :], fwd[:, :], ALU.subtract))
                dve.sem_inc(S.s_shifted, 1)

            @block.scalar
            def _(act):
                act.wait_ge(S.s_shifted, 1)
                act.activation(s[:, :], s[:, :], ACT.Exp, scale=float(HD) ** -0.5).then_inc(S.p_made, 1)

            @block.tensor
            def _(pe):
                for back in range(2):
                    pe.wait_ge(S.ends_made, back + 1)
                    for c in range(2):
                        last = pe.transpose(pr[0:1, (2 * back + c) * 128:(2 * back + c + 1) * 128], ends[:, 2 * back + c:2 * back + c + 1], m.ident[:, :])
                    last.then_inc(S.ends_turned, 1)
                    pe.wait_ge(S.carry_made, back + 1)
                    pe.wait_ge(S.seg_const, 2)
                    src = row[:, 3, 2:130] if back else row[:, 2, 0:128]
                    pe.matmul(pc[:, back:back + 1], src, one[:, :], start=True, stop=True).then_inc(S.carry_turned, 1)


def aggregate(nc, m):
    with ExitStack() as ctx:
        def sb(n, s, d=F32):
            return ctx.enter_context(nc.sbuf_tensor(n, s, d))
        pin = sb("p_in_t", [128, 128])
        pe_sb = sb("p_e", [128, 128])
        hot = sb("hot", [128, 4, TT])
        pv = sb("pv", [128, 4, D])
        pp = ctx.enter_context(nc.psum_tensor("app", [128, 512], F32))
        pa = [ctx.enter_context(nc.psum_tensor(f"apa{i}", [TT, 512], F32)) for i in range(4)]
        S = m.sem
        p_c = m.p_d.rearrange("h (k i) e -> k h i e", i=U)

        def chunks(eng, body):
            body(0)
            with eng.Fori(1, CH) as k:
                body(k)

        with nc.Block() as block:
            @block.sync
            def _(sp):
                def body(k):
                    wait(sp, S.p_turned, k)
                    sp.dma_start(pin[:, :], p_c[bass.ds(k, 1)].squeeze(0)).then_inc(S.p_in, 16)
                chunks(sp, body)

            @block.gpsimd
            def _(pool):
                gather_chunks(pool, m, m.v_d, S.idx2, S.pv_made, U)

            @block.scalar
            def _(act):
                def body(k):
                    act.wait_ge(S.p_turned, k + 1)
                    wait(act, S.summed, U * k)
                    act.activation(pe_sb[:, :], pp[:, 0:128], ACT.Copy).then_inc(S.p_e_made, 1)
                    if not (isinstance(k, int) and k == CH - 1):
                        stage_indices(act, m, k, S.pv_made, U, S.idx2)
                body(0)
                with act.Fori(1, CH - 1) as k:
                    body(k)
                body(CH - 1)

            @block.vector
            def _(dve):
                pw = pp[:, 0:128].rearrange("p (h i) -> p h i", h=H)

                def body(k):
                    wins = nc.values_load_multi_w_load_instructions(flat(m.win_of[0:1, bass.ds(k, 1), :]), engines=DVE_ONLY,
                                                                    min_val=0, max_val=NT - 1)[1]
                    dve.wait_ge(S.p_e_made, k + 1)
                    for u in range(U):
                        wait(dve, S.summed, U * k + u - 3)
                        dve.tensor_scalar(hot[:, u % 4, :], m.iota_w[:, :], at(m.loc_e, k)[:, u:u + 1], None, ALU.is_equal).then_inc(S.hot_made, 1)
                        dve.wait_ge(S.arrived[u], 16 * k + 16 * (CH + 1))
                        dve.tensor_tensor(pv[:, u % 4, :].rearrange("p (h d) -> p h d", h=H),
                                          m.slot[:, u, :].rearrange("p (h d) -> p h d", h=H),
                                          spread(pw[:, :, u], 2, HD), ALU.mult).then_inc(S.pv_made, 1)
                        if u >= 2:
                            add(k, u - 2, wins)
                    add(k, U - 2, wins)
                    add(k, U - 1, wins)

                def add(k, u, wins):
                    dve.wait_ge(S.summed, U * k + u + 1)
                    wait(dve, S.added, U * k + u)
                    dst = at(m.agg, wins[u])
                    dve.tensor_tensor(dst, dst, pa[u % 4][:, 0:D + H], ALU.add).then_inc(S.added, 1)
                chunks(dve, body)

            @block.tensor
            def _(pe):
                pev = pe_sb[:, :].rearrange("p (h i) -> p h i", h=H)

                def body(k):
                    pe.wait_ge(S.p_in, 16 * k + 16)
                    wait(pe, S.p_e_made, k)
                    wait(pe, S.pv_made, U * k)
                    pe.transpose(pp[:, 0:128], pin[:, :], m.ident[:, :]).then_inc(S.p_turned, 1)
                    for u in range(U):
                        wait(pe, S.added, U * k + u - 3)
                        pe.wait_ge(S.pv_made, U * k + u + 1)
                        pe.matmul(pa[u % 4][:, 0:D], hot[:, u % 4, :], pv[:, u % 4, :], start=True, stop=True)
                        if u == 0:
                            pe.wait_ge(S.p_e_made, k + 1)
                        pe.matmul(pa[u % 4][:, D:D + H], hot[:, u % 4, :], pev[:, :, u], start=True, stop=True).then_inc(S.summed, 1)
                chunks(pe, body)


def attention_out(nc, m, io):
    with ExitStack() as ctx:
        def sb(n, s, d=F32):
            return ctx.enter_context(nc.sbuf_tensor(n, s, d))
        rden = sb("rden", [TT, NT, H])
        an = sb("an", [TT, 2, D])
        hr = sb("hr", [TT, 2, D])
        anT = sb("anT", [128, 2, 2, TT])
        stats = sb("stats2", [TT, NT, 6])
        mean = sb("mean2", [TT, NT])
        tmp = sb("tmp2", [TT, NT])
        var = sb("var2", [TT, NT])
        gw = sb("gw", [128, 2, EX])
        gb = sb("gb", [TT, EX])
        pt = [ctx.enter_context(nc.psum_tensor(f"opt{i}", [128, 512], F32)) for i in range(2)]
        po = [ctx.enter_context(nc.psum_tensor(f"opo{i}", [TT, 512], F32)) for i in range(2)]
        S = m.sem

        def pairs(eng, body):
            for t in range(3):
                body(t, t % 2, False)
            with eng.Fori(2, 12) as k:
                body(2 * k - 1, 1, False)
                body(2 * k, 0, False)
            body(23, 1, False)
            body(24, 0, True)

        with nc.Block() as block:
            @block.sync
            def _(sp):
                sp.dma_start(gw[:, :, :], io.gate_w.rearrange("(c p) e -> p c e", p=128)).then_inc(S.gate_in, 16)
                sp.dma_start(gb[:, :], io.gate_b.partition_broadcast(TT)).then_inc(S.gate_in, 16)

            @block.gpsimd
            def _(pool):
                def stage(t, par, last):
                    pool.wait_ge(S.h_made, t + 1)
                    pool.nop(nofuse=True)
                    if not (isinstance(t, int) and t < 2):
                        pool.wait_ge(S.an_turned, NT + t - 1)
                        pool.nop(nofuse=True)
                    pool.tensor_copy(hr[:, par, :], at(m.q, t)).then_inc(S.hr_made, 1)
                pairs(pool, stage)

            @block.vector
            def _(dve):
                st = m.dve_steps.on(dve)
                st.link(dve.tensor_scalar(rden[:, :, :], m.agg[:, :, D:D + H], 0.5, None, ALU.max))
                st.link(dve.reciprocal(rden[:, :, :], rden[:, :, :]))

                def norm(t, par):
                    wait(dve, S.an_turned, t - 1)
                    dve.tensor_tensor(an[:, par, :].rearrange("p (h d) -> p h d", h=H),
                                      at(m.agg, t)[:, 0:D].rearrange("p (h d) -> p h d", h=H),
                                      spread(at(rden, t), 2, HD), ALU.mult).then_inc(S.an_made, 1)

                def body(t, par, last):
                    if not last:
                        norm(t + 1, 1 - par)
                    dve.wait_ge(S.out_prod, t + 1)
                    dve.tensor_tensor(at(m.base, t), at(m.base, t), po[par][:, 0:D], ALU.add).then_inc(S.x2_made, 1)
                    dve.wait_ge(S.x2_made, t + 1)
                    dve.bn_stats(at(stats, t), at(m.base, t)).then_inc(S.x2_stats, 1)
                norm(0, 0)
                pairs(dve, body)
                dve.wait_ge(S.x2_stats, NT)
                mean_and_var(dve, st, stats[:, :, :], mean[:, :], var[:, :], tmp[:, :]).then_inc(S.var2_made, 1)
                dve.wait_ge(S.std2_made, 1)
                st.link(dve.reciprocal(var[:, :], var[:, :]))
                with dve.Fori(0, NT) as t:
                    dve.tensor_scalar(at(m.q, t), at(m.base, t), at(mean.rearrange("p (t o) -> p t o", o=1), t), at(var.rearrange("p (t o) -> p t o", o=1), t),
                                      ALU.subtract, ALU.mult).then_inc(S.h_made, 1)
                dve.wait_ge(S.gate_in, 32)

                def logit(t, par, last):
                    dve.wait_ge(S.logit_prod, t + 1)
                    dve.tensor_tensor(at(m.logit, t), po[par][:, 256:256 + EX], gb[:, :], ALU.add).then_inc(S.logit_made, 1)
                pairs(dve, logit)

            @block.scalar
            def _(act):
                def out(t, par, first):
                    act.wait_ge(S.an_turned, first + t + 1)
                    wait(act, S.out_prod if first == 0 else S.logit_prod, t - 1)
                    act.activation(anT[:, par, :, :], pt[par][:, 0:2 * TT].rearrange("p (c n) -> p c n", c=2), ACT.Copy).then_inc(S.anT_made, 1)
                pairs(act, lambda t, par, last: out(t, par, 0))
                act.wait_ge(S.var2_made, 1)
                act.activation(var[:, :], var[:, :], ACT.Sqrt).then_inc(S.std2_made, 1)
                pairs(act, lambda t, par, last: out(t, par, NT))

            @block.tensor
            def _(pe):
                def turn(t, par, src, ready, first):
                    pe.wait_ge(ready, t + 1)
                    wait(pe, S.anT_made, first + t - 1)
                    for c in range(2):
                        mm = pe.transpose(pt[par][:, c * TT:(c + 1) * TT], src[:, c * 128:(c + 1) * 128], m.ident[0:TT, 0:TT])
                    mm.then_inc(S.an_turned, 1)

                def body(t, par, last):
                    if not last:
                        turn(t + 1, 1 - par, an[:, 1 - par, :], S.an_made, 0)
                    pe.wait_ge(S.anT_made, t + 1)
                    wait(pe, S.x2_made, t - 1)
                    for c in range(2):
                        mm = pe.matmul(po[par][:, 0:D], anT[:, par, c, :], m.woT[:, c, :], start=(c == 0), stop=(c == 1))
                    mm.then_inc(S.out_prod, 1)
                turn(0, 0, an[:, 0, :], S.an_made, 0)
                pairs(pe, body)

                def gate(t, par, last):
                    if not last:
                        turn(t + 1, 1 - par, hr[:, 1 - par, :], S.hr_made, NT)
                    pe.wait_ge(S.anT_made, NT + t + 1)
                    wait(pe, S.logit_made, t - 1)
                    for c in range(2):
                        mm = pe.matmul(po[par][:, 256:256 + EX], anT[:, par, c, :], gw[:, c, :], start=(c == 0), stop=(c == 1))
                    mm.then_inc(S.logit_prod, 1)
                turn(0, 0, hr[:, 0, :], S.hr_made, NT)
                pe.wait_ge(S.x2_made, NT)
                pe.wait_ge(S.gate_in, 32)
                pairs(pe, gate)


def route(nc, m):
    with ExitStack() as ctx:
        def sb(n, s, d=F32):
            return ctx.enter_context(nc.sbuf_tensor(n, s, d))
        pr = sb("probs", [TT, NT, EX])
        e1 = sb("rt_e1", [TT, NT])
        e2 = sb("rt_e2", [TT, NT])
        pos = sb("rt_pos", [TT, NT])
        eid = sb("rt_eid", [TT, NT])
        slot = sb("rt_slot", [TT, NT])
        kept = sb("rt_kept", [TT, NT])
        node = sb("rt_node", [TT, NT])
        iota_e = sb("iota_e", [TT, EX])
        hot = sb("rt_hot", [TT, NT, EX])
        tmp = sb("rt_tmp", [TT, NT, EX])
        tri = sb("rt_tri", [TT, TT])
        ones = sb("rt_ones", [TT, TT])
        tot = sb("rt_tot", [TT, EX, NT])
        run = sb("rt_run", [TT, EX, NT])
        keep = sb("rt_keep", [TT, EX, NT])
        put = sb("rt_put", [TT, NT], I32)
        pi = ctx.enter_context(nc.psum_tensor("rt_pi", [TT, 512], F32))
        pj = ctx.enter_context(nc.psum_tensor("rt_pj", [TT, 512], F32))
        S = m.sem
        L = m.logit
        with nc.Block() as block:
            @block.gpsimd
            def _(pool):
                pool.memset(ones[:], 1.0).then_inc(S.rt_const, 1)
                pool.memset(tri[:], 1.0).then_inc(S.rt_c0, 1)
                pool.memset(keep[:], 1.0).then_inc(S.rt_c0, 1)
                pool.wait_ge(S.rt_c0, 2)
                pool.affine_select(out=tri[:, :], in_=tri[:, :], compare_op=ALU.is_ge, fill=0.0, base=0,
                                   pattern=[[1, TT]], channel_multiplier=-1).then_inc(S.rt_const, 1)
                pool.memset(keep[:, :, 0:1], 0.0).then_inc(S.rt_const, 1)
                pool.iota(iota_e[:, :], pattern=[[1, EX]], base=0, channel_multiplier=0, allow_small_or_imprecise_dtypes=True).then_inc(S.rt_const, 1)
                pool.iota(node[:, :], pattern=[[TT, NT]], base=EX * CAP, channel_multiplier=1, allow_small_or_imprecise_dtypes=True).then_inc(S.rt_const, 1)
                pool.wait_ge(S.slots_known, 1)
                for t in range(NT):
                    pool.indirect_dma_start(m.slots, bass.IndirectOffsetOnAxis(ap=put[:, t:t + 1].bitcast(U32), axis=0),
                                            m.q[:, t, :], None).then_inc(S.rows_put, 16)
                pool.wait_ge(S.rows_put, 16 * NT)

            @block.vector
            def _(dve):
                st = m.dve_steps.on(dve)
                st.link(dve.tensor_reduce(e1[:, :], L[:, :, :], X, ALU.max))
                st.link(dve.tensor_tensor(pr[:, :, :], L[:, :, :], spread(e1[:, :], 2, EX), ALU.subtract))
                dve.sem_inc(S.l_shifted, 1)
                dve.wait_ge(S.l_exp, 1)
                st.link(dve.tensor_reduce(e1[:, :], pr[:, :, :], X, ALU.add))
                st.link(dve.reciprocal(e1[:, :], e1[:, :]))
                st.link(dve.tensor_tensor(pr[:, :, :], pr[:, :, :], spread(e1[:, :], 2, EX), ALU.mult))
                st.link(dve.tensor_reduce(m.prb[:, :], pr[:, :, :], X, ALU.max))
                dve.wait_ge(S.rt_const, 5)
                st.link(dve.tensor_tensor(tmp[:, :, :], pr[:, :, :], spread(m.prb[:, :], 2, EX), ALU.is_equal))
                st.link(dve.tensor_scalar(tmp[:, :, :], tmp[:, :, :], -float(EX), float(EX), ALU.mult, ALU.add))
                st.link(dve.tensor_tensor(tmp[:, :, :], tmp[:, :, :], spread(iota_e[:, :], 1, NT), ALU.add))
                st.link(dve.tensor_reduce(eid[:, :], tmp[:, :, :], X, ALU.min))
                st.link(dve.tensor_tensor(hot[:, :, :], spread(iota_e[:, :], 1, NT), spread(eid[:, :], 2, EX), ALU.is_equal))
                dve.sem_inc(S.hot_ready, 1)
                dve.wait_ge(S.counted, 1)
                st.link(dve.tensor_copy(tot[:, :, :], pj[:, 0:NT * EX].rearrange("p (t e) -> p e t", e=EX)))
                st.link(dve.tensor_tensor_scan(run.rearrange("p e t -> p (e t)"), keep.rearrange("p e t -> p (e t)"),
                                               tot.rearrange("p e t -> p (e t)"), 0.0, ALU.mult, ALU.add))
                st.link(dve.tensor_tensor(run[:, :, :], run[:, :, :], tot[:, :, :], ALU.subtract))
                st.link(dve.tensor_tensor(tmp[:, :, :], run.rearrange("p e t -> p t e"), pi[:, 0:NT * EX].rearrange("p (t e) -> p t e", e=EX), ALU.add))
                st.link(dve.tensor_tensor(tmp[:, :, :], tmp[:, :, :], hot[:, :, :], ALU.mult))
                st.link(dve.tensor_reduce(pos[:, :], tmp[:, :, :], X, ALU.add))
                st.then(dve.tensor_scalar(kept[:, :], pos[:, :], float(CAP), None, ALU.is_le))
                st.link(dve.tensor_scalar(pos[:, :], pos[:, :], float(CAP), -1.0, ALU.min, ALU.add))
                st.link(dve.scalar_tensor_tensor(out=slot[:, :], in0=eid[:, :], scalar=float(CAP), in1=pos[:, :], op0=ALU.mult, op1=ALU.add))
                st.then(dve.tensor_copy(m.slot_i[:, :], slot[:, :]))
                st.then(dve.tensor_tensor(m.prb[:, :], m.prb[:, :], kept[:, :], ALU.mult))
                st.link(dve.tensor_tensor(e2[:, :], slot[:, :], node[:, :], ALU.subtract))
                st.link(dve.tensor_tensor(e2[:, :], e2[:, :], kept[:, :], ALU.mult))
                st.link(dve.tensor_tensor(e2[:, :], e2[:, :], node[:, :], ALU.add))
                st.link(dve.tensor_copy(put[:, :], e2[:, :]))
                dve.sem_inc(S.slots_known, 1)

            @block.scalar
            def _(act):
                act.wait_ge(S.l_shifted, 1)
                act.activation(pr[:, :, :], pr[:, :, :], ACT.Exp).then_inc(S.l_exp, 1)

            @block.tensor
            def _(pe):
                pe.wait_ge(S.rt_const, 5)
                pe.wait_ge(S.hot_ready, 1)
                pe.matmul(pi[:, 0:NT * EX], tri[:, :], flat(hot[:, :, :]), start=True, stop=True)
                pe.matmul(pj[:, 0:NT * EX], ones[:, :], flat(hot[:, :, :]), start=True, stop=True).then_inc(S.counted, 1)


def experts(nc, m, io):
    MT = -(-CAP // 128)
    sizes = [min(128, CAP - 128 * i) for i in range(MT)]
    FC = FF // 128
    with ExitStack() as ctx:
        def sb(n, s, d=F32):
            return ctx.enter_context(nc.sbuf_tensor(n, s, d))
        w1 = [sb(f"w1_{i}", [128, 2, FF]) for i in range(2)]
        w2 = [sb(f"w2_{i}", [128, FC, D]) for i in range(2)]
        b1n = sb("b1n", [EX * FC, 128])
        b1 = sb("b1", [128, EX, FC])
        b2 = [sb(f"b2_{i}", [128, D]) for i in range(2)]
        hb = [sb(f"hb_{i}", [128, MT, D]) for i in range(2)]
        hT = sb("hT", [128, 2, 512])
        hm = sb("hm", [128, FC, 512])
        yb = sb("yb", [128, MT, D])
        pt = [ctx.enter_context(nc.psum_tensor(f"xpt{i}", [128, 512], F32)) for i in range(2)]
        p1 = [ctx.enter_context(nc.psum_tensor(f"xp1{i}", [128, 512], F32)) for i in range(3)]
        p2 = [ctx.enter_context(nc.psum_tensor(f"xp2{i}", [128, 512], F32)) for i in range(3)]
        S = m.sem
        w1d = io.w1.rearrange("e (c p) f -> e p c f", p=128)
        w2d = io.w2.rearrange("e (c p) d -> e p c d", p=128)

        def rounds(eng, body):
            for par in range(2):
                body(par, par, 0)
            with eng.Fori(1, EX // 2) as k:
                for par in range(2):
                    body(2 * k + par, par, k)

        with nc.Block() as block:
            @block.sync
            def _(sp):
                def body(e, par, k):
                    wait(sp, S.y_stored, 64 * (e - 1) if not isinstance(e, int) else 0)
                    one = bass.ds(e, 1)
                    sp.dma_start(w1[par][:, :, :], w1d[one].squeeze(0)).then_inc(S.ex_in[par], 16)
                    sp.dma_start(hb[par][:, 0:MT - 1, :], m.slots[bass.ds(e * CAP, 128 * (MT - 1)), :].rearrange("(c p) d -> p c d", p=128)).then_inc(S.ex_in[par], 16)
                    sp.dma_start(hb[par][0:sizes[-1], MT - 1, :], m.slots[bass.ds(e * CAP + 128 * (MT - 1), sizes[-1]), :]).then_inc(S.ex_in[par], 16)
                    sp.dma_start(w2[par][:, :, :], w2d[one].squeeze(0)).then_inc(S.ex_in[par], 16)
                    sp.dma_start(b2[par][:, :], io.b2[one, :].to_broadcast([128, D])).then_inc(S.ex_in[par], 16)
                sp.dma_start(b1n[:, :], io.b1.rearrange("e (c p) -> (e c) p", p=128)).then_inc(S.b1_in, 16)
                rounds(sp, body)

            @block.scalar
            def _(act):
                act.wait_ge(S.b1_turned, 1)
                act.activation(b1.rearrange("p e c -> p (e c)"), p1[2][:, 0:EX * FC], ACT.Copy).then_inc(S.b1_made, 1)
                act.wait_ge(S.b1_made, 1)

                def body(e, par, k):
                    for c in range(2):
                        act.wait_ge(S.hb_turned, 2 * e + c + 1)
                        if c == 0:
                            wait(act, S.up_prod, FC * e)
                        act.activation(hT[:, c, 0:CAP], pt[c][:, 0:CAP], ACT.Copy).then_inc(S.hT_made, 1)
                    for f in range(FC):
                        act.wait_ge(S.up_prod, FC * e + f + 1)
                        if f == 0:
                            wait(act, S.down_prod, MT * e)
                        act.activation(hm[:, f, 0:CAP], p1[f % 2][:, 0:CAP], ACT.Relu, bias=at(b1, e)[:, f:f + 1]).then_inc(S.hm_made, 1)
                    for i in range(MT):
                        act.wait_ge(S.y_ready, MT * e + i + 1)
                        act.dma_start(m.y_d[bass.ds(e * CAP + 128 * i, sizes[i]), :], yb[0:sizes[i], i, :]).then_inc(S.y_stored, 16)
                rounds(act, body)
                act.wait_ge(S.y_stored, 16 * MT * EX)

            @block.vector
            def _(dve):
                def body(e, par, k):
                    wait(dve, S.y_stored, 16 * MT * e)
                    for i in range(MT):
                        dve.wait_ge(S.down_prod, MT * e + i + 1)
                        dve.tensor_tensor(yb[0:sizes[i], i, :], p2[i % 2][0:sizes[i], 0:D], b2[par][0:sizes[i], :], ALU.add).then_inc(S.y_ready, 1)
                rounds(dve, body)

            @block.tensor
            def _(pe):
                pe.wait_ge(S.b1_in, 16)
                pe.transpose(p1[2][:, 0:EX * FC], b1n[:, :], m.ident[0:EX * FC, 0:EX * FC]).then_inc(S.b1_turned, 1)

                def body(e, par, k):
                    pe.wait_ge(S.ex_in[par], 80 * k + 80)
                    for c in range(2):
                        wait(pe, S.hT_made, 2 * e + c - 1)
                        for i in range(MT):
                            mm = pe.transpose(pt[c][:, 128 * i:128 * i + sizes[i]], hb[par][0:sizes[i], i, c * 128:(c + 1) * 128],
                                              m.ident[0:sizes[i], 0:sizes[i]])
                        mm.then_inc(S.hb_turned, 1)
                    pe.wait_ge(S.hT_made, 2 * e + 2)
                    for f in range(FC):
                        wait(pe, S.hm_made, FC * e + f - 1)
                        for c in range(2):
                            mm = pe.matmul(p1[f % 2][:, 0:CAP], w1[par][:, c, f * 128:(f + 1) * 128], hT[:, c, 0:CAP], start=(c == 0), stop=(c == 1))
                        mm.then_inc(S.up_prod, 1)
                    pe.wait_ge(S.hm_made, FC * e + FC)
                    for i in range(MT):
                        wait(pe, S.y_ready, MT * e + i - 1)
                        for f in range(FC):
                            mm = pe.matmul(p2[i % 2][0:sizes[i], 0:D], hm[:, f, 128 * i:128 * i + sizes[i]], w2[par][:, f, :],
                                           start=(f == 0), stop=(f == FC - 1))
                        mm.then_inc(S.down_prod, 1)
                rounds(pe, body)


def combine(nc, m, out):
    B = 4
    with ExitStack() as ctx:
        def sb(n, s, d=F32):
            return ctx.enter_context(nc.sbuf_tensor(n, s, d))
        y = sb("cb_y", [TT, NT, D])
        lo = sb("cb_lo", [TT, 2, D])
        hi = sb("cb_hi", [TT, 2, D])
        fin = sb("cb_fin", [TT, 2, D], I32)
        S = m.sem
        prb = m.prb.rearrange("p (t o) -> p t o", o=1)
        with nc.Block() as block:
            @block.gpsimd
            def _(pool):
                for t in range(NT):
                    wait(pool, S.out_made, t - U + 1)
                    pool.indirect_dma_start(y[:, t, :], None, m.y_d,
                                            bass.IndirectOffsetOnAxis(ap=m.slot_i[:, t:t + 1].bitcast(U32), axis=0)).then_inc(S.arrived[t % U], 16)

            @block.vector
            def _(dve):
                st = m.dve_steps.on(dve)
                for t in range(NT):
                    dve.wait_ge(S.arrived[t % U], 16 * (2 * CH + 1 + t // U))
                    st.link(dve.tensor_scalar(y[:, t, :], y[:, t, :], m.prb[:, t:t + 1], None, ALU.mult))
                    p = t % 2
                    st.then(dve.tensor_scalar(fin[:, p, :], y[:, t, :], 0.0, 0.0, ALU.mult, ALU.is_equal))
                    st.then(dve.tensor_scalar(lo[:, p, :], y[:, t, :], 0.0, -1.0e4, ALU.min, ALU.max))
                    st.link(dve.tensor_scalar(hi[:, p, :], y[:, t, :], 0.0, 1.0e4, ALU.max, ALU.min))
                    st.link(dve.tensor_tensor(lo[:, p, :], lo[:, p, :], hi[:, p, :], ALU.add))
                    st.link(dve.copy_predicated(lo[:, p, :], fin[:, p, :], y[:, t, :]))
                    dve.tensor_tensor(m.base[:, t, :], m.base[:, t, :], lo[:, p, :], ALU.add).then_inc(S.out_made, 1)

            @block.sync
            def _(sp):
                ot = out.rearrange("(t p) d -> p t d", p=TT)
                for t in range(NT):
                    sp.wait_ge(S.out_made, t + 1)
                    sp.dma_start(ot[:, t, :], m.base[:, t, :]).then_inc(S.out_stored, 16)
                sp.wait_ge(S.out_stored, 16 * NT)


SEMS = """dve_step xr_made qr_made hr_made edges_in tbl_const last_in keys_out keys_made tbl_iota ident_zero ident_made
rows_known before_made rows_counted tbl_turned w_in b_in bo_in zero_made zero_out qkv_out mixv_one squared base_x
var_made std_made xn_made w_ready ss_made norm_made rms_made projected w_turned w_evac xn_turned xnT_made mix_out
mem_in la_const y_scaled kmax1 q_shifted kmax_turned kmax2 kmax_row kmax3 kmax_wide k_shifted mem_turned mem_ready
q_exp q_soft ctx_made cd_made cd_turned cdT_made wc_prod wc_made y_prod y_made y_squared yss_made ynorm_made mk_exp
k_exp q_turned qT_made idx1 idx2 loc_in hotT_made q_spread prod_made reduced sc_made sc_turned scT_made s_stored
key_in s_in p_made p_stored seg_const ends_made ends_turned carry_made carry_turned s_shifted p_turned p_in summed
p_e_made pv_made hot_made added gate_in an_turned an_made out_prod x2_made x2_stats var2_made std2_made h_made
logit_prod logit_made anT_made rt_const rt_c0 slots_known rows_put l_shifted l_exp b1_in b1_turned b1_made hot_ready
counted y_stored hb_turned up_prod hT_made down_prod hm_made y_ready out_made out_stored""".split()


class Signals:

    def __init__(self, names, new):
        (self.dve_step, self.xr_made, self.qr_made, self.hr_made, self.edges_in, self.tbl_const, self.last_in,
         self.keys_out, self.keys_made, self.tbl_iota, self.ident_zero, self.ident_made, self.rows_known,
         self.before_made, self.rows_counted, self.tbl_turned, self.w_in, self.b_in, self.bo_in, self.zero_made,
         self.zero_out, self.qkv_out, self.mixv_one, self.squared, self.base_x, self.var_made, self.std_made,
         self.xn_made, self.w_ready, self.ss_made, self.norm_made, self.rms_made, self.projected, self.w_turned,
         self.w_evac, self.xn_turned, self.xnT_made, self.mix_out, self.mem_in, self.la_const, self.y_scaled,
         self.kmax1, self.q_shifted, self.kmax_turned, self.kmax2, self.kmax_row, self.kmax3, self.kmax_wide,
         self.k_shifted, self.mem_turned, self.mem_ready, self.q_exp, self.q_soft, self.ctx_made, self.cd_made,
         self.cd_turned, self.cdT_made, self.wc_prod, self.wc_made, self.y_prod, self.y_made, self.y_squared,
         self.yss_made, self.ynorm_made, self.mk_exp, self.k_exp, self.q_turned, self.qT_made, self.idx1, self.idx2,
         self.loc_in, self.hotT_made, self.q_spread, self.prod_made, self.reduced, self.sc_made, self.sc_turned,
         self.scT_made, self.s_stored, self.key_in, self.s_in, self.p_made, self.p_stored, self.seg_const,
         self.ends_made, self.ends_turned, self.carry_made, self.carry_turned, self.s_shifted, self.p_turned,
         self.p_in, self.summed, self.p_e_made, self.pv_made, self.hot_made, self.added, self.gate_in, self.an_turned,
         self.an_made, self.out_prod, self.x2_made, self.x2_stats, self.var2_made, self.std2_made, self.h_made,
         self.logit_prod, self.logit_made, self.anT_made, self.rt_const, self.rt_c0, self.slots_known, self.rows_put,
         self.l_shifted, self.l_exp, self.b1_in, self.b1_turned, self.b1_made, self.hot_ready, self.counted,
         self.y_stored, self.hb_turned, self.up_prod, self.hT_made, self.down_prod, self.hm_made, self.y_ready,
         self.out_made, self.out_stored) = (new(n) for n in names)


class Inputs:
    def __init__(self, x, src, dst, Wq, bq, Wk, bk, Wv, bv, Wo, bo, w_qkv, mem_kv, w_out, b_out, g_out, g_pre, gate_w,
                 gate_b, w1, b1, w2, b2):
        self.x = x
        self.src = src
        self.dst = dst
        self.Wq = Wq
        self.bq = bq
        self.Wk = Wk
        self.bk = bk
        self.Wv = Wv
        self.bv = bv
        self.Wo = Wo
        self.bo = bo
        self.w_qkv = w_qkv
        self.mem_kv = mem_kv
        self.w_out = w_out
        self.b_out = b_out
        self.g_out = g_out
        self.g_pre = g_pre
        self.gate_w = gate_w
        self.gate_b = gate_b
        self.w1 = w1
        self.b1 = b1
        self.w2 = w2
        self.b2 = b2


class Mem:
    pass


def graph_layer(nc, io, out, debug=False):
    m = Mem()
    scratch = "ExternalOutput" if debug else "Internal"

    def dram(n, s, d=F32):
        return nc.dram_tensor(n, s, d, kind=scratch).ap()
    m.edges = dram("edges_d", (EROWS, 256), I32)
    m.key = dram("key_d", ((SB + 1) * SL,))
    m.loc = dram("loc_d", (STEPS, 128), BF16)
    m.k_d = dram("k_d", (N, D))
    m.v_d = dram("v_d", (N, D))
    m.s_d = dram("s_d", (H, STEPS, 128))
    m.p_d = dram("p_d", (H, STEPS, 128))
    m.slots = dram("slots_d", (EX * CAP + N, D))
    m.y_d = dram("y_d", (EX * CAP, D))
    with ExitStack() as ctx:
        def sb(n, s, d=F32):
            return ctx.enter_context(nc.sbuf_tensor(n, s, d))
        def new(n):
            return ctx.enter_context(nc.semaphore(n))

        def several(n, count):
            return [new(f"{n}{i}") for i in range(count)]
        S = m.sem = Signals(SEMS, new)
        S.rows_in, S.x_in, S.kv_stored = several("rows_in", TG), several("x_in", 5), several("kv_stored", 2)
        S.arrived, S.ex_in = several("arrived", U), several("ex_in", 2)
        m.dve_steps = Steps(S.dve_step)
        m.base = sb("base", [TT, NT, D])
        m.ident = sb("ident", [128, 128])
        m.iota_w = sb("iota_w", [128, TT])
        m.iota_p = sb("iota_p", [128, 1])
        m.loc_e = sb("loc_e", [128, CH, U])
        m.pen_e = sb("pen_e", [128, CH, U])
        m.src_e = sb("src_e", [128, CH + 1, U], I32)
        m.win_of = sb("win_of", [1, CH, U], I32)
        m.idx = sb("idx", [128, U], I32)
        m.woT = sb("woT", [128, 2, D])
        m.logit = sb("logit", [TT, NT, EX])
        m.prb = sb("prb", [TT, NT])
        m.slot_i = sb("slot_i", [TT, NT], I32)
        m.q = sb("q", [TT, NT, D])
        edge_tables(nc, m, io)
        with ExitStack() as mix:
            def keep(n, c):
                return mix.enter_context(nc.sbuf_tensor(n, [TT, NT, c], F32))
            m.mixq, m.mixk, m.mixv, m.xn = keep("mixq", HID), keep("mixk", HID), keep("mixv", HID + 1), keep("xn", D)
            project(nc, m, io)
            linear_attention(nc, m, io)
        with ExitStack() as att:
            m.slot = att.enter_context(nc.sbuf_tensor("slot", [128, U, D], F32))
            scores(nc, m)
            m.agg = att.enter_context(nc.sbuf_tensor("agg", [TT, NT, D + H], F32))
            segment_softmax(nc, m)
            aggregate(nc, m)
            attention_out(nc, m, io)
        route(nc, m)
        experts(nc, m, io)
        combine(nc, m, out)


DEBUG = False
ARGS = {"x": "x", "src": "src", "dst": "dst", "Wq": "L0_gnn_Wq", "bq": "L0_gnn_bq", "Wk": "L0_gnn_Wk", "bk":
        "L0_gnn_bk", "Wv": "L0_gnn_Wv", "bv": "L0_gnn_bv", "Wo": "L0_gnn_Wo", "bo": "L0_gnn_bo", "w_qkv":
        "L0_mix_w_qkv", "mem_kv": "L0_mix_mem_kv", "w_out": "L0_mix_w_out", "b_out": "L0_mix_b_out", "g_out":
        "L0_mix_g_out", "g_pre": "L0_mix_g_pre", "gate_w": "L0_ffn_gate_w", "gate_b": "L0_ffn_gate_b", "w1":
        "L0_ffn_w1", "b1": "L0_ffn_b1", "w2": "L0_ffn_w2", "b2": "L0_ffn_b2"}
def kernel(**inputs):
    import concourse.bacc as _bacc
    from concourse.bass_utils import run_bass_kernel_spmd as _run

    nc = _bacc.Bacc("TRN2", target_bir_lowering=False, num_devices=1)
    arrays, params = {}, {}
    for short, name in ARGS.items():
        a = np.ascontiguousarray(inputs[name])
        arrays["in_" + short] = a
        params[short] = nc.dram_tensor("in_" + short, a.shape, mybir.dt.from_np(a.dtype), kind="ExternalInput").ap()
    out = nc.dram_tensor("out", (N, D), F32, kind="ExternalOutput").ap()
    graph_layer(nc, Inputs(**params), out, DEBUG)
    r = _run(nc, [arrays], core_ids=[0])
    return r.results[0]["out"]
```

```python
import numpy as np
import concourse.bass as bass
from concourse import mybir
from contextlib import ExitStack

F32 = mybir.dt.float32
I32 = mybir.dt.int32
U32 = mybir.dt.uint32
BF16 = mybir.dt.bfloat16
ALU = mybir.AluOpType
ACT = mybir.ActivationFunctionType
X = mybir.AxisListType.X
PE_ONLY = [mybir.EngineType.PE]
DVE_ONLY = [mybir.EngineType.DVE]

N, D, E = 3125, 256, 50000
TT, NT = 125, 25
H, HD = 8, 32
MH, MD, MEM, HID = 4, 32, 4, 128
QKV = 3 * HID
WALL = 3 * D + QKV
EX, FF = 8, 1024
CAP = -(-5 * N // (4 * EX))
U = 16
AHEAD = 6
EROWS = -(-(E // 128 + 1) // 8) * 8
STEPS = 416
CH = STEPS // U
TG, TP = 4, STEPS // 4
LG = 5
RG, RP = 4, EROWS // 4
VW = HD + 1
KV = D + H * VW
PAD_NODE = 4000.0
BIG = 1.0e30
RESET = 1.0e38
EPS = 1e-5
assert CH == NT + 1 and EROWS * 128 >= E and EROWS - 1 + NT <= STEPS and CAP == 489


def spread(ap, axis, n):
    a = ap.unsqueeze(axis)
    shape = list(a.shape)
    shape[axis] = n
    return a.to_broadcast(shape)


def flat(ap):
    return ap.rearrange("p a b -> p (a b)")


def at(t, i):
    if isinstance(i, int):
        return t[:, i]
    a = t[:, bass.ds(i, 1)]
    return a.squeeze(1)


def wait(eng, sem, value):
    if isinstance(value, int) and value <= 0:
        return
    eng.wait_ge(sem, value)


class Steps:

    def __init__(self, sem):
        self.eng, self.sem, self.c = None, sem, 0

    def on(self, eng):
        self.eng = eng
        return self

    def then(self, ins):
        ins.then_inc(self.sem, 1)
        self.c += 1

    def settle(self):
        self.eng.wait_ge(self.sem, self.c)

    def link(self, ins):
        self.then(ins)
        self.settle()


def mean_and_var(dve, st, stats, mean, var, tmp):
    st.then(dve.tensor_tensor(mean, stats[:, :, 1], stats[:, :, 4], ALU.add))
    st.then(dve.tensor_tensor(tmp, stats[:, :, 1], stats[:, :, 4], ALU.subtract))
    st.link(dve.tensor_tensor(var, stats[:, :, 2], stats[:, :, 5], ALU.add))
    st.then(dve.tensor_scalar(mean, mean, 0.5, None, ALU.mult))
    st.then(dve.tensor_scalar(var, var, 1.0 / D, EPS, ALU.mult, ALU.add))
    st.link(dve.tensor_tensor(tmp, tmp, tmp, ALU.mult))
    return dve.scalar_tensor_tensor(out=var, in0=tmp, scalar=0.25, in1=var, op0=ALU.mult, op1=ALU.add)


def edge_tables(nc, m, io):
    with ExitStack() as ctx:
        def sb(n, s, d=F32):
            return ctx.enter_context(nc.sbuf_tensor(n, s, d))
        wnat = sb("wnat", [128, 4, 2, D])
        sq = sb("sq", [TT, 2, D])
        padd = sb("padd", [1, EROWS * 128 - E], I32)
        pads = sb("pads", [1, EROWS * 128 - E], I32)
        last_i = sb("last_i", [RP, RG, 2 * 128], I32)
        last_f = sb("last_f", [RP, RG])
        thr = sb("thr", [RP, NT - 1])
        junk = sb("junk", [RP, NT - 1])
        wend = sb("wend", [RP, RG])
        wfound = sb("wfound", [RP, RG])
        pen2 = sb("pen2", [128, STEPS])
        loc_e = sb("loc_e", [128, STEPS])
        iota_i = sb("iota_i", [RP, STEPS])
        before = sb("before", [RP, RG, STEPS])
        ones = sb("ones_t", [RP, 2])
        step_no = sb("step_no", [TP, TG])
        row_no = sb("row_no", [TP, TG])
        row_i = sb("row_i", [TP, TG], I32)
        row_ib = sb("row_ib", [TP, TG], I32)
        win0 = sb("win0", [TP, TG])
        got = sb("got", [TP, TG, 2 * 128], I32)
        dst_f = sb("dst_f", [TP, TG, 128])
        src_f = sb("src_f", [TP, TG, 128])
        key = sb("key", [TP, TG, 128])
        loc16 = sb("loc16", [TP, TG, 128], BF16)
        drow = sb("drow", [2, STEPS])
        first_key = sb("first_key", [2, CH])
        front = sb("front", [1, 1])
        back = sb("back", [1, 1])
        xt = io.x.rearrange("(t p) d -> p t d", p=TT)
        psl = ctx.enter_context(nc.psum_tensor("psl", [128, TG, 128], F32))
        pss = ctx.enter_context(nc.psum_tensor("pss", [128, TG, 128], F32))
        psr = ctx.enter_context(nc.psum_tensor("psr", [128, 512], F32))
        pst = ctx.enter_context(nc.psum_tensor("pst", [128, 512], F32))
        pt = [ctx.enter_context(nc.psum_tensor(f"wpt{i}", [128, 512], F32)) for i in range(2)]
        S = m.sem
        with nc.Block() as block:
            @block.sync
            def _(sp):
                full = E // 128
                e2 = m.edges.rearrange("r (c e) -> r c e", c=2)
                ef = E - full * 128
                for c, a in ((0, io.dst), (1, io.src)):
                    sp.dma_start(e2[0:full, c, :], a[0:full * 128].rearrange("(r e) -> r e", e=128)).then_inc(S.edges_in, 16)
                    sp.dma_start(e2[full:full + 1, c, 0:ef], a[full * 128:E].rearrange("(r e) -> r e", r=1)).then_inc(S.edges_in, 16)
                sp.wait_ge(S.tbl_const, 5)
                for c, p in ((0, padd), (1, pads)):
                    sp.dma_start(e2[full:full + 1, c, ef:128], p[:, 0:128 - ef]).then_inc(S.edges_in, 16)
                    rest = EROWS - full - 1
                    sp.dma_start(e2[full + 1:EROWS, c, :], p[:, 0:rest * 128].rearrange("o (r e) -> o r e", r=rest)).then_inc(S.edges_in, 16)
                sp.dma_start(m.key[0:1].rearrange("(a n) -> a n", a=1), front[:, :]).then_inc(S.keys_out, 16)
                sp.dma_start(m.key[1 + STEPS * 128:2 + STEPS * 128].rearrange("(a n) -> a n", a=1), back[:, :]).then_inc(S.keys_out, 16)
                sp.wait_ge(S.edges_in, 128)
                sp.dma_start(last_i[:, :, :], m.edges.rearrange("(g p) c -> p g c", p=RP)).then_inc(S.last_in, 16)
                for g in range(NT // LG):
                    sp.dma_start(m.base[:, g * LG:(g + 1) * LG, :], xt[:, g * LG:(g + 1) * LG, :]).then_inc(S.x_in[g], 16)
                for w, a in enumerate((io.Wq, io.Wk, io.Wv, io.Wo)):
                    sp.dma_start(wnat[:, w, :, :], a.rearrange("(c p) i -> p c i", p=128)).then_inc(S.w_in, 16)
                sp.dma_start(m.wall[:, :, 3 * D:WALL], io.w_qkv.rearrange("(c p) n -> p c n", p=128)).then_inc(S.w_in, 16)
                sp.dma_start(m.gpre[:, :], io.g_pre.rearrange("(c p) -> p c", p=128), allow_slow_non_contiguous=True).then_inc(S.w_in, 16)
                for i, b in enumerate((io.bq, io.bk, io.bv)):
                    sp.dma_start(m.bqkv[:, i * D:(i + 1) * D], b.partition_broadcast(TT)).then_inc(S.b_in, 16)
                sp.dma_start(m.bo[:, :], io.bo.partition_broadcast(TT)).then_inc(S.bo_in, 16)
                sp.wait_ge(S.keys_made, 1)
                for g in range(TG):
                    o = 1 + g * TP * 128
                    sp.dma_start(m.key[o:o + TP * 128].rearrange("(p e) -> p e", p=TP), key[:, g, :]).then_inc(S.keys_out, 16)
                sp.dma_start(m.loc.rearrange("(g p) e -> p g e", p=TP), loc16[:, :, :]).then_inc(S.keys_out, 16)
                sp.wait_ge(S.keys_out, 16 * (3 + TG))
                first = bass.AP(m.key.tensor, 1, [[0, 2], [U * 128, CH], [1, 1]])
                sp.dma_start(first_key[:, :].unsqueeze(2), first, allow_slow_non_contiguous=True).then_inc(S.first_in, 16)

            @block.gpsimd
            def _(pool):
                pool.memset(padd[:], int(PAD_NODE)).then_inc(S.tbl_const, 1)
                pool.memset(pads[:], 0).then_inc(S.tbl_const, 1)
                pool.memset(front[:], -1.0).then_inc(S.tbl_const, 1)
                pool.memset(back[:], 1.0e6).then_inc(S.tbl_const, 1)
                pool.memset(m.src_e[:, CH, :], 0).then_inc(S.tbl_const, 1)
                pool.iota(thr[:, :], pattern=[[TT, NT - 1]], base=TT, channel_multiplier=0, allow_small_or_imprecise_dtypes=True).then_inc(S.tbl_iota, 1)
                pool.iota(iota_i[:, :], pattern=[[1, STEPS]], base=0, channel_multiplier=0, allow_small_or_imprecise_dtypes=True).then_inc(S.tbl_iota, 1)
                pool.iota(wend[:, :], pattern=[[RP, RG]], base=0, channel_multiplier=1, allow_small_or_imprecise_dtypes=True).then_inc(S.tbl_iota, 1)
                pool.iota(step_no[:, :], pattern=[[TP, TG]], base=0, channel_multiplier=1, allow_small_or_imprecise_dtypes=True).then_inc(S.tbl_iota, 1)
                pool.memset(ones[:], 1.0).then_inc(S.tbl_iota, 1)
                pool.memset(m.one_col[:], 1.0)
                pool.memset(m.ident[:], 0.0).then_inc(S.ident_zero, 1)
                pool.wait_ge(S.ident_zero, 1)
                pool.affine_select(out=m.ident[:, :], in_=m.ident[:, :], compare_op=ALU.not_equal, fill=1.0, base=0,
                                   pattern=[[-1, 128]], channel_multiplier=1).then_inc(S.ident_made, 1)
                pool.iota(m.iota_w[:, :], pattern=[[1, TT]], base=0, channel_multiplier=0, allow_small_or_imprecise_dtypes=True).then_inc(S.ident_made, 1)
                pool.iota(m.iota_p[:, :], pattern=[[0, 1]], base=0, channel_multiplier=1, allow_small_or_imprecise_dtypes=True).then_inc(S.ident_made, 1)
                pool.wait_ge(S.rows_known, 1)
                pool.wait_ge(S.edges_in, 128)
                for g in range(TG):
                    pool.indirect_dma_start(got[:, g, :], None, m.edges,
                                            bass.IndirectOffsetOnAxis(ap=row_i[:, g:g + 1].bitcast(U32), axis=0)).then_inc(S.rows_in[g], 16)

            @block.vector
            def _(dve):
                st = m.dve_steps.on(dve)

                def normalise(g):
                    dve.wait_ge(S.x_in[g], 16)
                    r = slice(g * LG, (g + 1) * LG)
                    for t in range(g * LG, (g + 1) * LG):
                        st.then(dve.bn_stats(m.stats[:, t, :], m.base[:, t, :]))
                    st.settle()
                    mean_and_var(dve, st, m.stats[:, r, :], m.mean[:, r], m.var[:, r], m.rms[:, r]).then_inc(S.var_made, 1)
                    dve.wait_ge(S.std_made, g + 1)
                    st.link(dve.reciprocal(m.rstd[:, r], m.rstd[:, r]))
                    for t in range(g * LG, (g + 1) * LG):
                        dve.tensor_scalar(m.xn[:, t, :], m.base[:, t, :], m.mean[:, t:t + 1], m.rstd[:, t:t + 1], ALU.subtract,
                                          ALU.mult).then_inc(S.xn_made, 1)
                    if g == 1:
                        dve.wait_ge(S.w_in, 96)
                        for c in range(2):
                            dve.tensor_scalar(m.wall[:, c, 3 * D:WALL], m.wall[:, c, 3 * D:WALL], m.gpre[:, c:c + 1], None,
                                              ALU.mult).then_inc(S.w_ready, 1)
                    dve.wait_ge(S.squared, (g + 1) * LG)
                    dve.tensor_scalar(m.ss[:, r], m.ss[:, r], 1e-24, None, ALU.max).then_inc(S.ss_made, 1)
                    dve.wait_ge(S.norm_made, g + 1)
                    st.link(dve.reciprocal(m.rms[:, r], m.rms[:, r]))
                    dve.tensor_scalar(m.rms[:, r], m.rms[:, r], float(D) ** 0.5, None, ALU.mult).then_inc(S.rms_made, 1)

                dve.wait_ge(S.last_in, 16)
                dve.wait_ge(S.tbl_iota, 5)
                st.link(dve.tensor_copy(last_f[:, :], last_i[:, :, 127]))
                for g in range(RG):
                    st.link(dve.tensor_scalar(junk[:, :], thr[:, :], last_f[:, g:g + 1], 0.0, ALU.is_le, ALU.add,
                                              accum_out=wfound[:, g:g + 1]))
                st.link(dve.tensor_tensor(wend[:, :], wend[:, :], wfound[:, :], ALU.add))
                for g in range(RG):
                    last = dve.tensor_scalar(before[:, g, :], iota_i[:, :], wend[:, g:g + 1], None, ALU.is_gt)
                    st.then(last)
                st.settle()
                dve.sem_inc(S.before_made, 1)
                dve.wait_ge(S.rows_counted, 1)
                st.link(dve.tensor_copy(row_no[:, :], psr[0:TP, 0:TG]))
                dve.tensor_copy(row_i[:, :], row_no[:, :]).then_inc(S.rows_known, 1)
                st.link(dve.tensor_tensor(win0[:, :], step_no[:, :], row_no[:, :], ALU.subtract))
                st.link(dve.tensor_scalar(win0[:, :], win0[:, :], float(TT), None, ALU.mult))
                st.link(dve.tensor_tensor(drow[:, :], iota_i[0:2, :], pst[0:2, 0:STEPS], ALU.subtract))
                st.link(dve.tensor_scalar(m.win_of.rearrange("p a b -> p (a b)"), drow[0:1, :], 0.0, float(NT - 1), ALU.max, ALU.min))
                normalise(0)
                for g in range(TG):
                    dve.wait_ge(S.rows_in[g], 16)
                    st.then(dve.tensor_copy(src_f[:, g, :], got[:, g, 128:256]))
                    st.link(dve.tensor_copy(dst_f[:, g, :], got[:, g, 0:128]))
                    st.link(dve.tensor_scalar(dst_f[:, g, :], dst_f[:, g, :], win0[:, g:g + 1], None, ALU.subtract))
                    st.then(dve.tensor_scalar(key[:, g, :], dst_f[:, g, :], 0.0, float(TT - 1), ALU.max, ALU.min))
                    st.link(dve.tensor_scalar(dst_f[:, g, :], dst_f[:, g, :], -1.0, float(TT), ALU.max, ALU.min))
                    st.then(dve.tensor_scalar(key[:, g, :], key[:, g, :], win0[:, g:g + 1], None, ALU.add))
                    st.then(dve.tensor_copy(loc16[:, g, :], dst_f[:, g, :]))
                st.settle()
                dve.sem_inc(S.keys_made, 1)
                dve.wait_ge(S.tbl_turned, 1)
                dve.wait_ge(S.tbl_const, 5)
                le = loc_e[:, :]
                pe_ = m.pen_e.rearrange("p a b -> p (a b)")
                for g in range(TG):
                    st.then(dve.tensor_copy(le[:, g * TP:(g + 1) * TP], psl[:, g, 0:TP]))
                    st.then(dve.tensor_copy(m.src_e.rearrange("p a b -> p (a b)")[:, g * TP:(g + 1) * TP], pss[:, g, 0:TP]))
                st.settle()
                st.then(dve.tensor_scalar(pe_, le, 0.0, -BIG, ALU.is_lt, ALU.mult))
                st.link(dve.tensor_scalar(pen2[:, :], le, float(TT) - 0.5, -BIG, ALU.is_gt, ALU.mult))
                st.link(dve.tensor_tensor(pe_, pe_, pen2[:, :], ALU.add))
                for g in range(1, NT // LG):
                    normalise(g)
                dve.wait_ge(S.first_in, 16)
                dve.scalar_tensor_tensor(out=m.first_loc[:, :], in0=drow.rearrange("p (k u) -> p k u", u=U)[:, :, 0],
                                         scalar=-float(TT), in1=first_key[:, :], op0=ALU.mult, op1=ALU.add)
                dve.tensor_scalar(m.nloc_e.rearrange("p a b -> p (a b)"), le, -1.0, None, ALU.mult)

            @block.scalar
            def _(act):
                for g in range(NT // LG):
                    if g == 1:
                        for w in range(4):
                            act.wait_ge(S.w_turned, w + 1)
                            src = pt[w % 2][:, :].rearrange("p (i o) -> p i o", i=2)
                            dst = m.wall[:, :, w * D:(w + 1) * D] if w < 3 else m.woT[:, :, :]
                            act.activation(dst, src, ACT.Copy).then_inc(S.w_evac, 1)
                    act.wait_ge(S.var_made, g + 1)
                    act.activation(m.rstd[:, g * LG:(g + 1) * LG], m.var[:, g * LG:(g + 1) * LG], ACT.Sqrt).then_inc(S.std_made, 1)
                    for t in range(g * LG, (g + 1) * LG):
                        act.wait_ge(S.xn_made, t + 1)
                        wait(act, S.squared, t - 1)
                        act.activation(sq[:, t % 2, :], m.xn[:, t, :], ACT.Square, accum_out=m.ss[:, t:t + 1]).then_inc(S.squared, 1)
                    act.wait_ge(S.ss_made, g + 1)
                    act.activation(m.rms[:, g * LG:(g + 1) * LG], m.ss[:, g * LG:(g + 1) * LG], ACT.Sqrt).then_inc(S.norm_made, 1)

            @block.tensor
            def _(pe):
                pe.wait_ge(S.before_made, 1)
                for j in range(TG):
                    for g in range(RG):
                        pe.matmul(psr[0:TP, j:j + 1], before[:, g, j * TP:(j + 1) * TP], ones[:, 0:1], start=(g == 0), stop=(g == RG - 1))
                for g in range(RG):
                    last = pe.matmul(pst[0:2, 0:STEPS], ones[:, :], before[:, g, :], start=(g == 0), stop=(g == RG - 1))
                last.then_inc(S.rows_counted, 1)
                pe.wait_ge(S.ident_made, 3)
                pe.wait_ge(S.w_in, 96)
                for w in range(4):
                    wait(pe, S.w_evac, w - 1)
                    for i in range(2):
                        for o in range(2):
                            last = pe.transpose(pt[w % 2][:, i * D + o * 128:i * D + (o + 1) * 128],
                                                wnat[:, w, o, i * 128:(i + 1) * 128], m.ident[:, :])
                    last.then_inc(S.w_turned, 1)
                pe.wait_ge(S.w_evac, 4)

                pe.wait_ge(S.keys_made, 1)
                pe.wait_ge(S.ident_made, 3)
                for g in range(TG):
                    pe.transpose(psl[:, g, 0:TP], dst_f[:, g, :], m.ident[0:TP, 0:TP])
                    last = pe.transpose(pss[:, g, 0:TP], src_f[:, g, :], m.ident[0:TP, 0:TP])
                last.then_inc(S.tbl_turned, 1)


def project(nc, m, io):
    with ExitStack() as ctx:
        def sb(n, s, d=F32):
            return ctx.enter_context(nc.sbuf_tensor(n, s, d))
        wall, bqkv, bo, rms = m.wall, m.bqkv, m.bo, m.rms
        xr = sb("xr", [TT, 2, D])
        xnT = sb("xnT", [128, 2, 2, TT])
        kst = sb("kst", [TT, 2, D])
        vst = sb("vst", [TT, 2, H, VW])
        qf = sb("qf", [TT, D])
        qr = sb("q_rest", [TT, D])
        keys = sb("keys", [128, CH, 130])
        zero = sb("zero", [128, 4 * D])
        pt = [ctx.enter_context(nc.psum_tensor(f"pt{i}", [128, 512], F32)) for i in range(2)]
        pa = [ctx.enter_context(nc.psum_tensor(f"pa{i}", [TT, 512], F32)) for i in range(2)]
        pb = [ctx.enter_context(nc.psum_tensor(f"pb{i}", [TT, 512], F32)) for i in range(2)]
        pc = [ctx.enter_context(nc.psum_tensor(f"pc{i}", [TT, 512], F32)) for i in range(2)]
        S = m.sem

        def tiles(eng, body):
            body(0, 0, 0, False)
            body(1, 1, 0, False)
            body(2, 0, 1, False)
            with eng.Fori(2, 12) as k:
                body(2 * k - 1, 1, k - 1, False)
                body(2 * k, 0, k, False)
            body(23, 1, 11, False)
            body(24, 0, 12, True)

        with nc.Block() as block:
            @block.sync
            def _(sp):
                for h in range(H):
                    sp.dma_start(keys[h * U:(h + 1) * U, :, :], bass.AP(m.key.tensor, 0, [[128, U], [U * 128, CH], [1, 130]])).then_inc(S.key_in, 16)
                sp.wait_ge(S.zero_made, 1)
                rows = EX * CAP
                for r in range(0, rows, 512):
                    p = min(512, rows - r) // 4
                    sp.dma_start(m.slots[r:r + 4 * p, :].rearrange("(p a) d -> p (a d)", a=4), zero[0:p, :]).then_inc(S.zero_out, 16)

                def body(t, par, turn, last):
                    sp.wait_ge(S.qkv_out, t + 1)
                    rows = bass.ds(t * TT, TT)
                    sp.dma_start(m.kv_d[rows, 0:D], kst[:, par, :]).then_inc(S.kv_stored[par], 16)
                    sp.dma_start(m.kv_d[rows, D:KV], vst[:, par, :, :].rearrange("p h c -> p (h c)")).then_inc(S.kv_stored[par], 16)
                tiles(sp, body)
                sp.wait_ge(S.kv_stored[0], 13 * 32)
                sp.wait_ge(S.kv_stored[1], 12 * 32)
                sp.wait_ge(S.zero_out, 16 * (-(-rows // 512)))

            @block.gpsimd
            def _(pool):
                pool.memset(zero[:], 0.0).then_inc(S.zero_made, 1)
                pool.memset(m.mixv[:, :, HID:HID + 1], 1.0)
                pool.memset(vst[:, :, :, HD:VW], 1.0).then_inc(S.mixv_one, 1)
                pool.wait_ge(S.bo_in, 16)

                def body(t, par, turn, last):
                    pool.wait_ge(S.squared, t + 1)
                    pool.nop(nofuse=True)
                    if not (isinstance(t, int) and t < 2):
                        pool.wait_ge(S.xn_turned, t - 1)
                        pool.nop(nofuse=True)
                    pool.tensor_copy(xr[:, par, :], at(m.xn, t)).then_inc(S.xr_made, 1)
                    pool.tensor_tensor(at(m.base, t), at(m.base, t), at(m.xn, t), ALU.add).then_inc(S.base_x, 1)
                    pool.wait_ge(S.base_x, t + 1)
                    pool.nop(nofuse=True)
                    pool.tensor_tensor(at(m.base, t), at(m.base, t), bo[:, :], ALU.add)
                tiles(pool, body)

            @block.vector
            def _(dve):
                st = m.dve_steps.on(dve)
                dve.wait_ge(S.b_in, 48)
                dve.wait_ge(S.key_in, 16 * H)
                dve.wait_ge(S.mixv_one, 1)

                def borders(c):
                    kc = at(keys, c)
                    dve.tensor_tensor(at(m.fwd, c), kc[:, 1:129], kc[:, 0:128], ALU.not_equal).then_inc(S.borders_made, 1)
                    dve.tensor_tensor(at(m.bwd, c), kc[:, 1:129], kc[:, 2:130], ALU.not_equal).then_inc(S.borders_made, 1)

                def penalties(c):
                    dve.wait_ge(S.borders_made, 2 * c + 2)
                    for i, b in enumerate((m.fwd, m.bwd)):
                        dve.tensor_scalar(at(b, c), at(b, c), -RESET, None, ALU.mult).then_inc(S.costs_made, 1)

                def any_border(c):
                    dve.wait_ge(S.costs_made, 2 * c + 2)
                    for i, b in enumerate((m.fwd, m.bwd)):
                        dve.tensor_reduce(at(m.edge_any, c)[:, i:i + 1], at(b, c), X, ALU.min)

                def body(t, par, turn, last):
                    q3 = at(m.q3, t)
                    dve.wait_ge(S.projected, t + 1)
                    wait(dve, S.kv_stored[par], 32 * turn)
                    wait(dve, S.q_split, 3 * t)
                    dve.tensor_tensor(qf[:, :], pa[par][:, 0:D], bqkv[:, 0:D], ALU.add).then_inc(S.q_whole, 1)
                    dve.tensor_tensor(kst[:, par, :], pa[par][:, D:2 * D], bqkv[:, D:2 * D], ALU.add)
                    dve.tensor_tensor(vst[:, par, :, 0:HD], pb[par][:, 0:D].rearrange("p (h d) -> p h d", h=H),
                                      bqkv[:, 2 * D:3 * D].rearrange("p (h d) -> p h d", h=H), ALU.add).then_inc(S.qkv_out, 1)
                    dve.wait_ge(S.q_whole, t + 1)
                    dve.tensor_copy(q3[:, 0, :], qf[:, :]).then_inc(S.q_split, 1)
                    borders(t + 1)
                    penalties(t)
                    dve.wait_ge(S.q_split, 3 * t + 1)
                    dve.tensor_tensor(qr[:, :], qf[:, :], q3[:, 0, :], ALU.subtract).then_inc(S.q_rest, 1)
                    dve.wait_ge(S.q_rest, t + 1)
                    dve.tensor_copy(q3[:, 1, :], qr[:, :]).then_inc(S.q_split, 1)
                    any_border(t)
                    dve.wait_ge(S.q_split, 3 * t + 2)
                    dve.tensor_tensor(q3[:, 2, :], qr[:, :], q3[:, 1, :], ALU.subtract).then_inc(S.q_split, 1)
                borders(0)
                tiles(dve, body)
                penalties(NT)
                any_border(NT)
            @block.scalar
            def _(act):
                def turn_out(t, par):
                    act.wait_ge(S.xn_turned, t + 1)
                    wait(act, S.projected, t - 1)
                    act.activation(xnT[:, par, :, :], pt[par][:, 0:2 * TT].rearrange("p (c n) -> p c n", c=2), ACT.Copy).then_inc(S.xnT_made, 1)

                def body(t, par, turn, last):
                    if not last:
                        turn_out(t + 1, 1 - par)
                    act.wait_ge(S.projected, t + 1)
                    if isinstance(t, int) and t == 0:
                        act.wait_ge(S.rms_made, NT // LG)
                    r = at(rms.rearrange("p (t o) -> p t o", o=1), t)
                    act.activation(at(m.mixq, t), pc[par][:, 0:HID], ACT.Copy, scale=r)
                    act.activation(at(m.mixk, t), pc[par][:, HID:2 * HID], ACT.Copy, scale=r)
                    act.activation(at(m.mixv, t)[:, 0:HID], pc[par][:, 2 * HID:3 * HID], ACT.Copy, scale=r).then_inc(S.mix_out, 1)
                turn_out(0, 0)
                tiles(act, body)

            @block.tensor
            def _(pe):
                def turn_in(t, par):
                    pe.wait_ge(S.xr_made, t + 1)
                    wait(pe, S.xnT_made, t - 1)
                    for c in range(2):
                        last = pe.transpose(pt[par][:, c * TT:(c + 1) * TT], xr[:, par, c * 128:(c + 1) * 128], m.ident[0:TT, 0:TT])
                    last.then_inc(S.xn_turned, 1)

                def body(t, par, turn, last):
                    if not last:
                        turn_in(t + 1, 1 - par)
                    pe.wait_ge(S.xnT_made, t + 1)
                    wait(pe, S.qkv_out, t - 1)
                    wait(pe, S.mix_out, t - 1)
                    for dst, a, b in ((pa, 0, 2 * D), (pb, 2 * D, 3 * D), (pc, 3 * D, WALL)):
                        for c in range(2):
                            mm = pe.matmul(dst[par][:, 0:b - a], xnT[:, par, c, :], wall[:, c, a:b], start=(c == 0), stop=(c == 1))
                    mm.then_inc(S.projected, 1)
                turn_in(0, 0)
                pe.wait_ge(S.w_ready, 2)
                tiles(pe, body)


def linear_attention(nc, m, io):
    with ExitStack() as ctx:
        def sb(n, s, d=F32):
            return ctx.enter_context(nc.sbuf_tensor(n, s, d))

        def ps(n, s):
            return ctx.enter_context(nc.psum_tensor(n, s, F32))
        qmax = sb("qmax", [TT, NT * MH])
        kpart = sb("kpart", [TT, HID])
        kmax = sb("kmax", [128, 2])
        mk = sb("mk", [128, MEM])
        mvm = sb("mvm", [128, MEM])
        kmrow = sb("kmrow", [1, HID])
        ones = sb("ones_m", [1, TT])
        memk = sb("memk", [MEM, HID])
        memv = sb("memv", [MEM, HID + 1])
        wo = sb("w_out_sb", [128, D])
        cd = sb("cd", [128, HID])
        cdT = sb("cdT", [128, HID])
        csum = sb("csum", [128, 1])
        wc = sb("wc", [128, D])
        bout = sb("bout", [TT, D])
        gout = sb("gout", [TT, D])
        qr = sb("qr", [TT, 2, HID])
        qT = sb("qT", [128, 2, TT])
        ysq = sb("ysq", [TT, 2, D])
        yss = sb("yss", [TT, NT])
        p1, p2, p3 = ps("p1", [128, 512]), ps("p2", [128, 512]), ps("p3", [128, 512])
        pq = [ps(f"pq{i}", [128, 512]) for i in range(2)]
        py = [ps(f"py{i}", [TT, 512]) for i in range(2)]
        S = m.sem
        y = m.xn
        qv = m.mixq.rearrange("p t (h d) -> p (t h) d", h=MH)
        qf = m.mixq.rearrange("p t c -> p (t c)")
        kf = m.mixk.rearrange("p t c -> p (t c)")
        with nc.Block() as block:
            @block.sync
            def _(sp):
                mem = io.mem_kv.rearrange("a h d m -> a (h d) m")
                sp.dma_start(mk[:, :], mem[0]).then_inc(S.mem_in, 16)
                sp.dma_start(mvm[:, :], mem[1]).then_inc(S.mem_in, 16)
                sp.dma_start(wo[:, :], io.w_out).then_inc(S.mem_in, 16)
                sp.dma_start(bout[:, :], io.b_out.partition_broadcast(TT)).then_inc(S.mem_in, 16)
                sp.dma_start(gout[:, :], io.g_out.partition_broadcast(TT)).then_inc(S.mem_in, 16)

            @block.gpsimd
            def _(pool):
                pool.memset(ones[:], 1.0).then_inc(S.la_const, 1)
                pool.memset(memv[:], 1.0).then_inc(S.la_const, 1)
                pool.memset(cd[:], 0.0).then_inc(S.la_const, 1)

                def stage(t, par):
                    if not (isinstance(t, int) and t < 2):
                        pool.wait_ge(S.q_turned, t - 1)
                        pool.nop(nofuse=True)
                    pool.tensor_copy(qr[:, par, :], at(m.mixq, t)).then_inc(S.qr_made, 1)
                pool.wait_ge(S.q_soft, 1)
                for t in range(3):
                    stage(t, t % 2)
                with pool.Fori(2, 13) as k:
                    stage(2 * k - 1, 1)
                    stage(2 * k, 0)
                with pool.Fori(0, NT) as t:
                    pool.wait_ge(S.y_scaled, t + 1)
                    pool.nop(nofuse=True)
                    pool.tensor_tensor(at(m.base, t), at(m.base, t), at(y, t), ALU.add)

            @block.vector
            def _(dve):
                st = m.dve_steps.on(dve)
                dve.tensor_reduce(kpart[:, :], m.mixk.rearrange("p t c -> p c t"), X, ALU.max).then_inc(S.kmax1, 1)
                st.link(dve.tensor_reduce(qmax[:, :], qv, X, ALU.max))
                dve.tensor_tensor(qv, qv, spread(qmax[:, :], 2, MD), ALU.subtract).then_inc(S.q_shifted, 1)
                dve.wait_ge(S.mem_in, 80)
                st.then(dve.tensor_reduce(kmax[:, 0:1], mk[:, :], X, ALU.max))
                dve.wait_ge(S.kmax_turned, 1)
                st.link(dve.tensor_reduce(kmax[:, 1:2], p1[:, 0:TT], X, ALU.max))
                st.link(dve.tensor_tensor(kmax[:, 0:1], kmax[:, 0:1], kmax[:, 1:2], ALU.max))
                dve.tensor_scalar(mk[:, :], mk[:, :], kmax[:, 0:1], None, ALU.subtract).then_inc(S.kmax2, 1)
                dve.wait_ge(S.kmax_row, 1)
                dve.tensor_copy(kmrow[:, :], p2[0:1, 0:HID]).then_inc(S.kmax3, 1)
                dve.wait_ge(S.kmax_wide, 1)
                dve.tensor_tensor(m.mixk[:, :, :], m.mixk[:, :, :], spread(p3[0:TT, 0:HID], 1, NT), ALU.subtract).then_inc(S.k_shifted, 1)
                dve.wait_ge(S.mem_turned, 1)
                dve.wait_ge(S.la_const, 3)
                dve.tensor_copy(memk[:, :], p2[0:MEM, 128:256])
                dve.tensor_copy(memv[:, 0:HID], p2[0:MEM, 256:384]).then_inc(S.mem_ready, 1)
                dve.wait_ge(S.q_exp, 1)
                st.link(dve.tensor_reduce(qmax[:, :], qv, X, ALU.add))
                st.link(dve.reciprocal(qmax[:, :], qmax[:, :]))
                dve.tensor_tensor(qv, qv, spread(qmax[:, :], 2, MD), ALU.mult).then_inc(S.q_soft, 1)
                st.then(dve.tensor_scalar(gout[:, :], gout[:, :], float(D) ** 0.5, None, ALU.mult))
                dve.wait_ge(S.ctx_made, 1)
                st.link(dve.reciprocal(csum[:, :], p1[:, 128 + HID:129 + HID]))
                for h in range(MH):
                    r = slice(h * MD, (h + 1) * MD)
                    last = dve.tensor_scalar(cd[r, r], p1[r, 128 + h * MD:128 + (h + 1) * MD], csum[r, 0:1], float(MD) ** -0.5, ALU.mult, ALU.mult)
                last.then_inc(S.cd_made, 1)
                dve.wait_ge(S.cd_turned, 1)
                dve.tensor_copy(cdT[:, :], p3[:, 0:HID]).then_inc(S.cdT_made, 1)
                dve.wait_ge(S.wc_prod, 1)
                dve.tensor_copy(wc[:, :], p3[:, 128:128 + D]).then_inc(S.wc_made, 1)

                def body(t, par):
                    dve.wait_ge(S.y_prod, t + 1)
                    dve.tensor_tensor(at(y, t), py[par][:, 0:D], bout[:, :], ALU.add).then_inc(S.y_made, 1)
                for t in range(3):
                    body(t, t % 2)
                with dve.Fori(2, 13) as k:
                    body(2 * k - 1, 1)
                    body(2 * k, 0)
                dve.wait_ge(S.y_squared, NT)
                dve.tensor_scalar(yss[:, :], yss[:, :], 1e-24, None, ALU.max).then_inc(S.yss_made, 1)
                dve.wait_ge(S.ynorm_made, 1)
                st.link(dve.reciprocal(yss[:, :], yss[:, :]))
                with dve.Fori(0, NT) as t:
                    dve.scalar_tensor_tensor(out=at(y, t), in0=at(y, t), scalar=at(yss.rearrange("p (t o) -> p t o", o=1), t),
                                             in1=gout[:, :], op0=ALU.mult, op1=ALU.mult).then_inc(S.y_scaled, 1)

            @block.scalar
            def _(act):
                act.wait_ge(S.q_shifted, 1)
                act.activation(qf, qf, ACT.Exp).then_inc(S.q_exp, 1)
                act.wait_ge(S.kmax2, 1)
                act.activation(mk[:, :], mk[:, :], ACT.Exp).then_inc(S.mk_exp, 1)
                act.wait_ge(S.k_shifted, 1)
                act.activation(kf, kf, ACT.Exp).then_inc(S.k_exp, 1)

                def body(t, par):
                    act.wait_ge(S.q_turned, t + 1)
                    wait(act, S.y_prod, t - 1)
                    act.activation(qT[:, par, :], pq[par][:, 0:TT], ACT.Copy).then_inc(S.qT_made, 1)

                def square(t, par):
                    act.wait_ge(S.y_made, t + 1)
                    wait(act, S.y_squared, t - 1)
                    act.activation(ysq[:, par, :], at(y, t), ACT.Square, accum_out=at(yss.rearrange("p (t o) -> p t o", o=1), t)).then_inc(S.y_squared, 1)
                body(0, 0)
                for t in range(1, 4):
                    body(t, t % 2)
                    square(t - 1, (t - 1) % 2)
                with act.Fori(2, 12) as k:
                    body(2 * k, 0)
                    square(2 * k - 1, 1)
                    body(2 * k + 1, 1)
                    square(2 * k, 0)
                body(24, 0)
                square(23, 1)
                square(24, 0)
                act.wait_ge(S.yss_made, 1)
                act.activation(yss[:, :], yss[:, :], ACT.Sqrt).then_inc(S.ynorm_made, 1)

            @block.tensor
            def _(pe):
                pe.wait_ge(S.kmax1, 1)
                pe.transpose(p1[:, 0:TT], kpart[:, :], m.ident[0:TT, 0:TT]).then_inc(S.kmax_turned, 1)
                pe.wait_ge(S.kmax2, 1)
                pe.transpose(p2[0:1, 0:HID], kmax[:, 0:1], m.ident[:, :]).then_inc(S.kmax_row, 1)
                pe.wait_ge(S.kmax3, 1)
                pe.wait_ge(S.la_const, 1)
                pe.matmul(p3[0:TT, 0:HID], ones[:, :], kmrow[:, :], start=True, stop=True).then_inc(S.kmax_wide, 1)
                pe.wait_ge(S.mk_exp, 1)
                pe.transpose(p2[0:MEM, 128:256], mk[:, :], m.ident[:, :])
                pe.transpose(p2[0:MEM, 256:384], mvm[:, :], m.ident[:, :]).then_inc(S.mem_turned, 1)
                pe.wait_ge(S.k_exp, 1)
                for t in range(NT):
                    pe.matmul(p1[:, 128:129 + HID], m.mixk[:, t, :], m.mixv[:, t, :], start=(t == 0), stop=False)
                pe.wait_ge(S.mem_ready, 1)
                pe.matmul(p1[:, 128:129 + HID], memk[:, :], memv[:, :], start=False, stop=True).then_inc(S.ctx_made, 1)
                pe.wait_ge(S.cd_made, 1)
                pe.transpose(p3[:, 0:HID], cd[:, :], m.ident[:, :]).then_inc(S.cd_turned, 1)
                pe.wait_ge(S.cdT_made, 1)
                pe.matmul(p3[:, 128:128 + D], cdT[:, :], wo[:, :], start=True, stop=True).then_inc(S.wc_prod, 1)
                pe.wait_ge(S.wc_made, 1)

                def turn(t, par):
                    pe.wait_ge(S.qr_made, t + 1)
                    wait(pe, S.qT_made, t - 1)
                    pe.transpose(pq[par][:, 0:TT], qr[:, par, :], m.ident[0:TT, 0:TT]).then_inc(S.q_turned, 1)

                def prod(t, par):
                    pe.wait_ge(S.qT_made, t + 1)
                    wait(pe, S.y_made, t - 1)
                    pe.matmul(py[par][:, 0:D], qT[:, par, :], wc[:, :], start=True, stop=True).then_inc(S.y_prod, 1)
                turn(0, 0)
                for t in range(1, 4):
                    turn(t, t % 2)
                    prod(t - 1, (t - 1) % 2)
                with pe.Fori(2, 12) as k:
                    turn(2 * k, 0)
                    prod(2 * k - 1, 1)
                    turn(2 * k + 1, 1)
                    prod(2 * k, 0)
                turn(24, 0)
                prod(23, 1)
                prod(24, 0)


(BORDER, BWD, LOCAL, ROWS, CARRY, CARRY_FLAT, KEEP, COLUMN, FORWARD, BACK_LOCAL, ROWS_BACK, CARRY_BACK, CARRY_BACK_FLAT, FALL,
 FALL_CAP, COLUMN_BACK, BACK, SHIFT, FIRST, FIRST_PAIR, FACTOR) = range(1, 22)
CHAIN = FACTOR
(PE_ENDS, PE_CARRY, PE_ENDS_BACK, PE_CARRY_BACK, PE_TURNED) = range(1, 6)
CHAIN_PE = PE_TURNED


def attention(nc, m):
    with ExitStack() as ctx:
        def sb(n, s, d=F32):
            return ctx.enter_context(nc.sbuf_tensor("at_" + n, s, d))

        def ps(n, s):
            return ctx.enter_context(nc.psum_tensor("at_" + n, s, F32))
        slot = sb("slot", [128, 2, U, KV])
        locrow = sb("locrow", [TT, U * 128], BF16)
        hotT = sb("hotT", [TT, U, 128], BF16)
        prod = sb("prod", [128, 2, 2, D])
        sc = sb("sc", [128, H, U])
        scp = sb("sc_pen", [128, H, U])
        bst = sb("border_st", [128, 2])
        bwd = sb("bwd_st", [128, 128], BF16)
        fm = sb("fwd_max", [128, 128])
        bm = sb("back_max", [128, 128])
        row = sb("row_f", [1, 2, H, U + 1])
        run = sb("run_f", [1, H, U + 1])
        rowb = sb("row_b", [1, 2, H, U + 1])
        runb = sb("run_b", [1, H, U + 1])
        line = sb("line", [1, 2, H, U])
        col = sb("col", [128, 2])
        pT = sb("pT", [128, 128])
        fall = sb("fall", [1, H])
        fall2 = sb("fall2", [2, H])
        pair = sb("pair", [2, TT])
        sign = sb("sign", [2, 2])
        fac = sb("fac", [TT, H])
        one = sb("one_c", [1, 1])
        habs = sb("habs", [128, 4, TT])
        hot = sb("hot", [128, 8, TT])
        pv = sb("pv", [128, 4, H, VW])
        pq = [ps(f"pq{i}", [128, 512]) for i in range(3)]
        pc = ps("pchain", [128, 512])
        pp = ps("pp", [128, 512])
        pa = [ps(f"pa{i}", [TT, 512]) for i in range(3)]
        S = m.sem
        scT = pc[:, 0:128]
        loc_c = m.loc.rearrange("(k i) e -> k (i e)", i=U)
        ph = pp[:, 0:128].rearrange("p (h i) -> p h i", h=H)

        def rounds(eng, body):
            body(0, None, 1, 0, 0)
            body(1, 0, 2, 1, 0)
            with eng.Fori(1, CH // 2 - 1) as k:
                body(2 * k, 2 * k - 1, 2 * k + 1, 0, k)
                body(2 * k + 1, 2 * k, 2 * k + 2, 1, k)
            body(CH - 2, CH - 3, CH - 1, 0, CH // 2 - 1)
            body(CH - 1, CH - 2, None, 1, CH // 2 - 1)
            body(None, CH - 1, None, 0, CH // 2)

        def windows_of(chunk, steps, engines):
            return nc.values_load_multi_w_load_instructions(
                flat(m.win_of[0:1, bass.ds(chunk, 1), steps]), engines=engines, min_val=0, max_val=NT - 1,
                skip_runtime_bounds_check_because="edge_tables clamps the windows to 0 .. NT - 1")[1]

        with nc.Block() as block:
            @block.sync
            def _(sp):
                def body(n, c, nxt, par, turn):
                    if n is not None:
                        wait(sp, S.hotT_made, n)
                        sp.dma_start(locrow[:, :], loc_c[bass.ds(n, 1), :].to_broadcast([TT, U * 128])).then_inc(S.loc_in, 16)
                rounds(sp, body)

            @block.gpsimd
            def _(pool):
                pool.memset(one[:], 1.0).then_inc(S.at_const, 1)
                pool.memset(row[:], -RESET).then_inc(S.at_const, 1)
                pool.memset(rowb[:], -RESET).then_inc(S.at_const, 1)
                pool.memset(fall2[:], 1.0).then_inc(S.at_const, 1)
                pool.iota(sign[:, 0:1], pattern=[[0, 1]], base=1, channel_multiplier=-2, allow_small_or_imprecise_dtypes=True).then_inc(S.at_const, 1)
                pool.iota(sign[:, 1:2], pattern=[[0, 1]], base=0, channel_multiplier=1, allow_small_or_imprecise_dtypes=True).then_inc(S.at_const, 1)
                for par in range(2):
                    for u in range(U):
                        pool.indirect_dma_start(slot[:, par, u, :], None, m.kv_d,
                                                bass.IndirectOffsetOnAxis(ap=m.src_e[:, par, u:u + 1].bitcast(U32), axis=0)).then_inc(S.arrived[par * 8 + u // 2], 16)
                with pool.Fori(1, CH // 2) as k:
                    for par in range(2):
                        for u in range(U):
                            if u % 4 == 0:
                                pool.wait_ge(S.idx_ready, 8 * k + 4 * par + u // 4 - 7)
                                pool.nop(nofuse=True)
                                pool.wait_ge(S.pv_made, 2 * U * k + U * par + u + 4 - 2 * U)
                                pool.nop(nofuse=True)
                            pool.indirect_dma_start(slot[:, par, u, :], None, m.kv_d,
                                                    bass.IndirectOffsetOnAxis(ap=m.idx[:, par, u:u + 1].bitcast(U32), axis=0)).then_inc(S.arrived[par * 8 + u // 2], 16)

            @block.scalar
            def _(act):
                def stage(c, par, q):
                    r = slice(4 * q, 4 * q + 4)
                    act.wait_ge(S.pv_made, U * c + 4 * q + 4)
                    act.activation(m.idx[:, par, r], at(m.src_e, c + 2)[:, r], ACT.Copy).then_inc(S.idx_ready, 1)

                def body(n, c, nxt, par, turn):
                    if c is None:
                        return
                    act.wait_ge(S.chain, CHAIN * c + FALL_CAP)
                    act.activation(fall2[0:1, :], fall[:, :], ACT.Exp, scale=float(HD) ** -0.5).then_inc(S.f_exp, 1)
                    act.wait_ge(S.chain, CHAIN * c + SHIFT)
                    act.activation(pT[:, :], pT[:, :], ACT.Exp, scale=float(HD) ** -0.5).then_inc(S.p_exp, 1)
                    for g in range(4):
                        wait(act, S.hot_made, 4 * c + g)
                        for u in range(4 * g, 4 * g + 4):
                            last = act.activation(habs[:, u % 4, :], m.iota_w[:, :], ACT.Abs, bias=at(m.nloc_e, c)[:, u:u + 1])
                        last.then_inc(S.hot_abs, 1)
                        act.wait_ge(S.hot_abs, 4 * c + g + 1)
                        wait(act, S.summed, U * c + 4 * g - 4)
                        act.activation(hot[:, 4 * (g % 2):4 * (g % 2) + 4, :], habs[:, :, :], ACT.Relu, bias=m.one_col[:, 0:1],
                                       scale=-1.0).then_inc(S.hot_made, 1)
                        if g and n is not None:
                            stage(c, 1 - par, g - 1)
                    if n is not None:
                        stage(c, 1 - par, 3)
                rounds(act, body)

            @block.vector
            def _(dve):
                def turned_hots(n):
                    dve.wait_ge(S.loc_in, 16 * n + 16)
                    wait(dve, S.q_spread, 8 * n)
                    dve.tensor_scalar(flat(hotT[:, :, :]), locrow[:, :], m.iota_p[0:TT, 0:1], None, ALU.is_equal).then_inc(S.hotT_made, 1)

                def reduce(n, j):
                    dve.wait_ge(S.prod_made, 8 * n + j + 1)
                    wait(dve, S.sc_made, n)
                    dve.tensor_reduce(sc[:, :, 2 * j:2 * j + 2].rearrange("p h i -> p i h"),
                                      prod[:, j % 2, :, :].rearrange("p i (h d) -> p i h d", h=H), X, ALU.add).then_inc(S.reduced, 1)

                def chain(c, piece):
                    def after(step):
                        dve.wait_ge(S.chain, CHAIN * c + step)

                    def turned(step):
                        dve.wait_ge(S.chain_pe, CHAIN_PE * c + step)

                    def then(ins):
                        ins.then_inc(S.chain, 1)
                    F = at(m.fwd, c)
                    if piece == 0:
                        dve.wait_ge(S.sc_turned, c + 1)
                        then(dve.tensor_copy(bst[:, :], at(m.edge_any, c)))
                        then(dve.tensor_copy(bwd[:, :], at(m.bwd, c)))
                        then(dve.tensor_tensor_scan(fm[:, :], F, scT, -RESET, ALU.add, ALU.max))
                    elif piece == 1:
                        turned(PE_ENDS)
                        then(dve.tensor_copy(row[:, :, :, 1:U + 1], pc[0:1, 128:384].rearrange("p (a h i) -> p a h i", a=2, h=H)))
                        after(ROWS)
                        then(dve.tensor_tensor_scan(run.rearrange("p h i -> p (h i)"), row[:, 1].rearrange("p h i -> p (h i)"),
                                                    row[:, 0].rearrange("p h i -> p (h i)"), -RESET, ALU.add, ALU.max))
                        after(CARRY)
                        then(dve.tensor_copy(line[:, 0, :, :], run[:, :, 0:U]))
                        then(dve.tensor_copy(row[:, 0, :, 0], run[:, :, U]))
                    elif piece == 2:
                        turned(PE_CARRY)
                        then(dve.tensor_copy(col[:, 0:1], pc[:, 384:385]))
                        after(COLUMN)
                        then(dve.tensor_tensor_scan(fm[:, :], F, scT, col[:, 0:1], ALU.add, ALU.max))
                    elif piece == 3:
                        after(FORWARD)
                        then(dve.tensor_tensor_scan(bm[:, ::-1], bwd[:, ::-1], fm[:, ::-1], -RESET, ALU.add, ALU.max))
                    elif piece == 4:
                        turned(PE_ENDS_BACK)
                        then(dve.tensor_copy(rowb[:, :, :, 0:U], pc[0:1, 128:384].rearrange("p (a h i) -> p a h i", a=2, h=H)))
                        after(ROWS_BACK)
                        then(dve.tensor_tensor_scan(runb.rearrange("p h i -> p (h i)")[:, ::-1],
                                                    rowb[:, 1].rearrange("p h i -> p (h i)")[:, ::-1],
                                                    rowb[:, 0].rearrange("p h i -> p (h i)")[:, ::-1], -RESET, ALU.add, ALU.max))
                        after(CARRY_BACK)
                        then(dve.tensor_copy(line[:, 1, :, :], runb[:, :, 1:U + 1]))
                        then(dve.tensor_tensor(fall[:, :], run[:, :, 0], runb[:, :, 0], ALU.subtract))
                        after(FALL)
                        then(dve.tensor_scalar(fall[:, :], fall[:, :], 0.0, None, ALU.min))
                    elif piece == 5:
                        turned(PE_CARRY_BACK)
                        then(dve.tensor_copy(col[:, 1:2], pc[:, 385:386]))
                        after(COLUMN_BACK)
                        then(dve.tensor_tensor_scan(bm[:, ::-1], bwd[:, ::-1], fm[:, ::-1], col[:, 1:2], ALU.add, ALU.max))
                        after(BACK)
                        then(dve.tensor_tensor(pT[:, :], scT, bm[:, :], ALU.subtract))
                    elif piece == 6:
                        after(SHIFT)
                        then(dve.tensor_scalar(pair[:, :], m.iota_w[0:2, :], at(m.first_loc.rearrange("p (k o) -> p k o", o=1), c), None, ALU.is_equal))
                        after(FIRST)
                        then(dve.tensor_scalar(pair[:, :], pair[:, :], sign[:, 0:1], sign[:, 1:2], ALU.mult, ALU.add))
                    else:
                        turned(PE_TURNED)
                        then(dve.tensor_copy(fac[:, :], pc[0:TT, 386:386 + H]))

                def add(c, u, wins):
                    dve.wait_ge(S.summed, U * c + u + 1)
                    wait(dve, S.added, U * c + u)
                    dst = at(m.agg, wins[u])
                    dve.tensor_tensor(dst, dst, pa[u % 3][:, 0:H * VW].rearrange("p (h c) -> p h c", h=H), ALU.add).then_inc(S.added, 1)

                def body(n, c, nxt, par, turn):
                    for j in range(8):
                        if n is not None:
                            dve.wait_ge(S.arrived[par * 8 + j], 32 * turn + 32)
                            dve.wait_ge(S.q_spread, 8 * n + j + 1)
                            wait(dve, S.reduced, 8 * n + j - 1)
                            dve.tensor_tensor(prod[:, j % 2, :, :], pq[j % 3][:, :].rearrange("p (i d) -> p i d", i=2),
                                              slot[:, par, 2 * j:2 * j + 2, 0:D], ALU.mult).then_inc(S.prod_made, 1)
                            if j:
                                reduce(n, j - 1)
                        if c is not None:
                            chain(c, j)
                    if n is not None:
                        reduce(n, 7)
                        if nxt is not None:
                            turned_hots(nxt)
                        dve.wait_ge(S.reduced, 8 * n + 8)
                        wait(dve, S.sc_turned, n)
                        dve.tensor_tensor(scp[:, :, :], sc[:, :, :], spread(at(m.pen_e, n), 1, H), ALU.add).then_inc(S.sc_made, 1)
                    if c is None:
                        return
                    wins = windows_of(c, slice(0, U), DVE_ONLY)
                    dve.wait_ge(S.chain, CHAIN * c + FACTOR)
                    wait(dve, S.added, U * c)
                    dst = at(m.agg, wins[0])
                    dve.tensor_tensor(dst, dst, spread(fac[:, :], 2, VW), ALU.mult).then_inc(S.rescaled, 1)
                    for u in range(U):
                        wait(dve, S.summed, U * c + u - 3)
                        dve.tensor_tensor(pv[:, u % 4, :, :], slot[:, 1 - par, u, D:KV].rearrange("p (h c) -> p h c", h=H),
                                          spread(ph[:, :, u], 2, VW), ALU.mult).then_inc(S.pv_made, 1)
                        if u == 3:
                            dve.wait_ge(S.rescaled, c + 1)
                        if u >= 3:
                            add(c, u - 3, wins)
                    for u in range(U - 3, U):
                        add(c, u, wins)
                turned_hots(0)
                dve.memset(m.agg.rearrange("p t h c -> p (t h c)"), 0.0).then_inc(S.at_const, 1)
                dve.wait_ge(S.at_const, 7)
                rounds(dve, body)

            @block.tensor
            def _(pe):
                def spread_q(n, u, window):
                    j = u // 2
                    if u % 2 == 0 and j >= 3:
                        wait(pe, S.prod_made, 8 * n + j - 2)
                    for part in range(3):
                        mm = pe.matmul(pq[j % 3][:, (u % 2) * D:(u % 2 + 1) * D], hotT[:, u, :], at(m.q3, window)[:, part, :],
                                       start=(part == 0), stop=(part == 2))
                    if u % 2:
                        mm.then_inc(S.q_spread, 1)

                def chain(c, piece):
                    if piece in (0, 2):
                        back = piece // 2
                        pe.wait_ge(S.chain, CHAIN * c + (BACK_LOCAL if back else LOCAL))
                        end = bm[:, 0:1] if back else fm[:, 127:128]
                        pe.transpose(pc[0:1, 128:256], end, m.ident[:, :])
                        pe.transpose(pc[0:1, 256:384], bst[:, back:back + 1], m.ident[:, :]).then_inc(S.chain_pe, 1)
                    elif piece in (1, 3):
                        back = piece // 2
                        pe.wait_ge(S.chain, CHAIN * c + (CARRY_BACK_FLAT if back else CARRY_FLAT))
                        pe.matmul(pc[:, 384 + back:385 + back], line[:, back].rearrange("p h i -> p (h i)"), one[:, :], start=True, stop=True).then_inc(S.chain_pe, 1)
                    else:
                        pe.wait_ge(S.p_exp, c + 1)
                        pe.transpose(pp[:, 0:128], pT[:, :], m.ident[:, :])
                        pe.wait_ge(S.f_exp, c + 1)
                        pe.wait_ge(S.chain, CHAIN * c + FIRST_PAIR)
                        pe.matmul(pc[0:TT, 386:386 + H], pair[:, :], fall2[:, :], start=True, stop=True).then_inc(S.chain_pe, 1)

                def body(n, c, nxt, par, turn):
                    if n is not None:
                        wins = windows_of(n, slice(AHEAD, U), PE_ONLY)
                    for j in range(8):
                        if n is not None and 2 * j >= AHEAD:
                            spread_q(n, 2 * j, wins[2 * j - AHEAD])
                            spread_q(n, 2 * j + 1, wins[2 * j + 1 - AHEAD])
                        if c is not None and j in (2, 3, 5, 6, 7):
                            chain(c, (2, 3, 5, 6, 7).index(j))
                    if nxt is not None:
                        ahead = windows_of(nxt, slice(0, AHEAD), PE_ONLY)
                    if n is not None:
                        pe.wait_ge(S.sc_made, n + 1)
                        if c is not None:
                            pe.wait_ge(S.chain, CHAIN * c + FACTOR)
                        pe.transpose(scT, scp[:, :, :].rearrange("p h i -> p (h i)"), m.ident[:, :]).then_inc(S.sc_turned, 1)
                    if c is None:
                        pe.wait_ge(S.hotT_made, nxt + 1)
                        for u in range(AHEAD):
                            spread_q(nxt, u, ahead[u])
                        return
                    for u in range(U):
                        if nxt is not None and u % 2 == 0 and u >= U - 2 * AHEAD:
                            if u == U - 2 * AHEAD:
                                pe.wait_ge(S.hotT_made, nxt + 1)
                            spread_q(nxt, u // 2 - 2, ahead[u // 2 - 2])
                        wait(pe, S.added, U * c + u - 2)
                        wait(pe, S.hot_made, 4 * c + u // 4 + 1)
                        pe.wait_ge(S.pv_made, U * c + u + 1)
                        pe.matmul(pa[u % 3][:, 0:H * VW], hot[:, u % 8, :], pv[:, u % 4, :, :].rearrange("p h c -> p (h c)"),
                                  start=True, stop=True).then_inc(S.summed, 1)
                pe.wait_ge(S.at_const, 7)
                first = windows_of(0, slice(0, AHEAD), PE_ONLY)
                pe.wait_ge(S.hotT_made, 1)
                for u in range(AHEAD):
                    spread_q(0, u, first[u])
                rounds(pe, body)


def attention_out(nc, m, io):
    with ExitStack() as ctx:
        def sb(n, s, d=F32):
            return ctx.enter_context(nc.sbuf_tensor(n, s, d))
        rden = sb("rden", [TT, NT, H])
        an = sb("an", [TT, 2, D])
        hr = sb("hr", [TT, 2, D])
        anT = sb("anT", [128, 2, 2, TT])
        stats = sb("stats2", [TT, NT, 6])
        mean = sb("mean2", [TT, NT])
        tmp = sb("tmp2", [TT, NT])
        var = sb("var2", [TT, NT])
        gw = sb("gw", [128, 2, EX])
        gb = sb("gb", [TT, EX])
        pt = [ctx.enter_context(nc.psum_tensor(f"opt{i}", [128, 512], F32)) for i in range(2)]
        po = [ctx.enter_context(nc.psum_tensor(f"opo{i}", [TT, 512], F32)) for i in range(2)]
        pl = ctx.enter_context(nc.psum_tensor("opl", [TT, NT, EX], F32))
        S = m.sem

        def pairs(eng, body):
            for t in range(3):
                body(t, t % 2, True)
            with eng.Fori(2, 12) as k:
                body(2 * k - 1, 1, True)
                body(2 * k, 0, True)
            body(23, 1, False)
            body(24, 0, False)

        with nc.Block() as block:
            @block.sync
            def _(sp):
                sp.dma_start(gw[:, :, :], io.gate_w.rearrange("(c p) e -> p c e", p=128)).then_inc(S.gate_in, 16)
                sp.dma_start(gb[:, :], io.gate_b.partition_broadcast(TT)).then_inc(S.gate_in, 16)

            @block.vector
            def _(dve):
                st = m.dve_steps.on(dve)
                st.link(dve.tensor_scalar(rden[:, :, :], m.agg[:, :, :, HD], 0.5, None, ALU.max))
                st.link(dve.reciprocal(rden[:, :, :], rden[:, :, :]))

                def norm(t, par):
                    wait(dve, S.an_turned, t - 1)
                    dve.tensor_tensor(an[:, par, :].rearrange("p (h d) -> p h d", h=H),
                                      at(m.agg, t)[:, :, 0:HD],
                                      spread(at(rden, t), 2, HD), ALU.mult).then_inc(S.an_made, 1)

                def body(t, par, ahead):
                    if ahead:
                        norm(t + 2, par)
                    dve.wait_ge(S.out_prod, t + 1)
                    dve.tensor_tensor(at(m.base, t), at(m.base, t), po[par][:, 0:D], ALU.add).then_inc(S.x2_made, 1)
                    if isinstance(t, int) and t == 0:
                        return
                    dve.wait_ge(S.x2_made, t)
                    dve.bn_stats(at(stats, t - 1), at(m.base, t - 1)).then_inc(S.x2_stats, 1)
                norm(0, 0)
                norm(1, 1)
                pairs(dve, body)
                dve.wait_ge(S.x2_made, NT)
                dve.bn_stats(stats[:, NT - 1], m.base[:, NT - 1]).then_inc(S.x2_stats, 1)
                dve.wait_ge(S.x2_stats, NT)
                mean_and_var(dve, st, stats[:, :, :], mean[:, :], var[:, :], tmp[:, :]).then_inc(S.var2_made, 1)
                dve.wait_ge(S.std2_made, 1)
                st.link(dve.reciprocal(var[:, :], var[:, :]))
                with dve.Fori(0, NT) as t:
                    dve.tensor_scalar(at(m.h, t), at(m.base, t), at(mean.rearrange("p (t o) -> p t o", o=1), t), at(var.rearrange("p (t o) -> p t o", o=1), t),
                                      ALU.subtract, ALU.mult).then_inc(S.h_made, 1)
                dve.wait_ge(S.gate_in, 32)
                dve.wait_ge(S.logit_prod, NT)
                dve.tensor_tensor(m.logit[:, :, :], pl[:, :, :], spread(gb[:, :], 1, NT), ALU.add)

            @block.scalar
            def _(act):
                def turned(t, par, first, used):
                    act.wait_ge(S.an_turned, first + t + 1)
                    wait(act, used, t - 1)
                    act.activation(anT[:, par, :, :], pt[par][:, 0:2 * TT].rearrange("p (c n) -> p c n", c=2), ACT.Copy).then_inc(S.anT_made, 1)

                def stage(t, par):
                    act.wait_ge(S.h_made, t + 1)
                    wait(act, S.an_turned, NT + t - 1 if not isinstance(t, int) or t > 1 else 0)
                    act.activation(hr[:, par, :], at(m.h, t), ACT.Copy).then_inc(S.hr_made, 1)

                def rows(t, par, ahead):
                    turned(t, par, NT, S.logit_prod)
                    if ahead:
                        stage(t + 2, par)
                pairs(act, lambda t, par, ahead: turned(t, par, 0, S.out_prod))
                act.wait_ge(S.var2_made, 1)
                act.activation(var[:, :], var[:, :], ACT.Sqrt).then_inc(S.std2_made, 1)
                stage(0, 0)
                stage(1, 1)
                pairs(act, rows)

            @block.tensor
            def _(pe):
                def turn(t, par, src, ready, first):
                    pe.wait_ge(ready, t + 1)
                    wait(pe, S.anT_made, first + t - 1)
                    for c in range(2):
                        mm = pe.transpose(pt[par][:, c * TT:(c + 1) * TT], src[:, c * 128:(c + 1) * 128], m.ident[0:TT, 0:TT])
                    mm.then_inc(S.an_turned, 1)

                def body(t, par, ahead):
                    pe.wait_ge(S.anT_made, t + 1)
                    wait(pe, S.x2_made, t - 1)
                    for c in range(2):
                        mm = pe.matmul(po[par][:, 0:D], anT[:, par, c, :], m.woT[:, c, :], start=(c == 0), stop=(c == 1))
                    mm.then_inc(S.out_prod, 1)
                    if ahead:
                        turn(t + 2, par, an[:, par, :], S.an_made, 0)
                turn(0, 0, an[:, 0, :], S.an_made, 0)
                turn(1, 1, an[:, 1, :], S.an_made, 0)
                pairs(pe, body)

                def gate(t, par, ahead):
                    pe.wait_ge(S.anT_made, NT + t + 1)
                    for c in range(2):
                        mm = pe.matmul(at(pl, t), anT[:, par, c, :], gw[:, c, :], start=(c == 0), stop=(c == 1))
                    mm.then_inc(S.logit_prod, 1)
                    if ahead:
                        turn(t + 2, par, hr[:, par, :], S.hr_made, NT)
                turn(0, 0, hr[:, 0, :], S.hr_made, NT)
                turn(1, 1, hr[:, 1, :], S.hr_made, NT)
                pe.wait_ge(S.gate_in, 32)
                pairs(pe, gate)


def route(nc, m):
    with ExitStack() as ctx:
        def sb(n, s, d=F32):
            return ctx.enter_context(nc.sbuf_tensor(n, s, d))
        pr = sb("probs", [TT, NT, EX])
        e1 = sb("rt_e1", [TT, NT])
        e2 = sb("rt_e2", [TT, NT])
        pos = sb("rt_pos", [TT, NT])
        eid = sb("rt_eid", [TT, NT])
        slot = sb("rt_slot", [TT, NT])
        kept = sb("rt_kept", [TT, NT])
        node = sb("rt_node", [TT, NT])
        iota_e = sb("iota_e", [TT, EX])
        hot = sb("rt_hot", [TT, NT, EX])
        tmp = sb("rt_tmp", [TT, NT, EX])
        tri = sb("rt_tri", [TT, TT])
        ones = sb("rt_ones", [TT, TT])
        tot = sb("rt_tot", [TT, EX, NT])
        run = sb("rt_run", [TT, EX, NT])
        keep = sb("rt_keep", [TT, EX, NT])
        put = sb("rt_put", [TT, NT], I32)
        pi = ctx.enter_context(nc.psum_tensor("rt_pi", [TT, 512], F32))
        pj = ctx.enter_context(nc.psum_tensor("rt_pj", [TT, 512], F32))
        S = m.sem
        L = m.logit
        with nc.Block() as block:
            @block.gpsimd
            def _(pool):
                pool.memset(ones[:], 1.0).then_inc(S.rt_const, 1)
                pool.memset(tri[:], 1.0).then_inc(S.rt_c0, 1)
                pool.memset(keep[:], 1.0).then_inc(S.rt_c0, 1)
                pool.wait_ge(S.rt_c0, 2)
                pool.affine_select(out=tri[:, :], in_=tri[:, :], compare_op=ALU.is_ge, fill=0.0, base=0,
                                   pattern=[[1, TT]], channel_multiplier=-1).then_inc(S.rt_const, 1)
                pool.memset(keep[:, :, 0:1], 0.0).then_inc(S.rt_const, 1)
                pool.iota(iota_e[:, :], pattern=[[1, EX]], base=0, channel_multiplier=0, allow_small_or_imprecise_dtypes=True).then_inc(S.rt_const, 1)
                pool.iota(node[:, :], pattern=[[TT, NT]], base=EX * CAP, channel_multiplier=1, allow_small_or_imprecise_dtypes=True).then_inc(S.rt_const, 1)
                pool.wait_ge(S.slots_known, 1)
                for t in range(NT):
                    pool.indirect_dma_start(m.slots, bass.IndirectOffsetOnAxis(ap=put[:, t:t + 1].bitcast(U32), axis=0),
                                            m.h[:, t, :], None).then_inc(S.rows_put, 16)
                pool.wait_ge(S.rows_put, 16 * NT)

            @block.vector
            def _(dve):
                st = m.dve_steps.on(dve)
                st.link(dve.tensor_reduce(e1[:, :], L[:, :, :], X, ALU.max))
                st.link(dve.tensor_tensor(pr[:, :, :], L[:, :, :], spread(e1[:, :], 2, EX), ALU.subtract))
                dve.sem_inc(S.l_shifted, 1)
                dve.wait_ge(S.l_exp, 1)
                st.link(dve.tensor_reduce(e1[:, :], pr[:, :, :], X, ALU.add))
                st.link(dve.reciprocal(e1[:, :], e1[:, :]))
                st.link(dve.tensor_tensor(pr[:, :, :], pr[:, :, :], spread(e1[:, :], 2, EX), ALU.mult))
                st.link(dve.tensor_reduce(m.prb[:, :], pr[:, :, :], X, ALU.max))
                dve.wait_ge(S.rt_const, 5)
                st.link(dve.tensor_tensor(tmp[:, :, :], pr[:, :, :], spread(m.prb[:, :], 2, EX), ALU.is_equal))
                st.link(dve.tensor_scalar(tmp[:, :, :], tmp[:, :, :], -float(EX), float(EX), ALU.mult, ALU.add))
                st.link(dve.tensor_tensor(tmp[:, :, :], tmp[:, :, :], spread(iota_e[:, :], 1, NT), ALU.add))
                st.link(dve.tensor_reduce(eid[:, :], tmp[:, :, :], X, ALU.min))
                st.link(dve.tensor_tensor(hot[:, :, :], spread(iota_e[:, :], 1, NT), spread(eid[:, :], 2, EX), ALU.is_equal))
                dve.sem_inc(S.hot_ready, 1)
                dve.wait_ge(S.counted, 1)
                st.link(dve.tensor_copy(tot[:, :, :], pj[:, 0:NT * EX].rearrange("p (t e) -> p e t", e=EX)))
                st.link(dve.tensor_tensor_scan(run.rearrange("p e t -> p (e t)"), keep.rearrange("p e t -> p (e t)"),
                                               tot.rearrange("p e t -> p (e t)"), 0.0, ALU.mult, ALU.add))
                st.link(dve.tensor_tensor(run[:, :, :], run[:, :, :], tot[:, :, :], ALU.subtract))
                st.link(dve.tensor_tensor(tmp[:, :, :], run.rearrange("p e t -> p t e"), pi[:, 0:NT * EX].rearrange("p (t e) -> p t e", e=EX), ALU.add))
                st.link(dve.tensor_tensor(tmp[:, :, :], tmp[:, :, :], hot[:, :, :], ALU.mult))
                st.link(dve.tensor_reduce(pos[:, :], tmp[:, :, :], X, ALU.add))
                st.then(dve.tensor_scalar(kept[:, :], pos[:, :], float(CAP), None, ALU.is_le))
                st.link(dve.tensor_scalar(pos[:, :], pos[:, :], float(CAP), -1.0, ALU.min, ALU.add))
                st.link(dve.scalar_tensor_tensor(out=slot[:, :], in0=eid[:, :], scalar=float(CAP), in1=pos[:, :], op0=ALU.mult, op1=ALU.add))
                st.then(dve.tensor_copy(m.slot_i[:, :], slot[:, :]))
                st.then(dve.tensor_tensor(m.prb[:, :], m.prb[:, :], kept[:, :], ALU.mult))
                st.link(dve.tensor_tensor(e2[:, :], slot[:, :], node[:, :], ALU.subtract))
                st.link(dve.tensor_tensor(e2[:, :], e2[:, :], kept[:, :], ALU.mult))
                st.link(dve.tensor_tensor(e2[:, :], e2[:, :], node[:, :], ALU.add))
                st.link(dve.tensor_copy(put[:, :], e2[:, :]))
                dve.sem_inc(S.slots_known, 1)

            @block.scalar
            def _(act):
                act.wait_ge(S.l_shifted, 1)
                act.activation(pr[:, :, :], pr[:, :, :], ACT.Exp).then_inc(S.l_exp, 1)

            @block.tensor
            def _(pe):
                pe.wait_ge(S.rt_const, 5)
                pe.wait_ge(S.hot_ready, 1)
                pe.matmul(pi[:, 0:NT * EX], tri[:, :], flat(hot[:, :, :]), start=True, stop=True)
                pe.matmul(pj[:, 0:NT * EX], ones[:, :], flat(hot[:, :, :]), start=True, stop=True).then_inc(S.counted, 1)


def experts(nc, m, io):
    MT = -(-CAP // 128)
    sizes = [min(128, CAP - 128 * i) for i in range(MT)]
    FC = FF // 128
    with ExitStack() as ctx:
        def sb(n, s, d=F32):
            return ctx.enter_context(nc.sbuf_tensor(n, s, d))
        w1 = [sb(f"w1_{i}", [128, 2, FF]) for i in range(2)]
        w2 = [sb(f"w2_{i}", [128, FC, D]) for i in range(2)]
        b1n = sb("b1n", [EX * FC, 128])
        b1 = sb("b1", [128, EX, FC])
        b2 = [sb(f"b2_{i}", [128, D]) for i in range(2)]
        hb = [sb(f"hb_{i}", [128, MT, D]) for i in range(2)]
        hT = sb("hT", [128, 2, 512])
        hm = sb("hm", [128, FC, 512])
        yb = sb("yb", [128, MT, D])
        pt = [ctx.enter_context(nc.psum_tensor(f"xpt{i}", [128, 512], F32)) for i in range(2)]
        p1 = [ctx.enter_context(nc.psum_tensor(f"xp1{i}", [128, 512], F32)) for i in range(3)]
        p2 = [ctx.enter_context(nc.psum_tensor(f"xp2{i}", [128, 512], F32)) for i in range(3)]
        S = m.sem
        w1d = io.w1.rearrange("e (c p) f -> e p c f", p=128)
        w2d = io.w2.rearrange("e (c p) d -> e p c d", p=128)

        def rounds(eng, body):
            for par in range(2):
                body(par, par, 0)
            with eng.Fori(1, EX // 2) as k:
                for par in range(2):
                    body(2 * k + par, par, k)

        with nc.Block() as block:
            @block.sync
            def _(sp):
                def body(e, par, k):
                    wait(sp, S.y_stored, 64 * (e - 1) if not isinstance(e, int) else 0)
                    one = bass.ds(e, 1)
                    sp.dma_start(w1[par][:, :, :], w1d[one].squeeze(0)).then_inc(S.ex_in[par], 16)
                    sp.dma_start(hb[par][:, 0:MT - 1, :], m.slots[bass.ds(e * CAP, 128 * (MT - 1)), :].rearrange("(c p) d -> p c d", p=128)).then_inc(S.ex_in[par], 16)
                    sp.dma_start(hb[par][0:sizes[-1], MT - 1, :], m.slots[bass.ds(e * CAP + 128 * (MT - 1), sizes[-1]), :]).then_inc(S.ex_in[par], 16)
                    sp.dma_start(w2[par][:, :, :], w2d[one].squeeze(0)).then_inc(S.ex_in[par], 16)
                    sp.dma_start(b2[par][:, :], io.b2[one, :].to_broadcast([128, D])).then_inc(S.ex_in[par], 16)
                sp.dma_start(b1n[:, :], io.b1.rearrange("e (c p) -> (e c) p", p=128)).then_inc(S.b1_in, 16)
                rounds(sp, body)

            @block.scalar
            def _(act):
                act.wait_ge(S.b1_turned, 1)
                act.activation(b1.rearrange("p e c -> p (e c)"), p1[2][:, 0:EX * FC], ACT.Copy).then_inc(S.b1_made, 1)
                act.wait_ge(S.b1_made, 1)

                def body(e, par, k):
                    for c in range(2):
                        act.wait_ge(S.hb_turned, 2 * e + c + 1)
                        if c == 0:
                            wait(act, S.up_prod, FC * e)
                        act.activation(hT[:, c, 0:CAP], pt[c][:, 0:CAP], ACT.Copy).then_inc(S.hT_made, 1)
                    for f in range(FC):
                        act.wait_ge(S.up_prod, FC * e + f + 1)
                        if f == 0:
                            wait(act, S.down_prod, MT * e)
                        act.activation(hm[:, f, 0:CAP], p1[f % 2][:, 0:CAP], ACT.Relu, bias=at(b1, e)[:, f:f + 1]).then_inc(S.hm_made, 1)
                    for i in range(MT):
                        act.wait_ge(S.y_ready, MT * e + i + 1)
                        act.dma_start(m.y_d[bass.ds(e * CAP + 128 * i, sizes[i]), :], yb[0:sizes[i], i, :]).then_inc(S.y_stored, 16)
                rounds(act, body)
                act.wait_ge(S.y_stored, 16 * MT * EX)

            @block.vector
            def _(dve):
                def body(e, par, k):
                    wait(dve, S.y_stored, 16 * MT * e)
                    for i in range(MT):
                        dve.wait_ge(S.down_prod, MT * e + i + 1)
                        dve.tensor_tensor(yb[0:sizes[i], i, :], p2[i % 2][0:sizes[i], 0:D], b2[par][0:sizes[i], :], ALU.add).then_inc(S.y_ready, 1)
                rounds(dve, body)

            @block.tensor
            def _(pe):
                pe.wait_ge(S.b1_in, 16)
                pe.transpose(p1[2][:, 0:EX * FC], b1n[:, :], m.ident[0:EX * FC, 0:EX * FC]).then_inc(S.b1_turned, 1)

                def body(e, par, k):
                    pe.wait_ge(S.ex_in[par], 80 * k + 80)
                    for c in range(2):
                        wait(pe, S.hT_made, 2 * e + c - 1)
                        for i in range(MT):
                            mm = pe.transpose(pt[c][:, 128 * i:128 * i + sizes[i]], hb[par][0:sizes[i], i, c * 128:(c + 1) * 128],
                                              m.ident[0:sizes[i], 0:sizes[i]])
                        mm.then_inc(S.hb_turned, 1)
                    pe.wait_ge(S.hT_made, 2 * e + 2)
                    for f in range(FC):
                        wait(pe, S.hm_made, FC * e + f - 1)
                        for c in range(2):
                            mm = pe.matmul(p1[f % 2][:, 0:CAP], w1[par][:, c, f * 128:(f + 1) * 128], hT[:, c, 0:CAP], start=(c == 0), stop=(c == 1))
                        mm.then_inc(S.up_prod, 1)
                    pe.wait_ge(S.hm_made, FC * e + FC)
                    for i in range(MT):
                        wait(pe, S.y_ready, MT * e + i - 1)
                        for f in range(FC):
                            mm = pe.matmul(p2[i % 2][0:sizes[i], 0:D], hm[:, f, 128 * i:128 * i + sizes[i]], w2[par][:, f, :],
                                           start=(f == 0), stop=(f == FC - 1))
                        mm.then_inc(S.down_prod, 1)
                rounds(pe, body)


def combine(nc, m, out):
    B = 4
    with ExitStack() as ctx:
        def sb(n, s, d=F32):
            return ctx.enter_context(nc.sbuf_tensor(n, s, d))
        y = sb("cb_y", [TT, NT, D])
        lo = sb("cb_lo", [TT, 2, D])
        hi = sb("cb_hi", [TT, 2, D])
        fin = sb("cb_fin", [TT, 2, D], I32)
        S = m.sem
        prb = m.prb.rearrange("p (t o) -> p t o", o=1)
        with nc.Block() as block:
            @block.gpsimd
            def _(pool):
                for t in range(NT):
                    wait(pool, S.out_made, t - U + 1)
                    pool.indirect_dma_start(y[:, t, :], None, m.y_d,
                                            bass.IndirectOffsetOnAxis(ap=m.slot_i[:, t:t + 1].bitcast(U32), axis=0)).then_inc(S.arrived[t % U], 16)

            @block.vector
            def _(dve):
                st = m.dve_steps.on(dve)
                for t in range(NT):
                    dve.wait_ge(S.arrived[t % U], 16 * (CH + 1 + t // U))
                    st.link(dve.tensor_scalar(y[:, t, :], y[:, t, :], m.prb[:, t:t + 1], None, ALU.mult))
                    p = t % 2
                    st.then(dve.tensor_scalar(fin[:, p, :], y[:, t, :], 0.0, 0.0, ALU.mult, ALU.is_equal))
                    st.then(dve.tensor_scalar(lo[:, p, :], y[:, t, :], 0.0, -1.0e4, ALU.min, ALU.max))
                    st.link(dve.tensor_scalar(hi[:, p, :], y[:, t, :], 0.0, 1.0e4, ALU.max, ALU.min))
                    st.link(dve.tensor_tensor(lo[:, p, :], lo[:, p, :], hi[:, p, :], ALU.add))
                    st.link(dve.copy_predicated(lo[:, p, :], fin[:, p, :], y[:, t, :]))
                    dve.tensor_tensor(m.base[:, t, :], m.base[:, t, :], lo[:, p, :], ALU.add).then_inc(S.out_made, 1)

            @block.sync
            def _(sp):
                ot = out.rearrange("(t p) d -> p t d", p=TT)
                for t in range(NT):
                    sp.wait_ge(S.out_made, t + 1)
                    sp.dma_start(ot[:, t, :], m.base[:, t, :]).then_inc(S.out_stored, 16)
                sp.wait_ge(S.out_stored, 16 * NT)


SEMS = """dve_step xr_made qr_made hr_made edges_in tbl_const last_in keys_out keys_made tbl_iota ident_zero ident_made
rows_known before_made rows_counted tbl_turned w_in b_in bo_in zero_made zero_out qkv_out mixv_one squared base_x
var_made std_made xn_made w_ready ss_made norm_made rms_made projected w_turned w_evac xn_turned xnT_made mix_out
mem_in la_const y_scaled kmax1 q_shifted kmax_turned kmax2 kmax_row kmax3 kmax_wide k_shifted mem_turned mem_ready
q_exp q_soft ctx_made cd_made cd_turned cdT_made wc_prod wc_made y_prod y_made y_squared yss_made ynorm_made mk_exp
k_exp q_turned qT_made gate_in an_turned an_made out_prod x2_made x2_stats var2_made std2_made h_made logit_prod
logit_made anT_made rt_const rt_c0 slots_known rows_put l_shifted l_exp b1_in b1_turned b1_made hot_ready counted
y_stored hb_turned up_prod hT_made down_prod hm_made y_ready out_made out_stored first_in key_in q_whole q_rest
q_split borders_made costs_made loc_in hotT_made q_spread prod_made reduced sc_made sc_turned chain chain_pe p_exp f_exp
pv_made hot_abs hot_made summed added idx_ready at_const rescaled""".split()


class Signals:

    def __init__(self, names, new):
        (self.dve_step, self.xr_made, self.qr_made, self.hr_made, self.edges_in, self.tbl_const, self.last_in,
         self.keys_out, self.keys_made, self.tbl_iota, self.ident_zero, self.ident_made, self.rows_known,
         self.before_made, self.rows_counted, self.tbl_turned, self.w_in, self.b_in, self.bo_in, self.zero_made,
         self.zero_out, self.qkv_out, self.mixv_one, self.squared, self.base_x, self.var_made, self.std_made,
         self.xn_made, self.w_ready, self.ss_made, self.norm_made, self.rms_made, self.projected, self.w_turned,
         self.w_evac, self.xn_turned, self.xnT_made, self.mix_out, self.mem_in, self.la_const, self.y_scaled,
         self.kmax1, self.q_shifted, self.kmax_turned, self.kmax2, self.kmax_row, self.kmax3, self.kmax_wide,
         self.k_shifted, self.mem_turned, self.mem_ready, self.q_exp, self.q_soft, self.ctx_made, self.cd_made,
         self.cd_turned, self.cdT_made, self.wc_prod, self.wc_made, self.y_prod, self.y_made, self.y_squared,
         self.yss_made, self.ynorm_made, self.mk_exp, self.k_exp, self.q_turned, self.qT_made, self.gate_in,
         self.an_turned, self.an_made, self.out_prod, self.x2_made, self.x2_stats, self.var2_made, self.std2_made,
         self.h_made, self.logit_prod, self.logit_made, self.anT_made, self.rt_const, self.rt_c0, self.slots_known,
         self.rows_put, self.l_shifted, self.l_exp, self.b1_in, self.b1_turned, self.b1_made, self.hot_ready,
         self.counted, self.y_stored, self.hb_turned, self.up_prod, self.hT_made, self.down_prod, self.hm_made,
         self.y_ready, self.out_made, self.out_stored, self.first_in, self.key_in, self.q_whole, self.q_rest,
         self.q_split, self.borders_made, self.costs_made, self.loc_in, self.hotT_made, self.q_spread, self.prod_made, self.reduced,
         self.sc_made, self.sc_turned, self.chain, self.chain_pe, self.p_exp, self.f_exp, self.pv_made,
         self.hot_abs, self.hot_made, self.summed, self.added, self.idx_ready, self.at_const, self.rescaled) = (new(n) for n in names)


class Inputs:
    def __init__(self, x, src, dst, Wq, bq, Wk, bk, Wv, bv, Wo, bo, w_qkv, mem_kv, w_out, b_out, g_out, g_pre, gate_w,
                 gate_b, w1, b1, w2, b2):
        self.x = x
        self.src = src
        self.dst = dst
        self.Wq = Wq
        self.bq = bq
        self.Wk = Wk
        self.bk = bk
        self.Wv = Wv
        self.bv = bv
        self.Wo = Wo
        self.bo = bo
        self.w_qkv = w_qkv
        self.mem_kv = mem_kv
        self.w_out = w_out
        self.b_out = b_out
        self.g_out = g_out
        self.g_pre = g_pre
        self.gate_w = gate_w
        self.gate_b = gate_b
        self.w1 = w1
        self.b1 = b1
        self.w2 = w2
        self.b2 = b2


class Mem:
    pass


def graph_layer(nc, io, out, debug=False):
    m = Mem()
    scratch = "ExternalOutput" if debug else "Internal"

    def dram(n, s, d=F32):
        return nc.dram_tensor(n, s, d, kind=scratch).ap()
    m.edges = dram("edges_d", (EROWS, 256), I32)
    m.key = dram("key_d", (STEPS * 128 + 2,))
    m.loc = dram("loc_d", (STEPS, 128), BF16)
    m.kv_d = dram("kv_d", (N, KV))
    m.slots = dram("slots_d", (EX * CAP + N, D))
    m.y_d = dram("y_d", (EX * CAP, D))
    with ExitStack() as ctx:
        def sb(n, s, d=F32):
            return ctx.enter_context(nc.sbuf_tensor(n, s, d))
        def new(n):
            return ctx.enter_context(nc.semaphore(n))

        def several(n, count):
            return [new(f"{n}{i}") for i in range(count)]
        S = m.sem = Signals(SEMS, new)
        S.rows_in, S.x_in, S.kv_stored = several("rows_in", TG), several("x_in", 5), several("kv_stored", 2)
        S.arrived, S.ex_in = several("arrived", U), several("ex_in", 2)
        m.dve_steps = Steps(S.dve_step)
        m.base = sb("base", [TT, NT, D])
        m.ident = sb("ident", [128, 128])
        m.iota_w = sb("iota_w", [128, TT])
        m.iota_p = sb("iota_p", [128, 1])
        m.one_col = sb("one_col", [128, 1])
        m.pen_e = sb("pen_e", [128, CH, U])
        m.src_e = sb("src_e", [128, CH + 1, U], I32)
        m.win_of = sb("win_of", [1, CH, U], I32)
        m.idx = sb("idx", [128, 2, U], I32)
        m.nloc_e = sb("nloc_e", [128, CH, U])
        m.first_loc = sb("first_loc", [2, CH])
        m.edge_any = sb("edge_any", [128, CH, 2])
        m.woT = sb("woT", [128, 2, D])
        m.logit = sb("logit", [TT, NT, EX])
        m.prb = sb("prb", [TT, NT])
        m.slot_i = sb("slot_i", [TT, NT], I32)
        with ExitStack() as att:
            m.q3 = att.enter_context(nc.sbuf_tensor("q3", [TT, NT, 3, D], BF16))
            m.fwd = att.enter_context(nc.sbuf_tensor("fwd", [128, CH, 128], BF16))
            m.bwd = att.enter_context(nc.sbuf_tensor("bwd", [128, CH, 128], BF16))
            with ExitStack() as mix:
                def keep(n, c):
                    return mix.enter_context(nc.sbuf_tensor(n, [TT, NT, c], F32))
                m.mixq, m.mixk, m.mixv, m.xn = keep("mixq", HID), keep("mixk", HID), keep("mixv", HID + 1), keep("xn", D)
                with ExitStack() as prep:
                    def ready(n, s):
                        return prep.enter_context(nc.sbuf_tensor(n, s, F32))
                    m.wall, m.gpre = ready("wall", [128, 2, WALL]), ready("gpre", [128, 2])
                    m.bqkv, m.bo = ready("bqkv", [TT, 3 * D]), ready("bo", [TT, D])
                    m.stats, m.rstd = ready("stats", [TT, NT, 6]), ready("rstd", [TT, NT])
                    m.mean, m.var, m.ss, m.rms = (ready(n, [TT, NT]) for n in ("mean", "var", "ss", "rms"))
                    edge_tables(nc, m, io)
                    project(nc, m, io)
                linear_attention(nc, m, io)
            m.agg = att.enter_context(nc.sbuf_tensor("agg", [TT, NT, H, VW], F32))
            attention(nc, m)
            m.h = m.q3.rearrange("p t a d -> p (t a d)")[:, 0:NT * 2 * D].bitcast(F32).rearrange("p (t d) -> p t d", t=NT)
            attention_out(nc, m, io)
            route(nc, m)
        experts(nc, m, io)
        combine(nc, m, out)


DEBUG = False
ARGS = {"x": "x", "src": "src", "dst": "dst", "Wq": "L0_gnn_Wq", "bq": "L0_gnn_bq", "Wk": "L0_gnn_Wk", "bk":
        "L0_gnn_bk", "Wv": "L0_gnn_Wv", "bv": "L0_gnn_bv", "Wo": "L0_gnn_Wo", "bo": "L0_gnn_bo", "w_qkv":
        "L0_mix_w_qkv", "mem_kv": "L0_mix_mem_kv", "w_out": "L0_mix_w_out", "b_out": "L0_mix_b_out", "g_out":
        "L0_mix_g_out", "g_pre": "L0_mix_g_pre", "gate_w": "L0_ffn_gate_w", "gate_b": "L0_ffn_gate_b", "w1":
        "L0_ffn_w1", "b1": "L0_ffn_b1", "w2": "L0_ffn_w2", "b2": "L0_ffn_b2"}
def kernel(**inputs):
    import concourse.bacc as _bacc
    from concourse.bass_utils import run_bass_kernel_spmd as _run

    nc = _bacc.Bacc("TRN2", target_bir_lowering=False, num_devices=1)
    arrays, params = {}, {}
    for short, name in ARGS.items():
        a = np.ascontiguousarray(inputs[name])
        arrays["in_" + short] = a
        params[short] = nc.dram_tensor("in_" + short, a.shape, mybir.dt.from_np(a.dtype), kind="ExternalInput").ap()
    out = nc.dram_tensor("out", (N, D), F32, kind="ExternalOutput").ap()
    graph_layer(nc, Inputs(**params), out, DEBUG)
    r = _run(nc, [arrays], core_ids=[0])
    return r.results[0]["out"]
```

```python
import numpy as np
import concourse.bass as bass
from concourse import mybir
from contextlib import ExitStack

F32 = mybir.dt.float32
I32 = mybir.dt.int32
U32 = mybir.dt.uint32
BF16 = mybir.dt.bfloat16
ALU = mybir.AluOpType
ACT = mybir.ActivationFunctionType
X = mybir.AxisListType.X
PE_ONLY = [mybir.EngineType.PE]
DVE_ONLY = [mybir.EngineType.DVE]

N, D, E = 3125, 256, 50000
TT, NT = 125, 25
H, HD = 8, 32
MH, MD, MEM, HID = 4, 32, 4, 128
QKV = 3 * HID
WALL = 3 * D + QKV
EX, FF = 8, 1024
CAP = -(-5 * N // (4 * EX))
U = 16
AHEAD = 4
EROWS = -(-(E // 128 + 1) // 8) * 8
STEPS = 416
CH = STEPS // U
TG, TP = 4, STEPS // 4
LATE = 3
LG = 5
RG, RP = 4, EROWS // 4
VW = HD + 1
KV = D + H * VW
PAD_NODE = 4000.0
BIG = 1.0e30
RESET = 1.0e38
EPS = 1e-5
assert CH == NT + 1 and EROWS * 128 >= E and EROWS - 1 + NT <= STEPS and CAP == 489


def spread(ap, axis, n):
    a = ap.unsqueeze(axis)
    shape = list(a.shape)
    shape[axis] = n
    return a.to_broadcast(shape)


def flat(ap):
    return ap.rearrange("p a b -> p (a b)")


def at(t, i):
    if isinstance(i, int):
        return t[:, i]
    a = t[:, bass.ds(i, 1)]
    return a.squeeze(1)


def wait(eng, sem, value):
    if isinstance(value, int) and value <= 0:
        return
    eng.wait_ge(sem, value)


class Steps:

    def __init__(self, sem):
        self.eng, self.sem, self.c = None, sem, 0

    def on(self, eng):
        self.eng = eng
        return self

    def then(self, ins):
        ins.then_inc(self.sem, 1)
        self.c += 1

    def settle(self):
        self.eng.wait_ge(self.sem, self.c)

    def link(self, ins):
        self.then(ins)
        self.settle()


def mean_and_var(dve, st, stats, mean, var, tmp):
    st.then(dve.tensor_tensor(mean, stats[:, :, 1], stats[:, :, 4], ALU.add))
    st.then(dve.tensor_tensor(tmp, stats[:, :, 1], stats[:, :, 4], ALU.subtract))
    st.link(dve.tensor_tensor(var, stats[:, :, 2], stats[:, :, 5], ALU.add))
    st.then(dve.tensor_scalar(mean, mean, 0.5, None, ALU.mult))
    st.then(dve.tensor_scalar(var, var, 1.0 / D, EPS, ALU.mult, ALU.add))
    st.link(dve.tensor_tensor(tmp, tmp, tmp, ALU.mult))
    return dve.scalar_tensor_tensor(out=var, in0=tmp, scalar=0.25, in1=var, op0=ALU.mult, op1=ALU.add)


def edge_tables(nc, m, io):
    with ExitStack() as ctx:
        def sb(n, s, d=F32):
            return ctx.enter_context(nc.sbuf_tensor(n, s, d))
        wnat, sq = m.wnat, m.sq
        padd = sb("padd", [1, EROWS * 128 - E], I32)
        pads = sb("pads", [1, EROWS * 128 - E], I32)
        last_i = sb("last_i", [RP, RG, 2 * 128], I32)
        last_f = sb("last_f", [RP, RG])
        thr = sb("thr", [RP, NT - 1])
        junk = sb("junk", [RP, NT - 1])
        wend = sb("wend", [RP, RG])
        wfound = sb("wfound", [RP, RG])
        pen2 = sb("pen2", [128, STEPS])
        loc_e = sb("loc_e", [128, STEPS])
        iota_i = sb("iota_i", [RP, STEPS])
        before = m.q3.rearrange("p t a d -> p (t a d)")[0:RP, 0:RG * STEPS].rearrange("p (g i) -> p g i", g=RG)
        ones = sb("ones_t", [RP, 2], BF16)
        step_no = sb("step_no", [TP, TG])
        row_no = sb("row_no", [TP, TG])
        row_i = sb("row_i", [TP, TG], I32)
        win0 = sb("win0", [TP, TG])
        got = sb("got", [TP, TG, 2 * 128], I32)
        dst_f = sb("dst_f", [TP, TG, 128])
        src_f, key = (m.early[0:TP, RG * STEPS + i * TG * 128:RG * STEPS + (i + 1) * TG * 128].rearrange("p (g e) -> p g e", g=TG)
                      for i in range(2))
        loc16 = sb("loc16", [TP, TG, 128], BF16)
        drow = sb("drow", [2, STEPS])
        first_key = sb("first_key", [2, CH])
        front = sb("front", [1, 1])
        back = sb("back", [1, 1])
        xt = io.x.rearrange("(t p) d -> p t d", p=TT)
        psl = ctx.enter_context(nc.psum_tensor("psl", [128, TG, 128], F32))
        pss = ctx.enter_context(nc.psum_tensor("pss", [128, TG, 128], F32))
        psr = ctx.enter_context(nc.psum_tensor("psr", [128, 512], F32))
        pst = ctx.enter_context(nc.psum_tensor("pst", [128, 512], F32))
        pt = [ctx.enter_context(nc.psum_tensor(f"wpt{i}", [128, 512], F32)) for i in range(2)]
        S = m.sem
        with nc.Block() as block:
            @block.sync
            def _(sp):
                def nodes(g):
                    sp.dma_start(m.base[:, g * LG:(g + 1) * LG, :], xt[:, g * LG:(g + 1) * LG, :]).then_inc(S.x_in[g], 16)
                nodes(0)
                full = E // 128
                e2 = m.edges.rearrange("r (c e) -> r c e", c=2)
                ef = E - full * 128
                for c, a in ((0, io.dst), (1, io.src)):
                    sp.dma_start(e2[0:full, c, :], a[0:full * 128].rearrange("(r e) -> r e", e=128)).then_inc(S.edges_in, 16)
                    sp.dma_start(e2[full:full + 1, c, 0:ef], a[full * 128:E].rearrange("(r e) -> r e", r=1)).then_inc(S.edges_in, 16)
                sp.wait_ge(S.tbl_const, 5)
                for c, p in ((0, padd), (1, pads)):
                    sp.dma_start(e2[full:full + 1, c, ef:128], p[:, 0:128 - ef]).then_inc(S.edges_in, 16)
                    rest = EROWS - full - 1
                    sp.dma_start(e2[full + 1:EROWS, c, :], p[:, 0:rest * 128].rearrange("o (r e) -> o r e", r=rest)).then_inc(S.edges_in, 16)
                sp.dma_start(m.key[0:1].rearrange("(a n) -> a n", a=1), front[:, :]).then_inc(S.keys_out, 16)
                sp.dma_start(m.key[1 + STEPS * 128:2 + STEPS * 128].rearrange("(a n) -> a n", a=1), back[:, :]).then_inc(S.keys_out, 16)
                sp.wait_ge(S.edges_in, 128)
                sp.dma_start(last_i[:, :, :], m.edges.rearrange("(g p) c -> p g c", p=RP)).then_inc(S.last_in, 16)
                for g in range(1, NT // LG):
                    nodes(g)
                for w, a in enumerate((io.Wq, io.Wk, io.Wv, io.Wo)):
                    sp.dma_start(wnat[:, w, :, :], a.rearrange("(c p) i -> p c i", p=128)).then_inc(S.w_in, 16)
                sp.dma_start(m.wall[:, :, 3 * D:WALL], io.w_qkv.rearrange("(c p) n -> p c n", p=128)).then_inc(S.w_in, 16)
                sp.dma_start(m.gpre[:, :], io.g_pre.rearrange("(c p) -> p c", p=128), allow_slow_non_contiguous=True).then_inc(S.w_in, 16)
                for i, b in enumerate((io.bq, io.bk, io.bv)):
                    sp.dma_start(m.bqkv[:, i * D:(i + 1) * D], b.partition_broadcast(TT)).then_inc(S.b_in, 16)
                sp.dma_start(m.bo[:, :], io.bo.partition_broadcast(TT)).then_inc(S.bo_in, 16)
                sp.wait_ge(S.keys_made, 1)
                for g in range(TG):
                    o = 1 + g * TP * 128
                    sp.dma_start(m.key[o:o + TP * 128].rearrange("(p e) -> p e", p=TP), key[:, g, :]).then_inc(S.keys_out, 16)
                sp.dma_start(m.loc.rearrange("(g p) e -> p g e", p=TP), loc16[:, :, :]).then_inc(S.keys_out, 16)
                sp.wait_ge(S.keys_out, 16 * (3 + TG))
                first = bass.AP(m.key.tensor, 1, [[0, 2], [U * 128, CH], [1, 1]])
                sp.dma_start(first_key[:, :].unsqueeze(2), first, allow_slow_non_contiguous=True).then_inc(S.first_in, 16)

            @block.gpsimd
            def _(pool):
                pool.memset(padd[:], int(PAD_NODE)).then_inc(S.tbl_const, 1)
                pool.memset(pads[:], 0).then_inc(S.tbl_const, 1)
                pool.memset(front[:], -1.0).then_inc(S.tbl_const, 1)
                pool.memset(back[:], 1.0e6).then_inc(S.tbl_const, 1)
                pool.memset(m.src_e[:, CH, :], 0).then_inc(S.tbl_const, 1)
                pool.iota(thr[:, :], pattern=[[TT, NT - 1]], base=TT, channel_multiplier=0, allow_small_or_imprecise_dtypes=True).then_inc(S.tbl_iota, 1)
                pool.iota(iota_i[:, :], pattern=[[1, STEPS]], base=0, channel_multiplier=0, allow_small_or_imprecise_dtypes=True).then_inc(S.tbl_iota, 1)
                pool.iota(wend[:, :], pattern=[[RP, RG]], base=0, channel_multiplier=1, allow_small_or_imprecise_dtypes=True).then_inc(S.tbl_iota, 1)
                pool.iota(step_no[:, :], pattern=[[TP, TG]], base=0, channel_multiplier=1, allow_small_or_imprecise_dtypes=True).then_inc(S.tbl_iota, 1)
                pool.memset(ones[:], 1.0).then_inc(S.tbl_iota, 1)
                pool.memset(m.one_col[:], 1.0)
                pool.memset(m.ident[:], 0.0).then_inc(S.ident_zero, 1)
                pool.wait_ge(S.ident_zero, 1)
                pool.affine_select(out=m.ident[:, :], in_=m.ident[:, :], compare_op=ALU.not_equal, fill=1.0, base=0,
                                   pattern=[[-1, 128]], channel_multiplier=1).then_inc(S.ident_made, 1)
                pool.iota(m.iota_w[:, :], pattern=[[1, TT]], base=0, channel_multiplier=0, allow_small_or_imprecise_dtypes=True).then_inc(S.ident_made, 1)
                pool.iota(m.iota_p[:, :], pattern=[[0, 1]], base=0, channel_multiplier=1, allow_small_or_imprecise_dtypes=True).then_inc(S.ident_made, 1)
                pool.wait_ge(S.rows_known, 1)
                pool.wait_ge(S.edges_in, 128)
                for g in range(TG):
                    pool.indirect_dma_start(got[:, g, :], None, m.edges,
                                            bass.IndirectOffsetOnAxis(ap=row_i[:, g:g + 1].bitcast(U32), axis=0)).then_inc(S.rows_in[g], 16)

            @block.vector
            def _(dve):
                st = m.dve_steps.on(dve)

                def normalise(g):
                    dve.wait_ge(S.x_in[g], 16)
                    r = slice(g * LG, (g + 1) * LG)
                    for t in range(g * LG, (g + 1) * LG):
                        st.then(dve.bn_stats(m.stats[:, t, :], m.base[:, t, :]))
                    st.settle()
                    mean_and_var(dve, st, m.stats[:, r, :], m.mean[:, r], m.var[:, r], m.rms[:, r]).then_inc(S.var_made, 1)
                    dve.wait_ge(S.std_made, g + 1)
                    st.link(dve.reciprocal(m.rstd[:, r], m.rstd[:, r]))
                    for t in range(g * LG, (g + 1) * LG):
                        dve.tensor_scalar(m.xn[:, t, :], m.base[:, t, :], m.mean[:, t:t + 1], m.rstd[:, t:t + 1], ALU.subtract,
                                          ALU.mult).then_inc(S.xn_made, 1)

                def root_mean_squares():
                    dve.wait_ge(S.squared, NT)
                    dve.tensor_scalar(m.ss[:, :], m.ss[:, :], 1e-24, None, ALU.max).then_inc(S.ss_made, 1)
                    dve.wait_ge(S.w_in, 96)
                    for c in range(2):
                        dve.tensor_scalar(m.wall[:, c, 3 * D:WALL], m.wall[:, c, 3 * D:WALL], m.gpre[:, c:c + 1], None,
                                          ALU.mult).then_inc(S.w_ready, 1)
                    dve.wait_ge(S.norm_made, 1)
                    st.link(dve.reciprocal(m.rms[:, :], m.rms[:, :]))
                    dve.tensor_scalar(m.rms[:, :], m.rms[:, :], float(D) ** 0.5, None, ALU.mult).then_inc(S.rms_made, 1)

                normalise(0)
                dve.wait_ge(S.last_in, 16)
                dve.wait_ge(S.tbl_iota, 5)
                st.link(dve.tensor_copy(last_f[:, :], last_i[:, :, 127]))
                for g in range(RG):
                    st.link(dve.tensor_scalar(junk[:, :], thr[:, :], last_f[:, g:g + 1], 0.0, ALU.is_le, ALU.add,
                                              accum_out=wfound[:, g:g + 1]))
                st.link(dve.tensor_tensor(wend[:, :], wend[:, :], wfound[:, :], ALU.add))
                for g in range(RG):
                    last = dve.tensor_scalar(before[:, g, :], iota_i[:, :], wend[:, g:g + 1], None, ALU.is_gt)
                    st.then(last)
                st.settle()
                dve.sem_inc(S.before_made, 1)
                normalise(1)
                dve.wait_ge(S.rows_counted, 1)
                st.link(dve.tensor_copy(row_no[:, :], psr[0:TP, 0:TG]))
                dve.tensor_copy(row_i[:, :], row_no[:, :]).then_inc(S.rows_known, 1)
                st.link(dve.tensor_tensor(win0[:, :], step_no[:, :], row_no[:, :], ALU.subtract))
                st.link(dve.tensor_scalar(win0[:, :], win0[:, :], float(TT), None, ALU.mult))
                st.link(dve.tensor_tensor(drow[:, :], iota_i[0:2, :], pst[0:2, 0:STEPS], ALU.subtract))
                st.link(dve.tensor_scalar(m.win_of.rearrange("p a b -> p (a b)"), drow[0:1, :], 0.0, float(NT - 1), ALU.max, ALU.min))
                normalise(2)
                for g in range(TG):
                    dve.wait_ge(S.rows_in[g], 16)
                    st.then(dve.tensor_copy(src_f[:, g, :], got[:, g, 128:256]))
                    st.link(dve.tensor_copy(dst_f[:, g, :], got[:, g, 0:128]))
                    st.link(dve.tensor_scalar(dst_f[:, g, :], dst_f[:, g, :], win0[:, g:g + 1], None, ALU.subtract))
                    st.then(dve.tensor_scalar(key[:, g, :], dst_f[:, g, :], 0.0, float(TT - 1), ALU.max, ALU.min))
                    st.link(dve.tensor_scalar(dst_f[:, g, :], dst_f[:, g, :], -1.0, float(TT), ALU.max, ALU.min))
                    st.then(dve.tensor_scalar(key[:, g, :], key[:, g, :], win0[:, g:g + 1], None, ALU.add))
                    st.then(dve.tensor_copy(loc16[:, g, :], dst_f[:, g, :]))
                st.settle()
                dve.sem_inc(S.keys_made, 1)
                dve.wait_ge(S.tbl_turned, 1)
                dve.wait_ge(S.tbl_const, 5)
                le = loc_e[:, :]
                pe_ = m.pen_e.rearrange("p a b -> p (a b)")
                for g in range(TG):
                    st.then(dve.tensor_copy(le[:, g * TP:(g + 1) * TP], psl[:, g, 0:TP]))
                    st.then(dve.tensor_copy(m.src_e.rearrange("p a b -> p (a b)")[:, g * TP:(g + 1) * TP], pss[:, g, 0:TP]))
                st.settle()
                st.then(dve.tensor_scalar(pe_, le, 0.0, -BIG, ALU.is_lt, ALU.mult))
                st.link(dve.tensor_scalar(pen2[:, :], le, float(TT) - 0.5, -BIG, ALU.is_gt, ALU.mult))
                st.link(dve.tensor_tensor(pe_, pe_, pen2[:, :], ALU.add))
                for g in range(3, NT // LG):
                    normalise(g)
                root_mean_squares()
                dve.wait_ge(S.first_in, 16)
                dve.scalar_tensor_tensor(out=m.first_loc[:, :], in0=drow.rearrange("p (k u) -> p k u", u=U)[:, :, 0],
                                         scalar=-float(TT), in1=first_key[:, :], op0=ALU.mult, op1=ALU.add)
                dve.tensor_scalar(m.nloc_e.rearrange("p a b -> p (a b)"), le, -1.0, None, ALU.mult)

            @block.scalar
            def _(act):
                for g in range(NT // LG):
                    if g == 3:
                        for w in range(4):
                            act.wait_ge(S.w_turned, w + 1)
                            src = pt[w % 2][:, :].rearrange("p (i o) -> p i o", i=2)
                            dst = m.wall[:, :, w * D:(w + 1) * D] if w < 3 else m.woT[:, :, :]
                            act.activation(dst, src, ACT.Copy).then_inc(S.w_evac, 1)
                    act.wait_ge(S.var_made, g + 1)
                    act.activation(m.rstd[:, g * LG:(g + 1) * LG], m.var[:, g * LG:(g + 1) * LG], ACT.Sqrt).then_inc(S.std_made, 1)
                    for t in range(g * LG, (g + 1) * LG):
                        act.wait_ge(S.xn_made, t + 1)
                        wait(act, S.squared, t - 1)
                        act.activation(sq[:, t % 2, :], m.xn[:, t, :], ACT.Square, accum_out=m.ss[:, t:t + 1]).then_inc(S.squared, 1)
                act.wait_ge(S.ss_made, 1)
                act.activation(m.rms[:, :], m.ss[:, :], ACT.Sqrt).then_inc(S.norm_made, 1)

            @block.tensor
            def _(pe):
                pe.wait_ge(S.before_made, 1)
                for j in range(TG):
                    for g in range(RG):
                        pe.matmul(psr[0:TP, j:j + 1], before[:, g, j * TP:(j + 1) * TP], ones[:, 0:1], start=(g == 0), stop=(g == RG - 1))
                for g in range(RG):
                    last = pe.matmul(pst[0:2, 0:STEPS], ones[:, :], before[:, g, :], start=(g == 0), stop=(g == RG - 1))
                last.then_inc(S.rows_counted, 1)
                pe.wait_ge(S.ident_made, 3)
                pe.wait_ge(S.w_in, 96)
                for w in range(4):
                    wait(pe, S.w_evac, w - 1)
                    for i in range(2):
                        for o in range(2):
                            last = pe.transpose(pt[w % 2][:, i * D + o * 128:i * D + (o + 1) * 128],
                                                wnat[:, w, o, i * 128:(i + 1) * 128], m.ident[:, :])
                    last.then_inc(S.w_turned, 1)
                pe.wait_ge(S.w_evac, 4)

                pe.wait_ge(S.keys_made, 1)
                pe.wait_ge(S.ident_made, 3)
                for g in range(TG):
                    pe.transpose(psl[:, g, 0:TP], dst_f[:, g, :], m.ident[0:TP, 0:TP])
                    last = pe.transpose(pss[:, g, 0:TP], src_f[:, g, :], m.ident[0:TP, 0:TP])
                last.then_inc(S.tbl_turned, 1)


def project(nc, m):
    with ExitStack() as ctx:
        def sb(n, s, d=F32):
            return ctx.enter_context(nc.sbuf_tensor(n, s, d))
        wall, bqkv, bo, rms = m.wall, m.bqkv, m.bo, m.rms
        xr = sb("xr", [TT, 2, D])
        xnT = sb("xnT", [128, 2, 2, TT])
        kst = sb("kst", [TT, 2, D])
        vst = sb("vst", [TT, 2, H, VW])
        qf = sb("qf", [TT, D])
        qr = sb("q_rest", [TT, D])
        keys, zero = m.keys, m.zero
        pt = [ctx.enter_context(nc.psum_tensor(f"pt{i}", [128, 512], F32)) for i in range(2)]
        pa = [ctx.enter_context(nc.psum_tensor(f"pa{i}", [TT, 512], F32)) for i in range(2)]
        pb = [ctx.enter_context(nc.psum_tensor(f"pb{i}", [TT, 512], F32)) for i in range(2)]
        pc = [ctx.enter_context(nc.psum_tensor(f"pc{i}", [TT, 512], F32)) for i in range(2)]
        S = m.sem

        def tiles(eng, body):
            body(0, 0, 0, False)
            body(1, 1, 0, False)
            body(2, 0, 1, False)
            with eng.Fori(2, 12) as k:
                body(2 * k - 1, 1, k - 1, False)
                body(2 * k, 0, k, False)
            body(23, 1, 11, False)
            body(24, 0, 12, True)

        with nc.Block() as block:
            @block.sync
            def _(sp):
                for h in range(H):
                    sp.dma_start(keys[h * U:(h + 1) * U, :, :], bass.AP(m.key.tensor, 0, [[128, U], [U * 128, CH], [1, 130]])).then_inc(S.key_in, 16)
                sp.wait_ge(S.zero_made, 1)
                rows = EX * CAP
                for r in range(0, rows, 512):
                    p = min(512, rows - r) // 4
                    sp.dma_start(m.slots[r:r + 4 * p, :].rearrange("(p a) d -> p (a d)", a=4), zero[0:p, :]).then_inc(S.zero_out, 16)

                def body(t, par, turn, last):
                    sp.wait_ge(S.qkv_out, t + 1)
                    rows = bass.ds(t * TT, TT)
                    sp.dma_start(m.kv_d[rows, 0:D], kst[:, par, :]).then_inc(S.kv_stored[par], 16)
                    sp.dma_start(m.kv_d[rows, D:KV], vst[:, par, :, :].rearrange("p h c -> p (h c)")).then_inc(S.kv_stored[par], 16)
                tiles(sp, body)
                sp.wait_ge(S.kv_stored[0], 13 * 32)
                sp.wait_ge(S.kv_stored[1], 12 * 32)
                sp.wait_ge(S.zero_out, 16 * (-(-rows // 512)))

            @block.gpsimd
            def _(pool):
                pool.memset(zero[:], 0.0).then_inc(S.zero_made, 1)
                pool.memset(m.mixv[:, :, HID:HID + 1], 1.0)
                pool.memset(vst[:, :, :, HD:VW], 1.0).then_inc(S.mixv_one, 1)
                pool.wait_ge(S.bo_in, 16)

                def body(t, par, turn, last):
                    pool.wait_ge(S.squared, t + 1)
                    pool.nop(nofuse=True)
                    if not (isinstance(t, int) and t < 2):
                        pool.wait_ge(S.xn_turned, t - 1)
                        pool.nop(nofuse=True)
                    pool.tensor_copy(xr[:, par, :], at(m.xn, t)).then_inc(S.xr_made, 1)
                    pool.tensor_tensor(at(m.base, t), at(m.base, t), at(m.xn, t), ALU.add).then_inc(S.base_x, 1)
                    pool.wait_ge(S.base_x, t + 1)
                    pool.nop(nofuse=True)
                    pool.tensor_tensor(at(m.base, t), at(m.base, t), bo[:, :], ALU.add)
                tiles(pool, body)

            @block.vector
            def _(dve):
                dve.wait_ge(S.b_in, 48)
                dve.wait_ge(S.key_in, 16 * H)
                dve.wait_ge(S.mixv_one, 1)

                def borders(c):
                    kc = at(keys, c)
                    dve.tensor_tensor(at(m.fwd, c), kc[:, 1:129], kc[:, 0:128], ALU.not_equal).then_inc(S.borders_made, 1)
                    dve.tensor_tensor(at(m.bwd, c), kc[:, 1:129], kc[:, 2:130], ALU.not_equal).then_inc(S.borders_made, 1)

                def penalties(c):
                    dve.wait_ge(S.borders_made, 2 * c + 2)
                    for b in (m.fwd, m.bwd):
                        dve.tensor_scalar(at(b, c), at(b, c), -RESET, None, ALU.mult).then_inc(S.costs_made, 1)

                def any_border(c):
                    dve.wait_ge(S.costs_made, 2 * c + 2)
                    for i, b in enumerate((m.fwd, m.bwd)):
                        dve.tensor_reduce(at(m.edge_any, c)[:, i:i + 1], at(b, c), X, ALU.min)

                def body(t, par, turn, last):
                    q3 = at(m.q3, t)
                    dve.wait_ge(S.projected, t + 1)
                    wait(dve, S.kv_stored[par], 32 * turn)
                    wait(dve, S.q_split, 3 * t)
                    dve.tensor_tensor(qf[:, :], pa[par][:, 0:D], bqkv[:, 0:D], ALU.add).then_inc(S.q_whole, 1)
                    dve.tensor_tensor(kst[:, par, :], pa[par][:, D:2 * D], bqkv[:, D:2 * D], ALU.add)
                    dve.tensor_tensor(vst[:, par, :, 0:HD], pb[par][:, 0:D].rearrange("p (h d) -> p h d", h=H),
                                      bqkv[:, 2 * D:3 * D].rearrange("p (h d) -> p h d", h=H), ALU.add).then_inc(S.qkv_out, 1)
                    dve.wait_ge(S.q_whole, t + 1)
                    dve.tensor_copy(q3[:, 0, :], qf[:, :]).then_inc(S.q_split, 1)
                    borders(t + 1)
                    penalties(t)
                    dve.wait_ge(S.q_split, 3 * t + 1)
                    dve.tensor_tensor(qr[:, :], qf[:, :], q3[:, 0, :], ALU.subtract).then_inc(S.q_rest, 1)
                    dve.wait_ge(S.q_rest, t + 1)
                    dve.tensor_copy(q3[:, 1, :], qr[:, :]).then_inc(S.q_split, 1)
                    any_border(t)
                    dve.wait_ge(S.q_split, 3 * t + 2)
                    dve.tensor_tensor(q3[:, 2, :], qr[:, :], q3[:, 1, :], ALU.subtract).then_inc(S.q_split, 1)
                borders(0)
                tiles(dve, body)
                penalties(NT)
                any_border(NT)
            @block.scalar
            def _(act):
                def turn_out(t, par):
                    act.wait_ge(S.xn_turned, t + 1)
                    wait(act, S.projected, t - 1)
                    act.activation(xnT[:, par, :, :], pt[par][:, 0:2 * TT].rearrange("p (c n) -> p c n", c=2), ACT.Copy).then_inc(S.xnT_made, 1)

                def body(t, par, turn, last):
                    if not last:
                        turn_out(t + 1, 1 - par)
                    act.wait_ge(S.projected, t + 1)
                    if isinstance(t, int) and t == 0:
                        act.wait_ge(S.rms_made, 1)
                    r = at(rms.rearrange("p (t o) -> p t o", o=1), t)
                    act.activation(at(m.mixq, t), pc[par][:, 0:HID], ACT.Copy, scale=r)
                    act.activation(at(m.mixk, t), pc[par][:, HID:2 * HID], ACT.Copy, scale=r)
                    act.activation(at(m.mixv, t)[:, 0:HID], pc[par][:, 2 * HID:3 * HID], ACT.Copy, scale=r).then_inc(S.mix_out, 1)
                turn_out(0, 0)
                tiles(act, body)

            @block.tensor
            def _(pe):
                def turn_in(t, par):
                    pe.wait_ge(S.xr_made, t + 1)
                    wait(pe, S.xnT_made, t - 1)
                    for c in range(2):
                        last = pe.transpose(pt[par][:, c * TT:(c + 1) * TT], xr[:, par, c * 128:(c + 1) * 128], m.ident[0:TT, 0:TT])
                    last.then_inc(S.xn_turned, 1)

                def body(t, par, turn, last):
                    if not last:
                        turn_in(t + 1, 1 - par)
                    pe.wait_ge(S.xnT_made, t + 1)
                    wait(pe, S.qkv_out, t - 1)
                    wait(pe, S.mix_out, t - 1)
                    for dst, a, b in ((pa, 0, 2 * D), (pb, 2 * D, 3 * D), (pc, 3 * D, WALL)):
                        for c in range(2):
                            mm = pe.matmul(dst[par][:, 0:b - a], xnT[:, par, c, :], wall[:, c, a:b], start=(c == 0), stop=(c == 1))
                    mm.then_inc(S.projected, 1)
                turn_in(0, 0)
                pe.wait_ge(S.w_ready, 2)
                tiles(pe, body)


def gather_chunk(pool, m, par, slot):
    for u in range(U):
        pool.indirect_dma_start(slot[:, u, :], None, m.kv_d,
                                bass.IndirectOffsetOnAxis(ap=m.src_e[:, par, u:u + 1].bitcast(U32), axis=0)).then_inc(m.sem.arrived[par * 8 + u // 2], 16)


def linear_attention(nc, m, io):
    with ExitStack() as ctx:
        def sb(n, s, d=F32):
            return ctx.enter_context(nc.sbuf_tensor(n, s, d))

        def ps(n, s):
            return ctx.enter_context(nc.psum_tensor(n, s, F32))
        qmax = sb("qmax", [TT, NT * MH])
        kpart = sb("kpart", [TT, HID])
        kmax = sb("kmax", [128, 2])
        mk = sb("mk", [128, MEM])
        mvm = sb("mvm", [128, MEM])
        kmrow = sb("kmrow", [1, HID])
        ones = sb("ones_m", [1, TT])
        memk = sb("memk", [MEM, HID])
        memv = sb("memv", [MEM, HID + 1])
        wo = sb("w_out_sb", [128, D])
        cd = sb("cd", [128, HID])
        cdT = sb("cdT", [128, HID])
        csum = sb("csum", [128, 1])
        wc = sb("wc", [128, D])
        bout = sb("bout", [TT, D])
        gout = sb("gout", [TT, D])
        qr = sb("qr", [TT, 2, HID])
        qT = sb("qT", [128, 2, TT])
        ysq = sb("ysq", [TT, 2, D])
        yss = sb("yss", [TT, NT])
        p1, p2, p3 = ps("p1", [128, 512]), ps("p2", [128, 512]), ps("p3", [128, 512])
        pq = [ps(f"pq{i}", [128, 512]) for i in range(2)]
        py = [ps(f"py{i}", [TT, 512]) for i in range(2)]
        S = m.sem
        y = m.xn
        qv = m.mixq.rearrange("p t (h d) -> p (t h) d", h=MH)
        qf = m.mixq.rearrange("p t c -> p (t c)")
        yss_t = yss.rearrange("p (t o) -> p t o", o=1)

        def turns(eng, body):
            for t in range(5):
                body(t, t % 2)
            with eng.Fori(3, 12) as k:
                body(2 * k - 1, 1)
                body(2 * k, 0)
            for t in range(23, NT + 4):
                body(t, t % 2)

        def exists(t):
            return not isinstance(t, int) or 0 <= t < NT

        kf = m.mixk.rearrange("p t c -> p (t c)")
        with nc.Block() as block:
            @block.sync
            def _(sp):
                mem = io.mem_kv.rearrange("a h d m -> a (h d) m")
                sp.dma_start(mk[:, :], mem[0]).then_inc(S.mem_in, 16)
                sp.dma_start(mvm[:, :], mem[1]).then_inc(S.mem_in, 16)
                sp.dma_start(wo[:, :], io.w_out).then_inc(S.mem_in, 16)
                sp.dma_start(bout[:, :], io.b_out.partition_broadcast(TT)).then_inc(S.mem_in, 16)
                sp.dma_start(gout[:, :], io.g_out.partition_broadcast(TT)).then_inc(S.mem_in, 16)

            @block.gpsimd
            def _(pool):
                pool.memset(ones[:], 1.0).then_inc(S.la_const, 1)
                pool.memset(memv[:], 1.0).then_inc(S.la_const, 1)
                pool.memset(cd[:], 0.0).then_inc(S.la_const, 1)
                gather_chunk(pool, m, 0, m.slot0)

                with pool.Fori(0, NT) as t:
                    pool.wait_ge(S.y_scaled, t + 1)
                    pool.nop(nofuse=True)
                    pool.tensor_tensor(at(m.base, t), at(m.base, t), at(y, t), ALU.add)

            @block.vector
            def _(dve):
                st = m.dve_steps.on(dve)
                dve.tensor_reduce(kpart[:, :], m.mixk.rearrange("p t c -> p c t"), X, ALU.max).then_inc(S.kmax1, 1)
                st.link(dve.tensor_reduce(qmax[:, :], qv, X, ALU.max))
                dve.tensor_tensor(qv, qv, spread(qmax[:, :], 2, MD), ALU.subtract).then_inc(S.q_shifted, 1)
                dve.wait_ge(S.mem_in, 80)
                st.then(dve.tensor_reduce(kmax[:, 0:1], mk[:, :], X, ALU.max))
                dve.wait_ge(S.kmax_turned, 1)
                st.link(dve.tensor_reduce(kmax[:, 1:2], p1[:, 0:TT], X, ALU.max))
                st.link(dve.tensor_tensor(kmax[:, 0:1], kmax[:, 0:1], kmax[:, 1:2], ALU.max))
                dve.tensor_scalar(mk[:, :], mk[:, :], kmax[:, 0:1], None, ALU.subtract).then_inc(S.kmax2, 1)
                dve.wait_ge(S.kmax_row, 1)
                dve.tensor_copy(kmrow[:, :], p2[0:1, 0:HID]).then_inc(S.kmax3, 1)
                dve.wait_ge(S.kmax_wide, 1)
                dve.tensor_tensor(m.mixk[:, :, :], m.mixk[:, :, :], spread(p3[0:TT, 0:HID], 1, NT), ALU.subtract).then_inc(S.k_shifted, 1)
                dve.wait_ge(S.mem_turned, 1)
                dve.wait_ge(S.la_const, 3)
                dve.tensor_copy(memk[:, :], p2[0:MEM, 128:256])
                dve.tensor_copy(memv[:, 0:HID], p2[0:MEM, 256:384]).then_inc(S.mem_ready, 1)
                dve.wait_ge(S.q_exp, 1)
                st.link(dve.tensor_reduce(qmax[:, :], qv, X, ALU.add))
                st.link(dve.reciprocal(qmax[:, :], qmax[:, :]))
                dve.tensor_tensor(qv, qv, spread(qmax[:, :], 2, MD), ALU.mult).then_inc(S.q_soft, 1)
                st.then(dve.tensor_scalar(gout[:, :], gout[:, :], float(D) ** 0.5, None, ALU.mult))
                dve.wait_ge(S.ctx_made, 1)
                st.link(dve.reciprocal(csum[:, :], p1[:, 128 + HID:129 + HID]))
                for h in range(MH):
                    r = slice(h * MD, (h + 1) * MD)
                    last = dve.tensor_scalar(cd[r, r], p1[r, 128 + h * MD:128 + (h + 1) * MD], csum[r, 0:1], float(MD) ** -0.5, ALU.mult, ALU.mult)
                last.then_inc(S.cd_made, 1)
                dve.wait_ge(S.cd_turned, 1)
                dve.tensor_copy(cdT[:, :], p3[:, 0:HID]).then_inc(S.cdT_made, 1)
                dve.wait_ge(S.wc_prod, 1)
                dve.tensor_copy(wc[:, :], p3[:, 128:128 + D]).then_inc(S.wc_made, 1)

                def body(t, par):
                    if exists(t):
                        dve.wait_ge(S.y_prod, t + 1)
                        dve.tensor_tensor(at(y, t), py[par][:, 0:D], bout[:, :], ALU.add).then_inc(S.y_made, 1)
                    if exists(t - 2):
                        dve.wait_ge(S.y_squared, t - 1)
                        dve.tensor_scalar(at(yss_t, t - 2), at(yss_t, t - 2), 1e-24, None, ALU.max).then_inc(S.yss_made, 1)
                    if exists(t - 3):
                        dve.wait_ge(S.ynorm_made, t - 2)
                        dve.nop(nofuse=True)
                        dve.reciprocal(at(yss_t, t - 3), at(yss_t, t - 3)).then_inc(S.yinv_made, 1)
                    if exists(t - 4):
                        dve.wait_ge(S.yinv_made, t - 3)
                        dve.scalar_tensor_tensor(out=at(y, t - 4), in0=at(y, t - 4), scalar=at(yss_t, t - 4), in1=gout[:, :],
                                                 op0=ALU.mult, op1=ALU.mult).then_inc(S.y_scaled, 1)
                turns(dve, body)

            @block.scalar
            def _(act):
                act.wait_ge(S.q_shifted, 1)
                act.activation(qf, qf, ACT.Exp).then_inc(S.q_exp, 1)
                act.wait_ge(S.kmax2, 1)
                act.activation(mk[:, :], mk[:, :], ACT.Exp).then_inc(S.mk_exp, 1)
                act.wait_ge(S.k_shifted, 1)
                act.activation(kf, kf, ACT.Exp).then_inc(S.k_exp, 1)

                def stage(t, par):
                    wait(act, S.q_turned, t - 1)
                    act.activation(qr[:, par, :], at(m.mixq, t), ACT.Copy).then_inc(S.qr_made, 1)

                def body(t, par):
                    if exists(t):
                        act.wait_ge(S.q_turned, t + 1)
                        wait(act, S.y_prod, t - 1)
                        act.activation(qT[:, par, :], pq[par][:, 0:TT], ACT.Copy).then_inc(S.qT_made, 1)
                    if exists(t + 2):
                        stage(t + 2, par)
                    if exists(t - 1):
                        act.wait_ge(S.y_made, t)
                        wait(act, S.y_squared, t - 2)
                        act.activation(ysq[:, 1 - par, :], at(y, t - 1), ACT.Square, accum_out=at(yss_t, t - 1)).then_inc(S.y_squared, 1)
                    if exists(t - 3):
                        act.wait_ge(S.yss_made, t - 2)
                        act.activation(at(yss_t, t - 3), at(yss_t, t - 3), ACT.Sqrt).then_inc(S.ynorm_made, 1)
                act.wait_ge(S.q_soft, 1)
                stage(0, 0)
                stage(1, 1)
                turns(act, body)

            @block.tensor
            def _(pe):
                pe.wait_ge(S.kmax1, 1)
                pe.transpose(p1[:, 0:TT], kpart[:, :], m.ident[0:TT, 0:TT]).then_inc(S.kmax_turned, 1)
                pe.wait_ge(S.kmax2, 1)
                pe.transpose(p2[0:1, 0:HID], kmax[:, 0:1], m.ident[:, :]).then_inc(S.kmax_row, 1)
                pe.wait_ge(S.kmax3, 1)
                pe.wait_ge(S.la_const, 1)
                pe.matmul(p3[0:TT, 0:HID], ones[:, :], kmrow[:, :], start=True, stop=True).then_inc(S.kmax_wide, 1)
                pe.wait_ge(S.mk_exp, 1)
                pe.transpose(p2[0:MEM, 128:256], mk[:, :], m.ident[:, :])
                pe.transpose(p2[0:MEM, 256:384], mvm[:, :], m.ident[:, :]).then_inc(S.mem_turned, 1)
                pe.wait_ge(S.k_exp, 1)
                for t in range(NT):
                    pe.matmul(p1[:, 128:129 + HID], m.mixk[:, t, :], m.mixv[:, t, :], start=(t == 0), stop=False)
                pe.wait_ge(S.mem_ready, 1)
                pe.matmul(p1[:, 128:129 + HID], memk[:, :], memv[:, :], start=False, stop=True).then_inc(S.ctx_made, 1)
                pe.wait_ge(S.cd_made, 1)
                pe.transpose(p3[:, 0:HID], cd[:, :], m.ident[:, :]).then_inc(S.cd_turned, 1)
                pe.wait_ge(S.cdT_made, 1)
                pe.matmul(p3[:, 128:128 + D], cdT[:, :], wo[:, :], start=True, stop=True).then_inc(S.wc_prod, 1)
                pe.wait_ge(S.wc_made, 1)

                def turn(t, par):
                    pe.wait_ge(S.qr_made, t + 1)
                    wait(pe, S.qT_made, t - 1)
                    pe.transpose(pq[par][:, 0:TT], qr[:, par, :], m.ident[0:TT, 0:TT]).then_inc(S.q_turned, 1)

                def body(t, par):
                    if exists(t):
                        pe.wait_ge(S.qT_made, t + 1)
                        wait(pe, S.y_made, t - 1)
                        pe.matmul(py[par][:, 0:D], qT[:, par, :], wc[:, :], start=True, stop=True).then_inc(S.y_prod, 1)
                    if exists(t + 2):
                        turn(t + 2, par)
                turn(0, 0)
                turn(1, 1)
                turns(pe, body)


(LOCAL, CARRY, CARRY_FLAT, KEEP, COLUMN, FORWARD, BACK_LOCAL, CARRY_BACK, CARRY_BACK_FLAT, FALL,
 COLUMN_BACK, FALL_CAP, BACK, SHIFT, FIRST, FIRST_PAIR, FACTOR) = range(1, 18)
CHAIN = FACTOR
(PE_ENDS, PE_CARRY, PE_ENDS_BACK, PE_CARRY_BACK, PE_TURNED) = range(1, 6)
CHAIN_PE = PE_TURNED
(ACT_BORDERS, ACT_ROWS, ACT_ROWS_BACK, ACT_FALL, ACT_WEIGHTS) = range(1, 6)
CHAIN_ACT = ACT_WEIGHTS


def attention(nc, m):
    with ExitStack() as ctx:
        def sb(n, s, d=F32):
            return ctx.enter_context(nc.sbuf_tensor("at_" + n, s, d))

        def ps(n, s):
            return ctx.enter_context(nc.psum_tensor("at_" + n, s, F32))
        slot = [m.slot0, sb("slot1", [128, U, KV])]
        locrow = sb("locrow", [TT, U * 128], BF16)
        hotT = sb("hotT", [TT, U, 128], BF16)
        prod = sb("prod", [128, 2, 2, D])
        sc = sb("sc", [128, H, U])
        scp = sb("sc_pen", [128, H, U])
        bst = sb("border_st", [128, 2])
        bwd = sb("bwd_st", [128, 128], BF16)
        fm = sb("fwd_max", [128, 128])
        bm = sb("back_max", [128, 128])
        row = sb("row_f", [1, 2, H, U + 1])
        run = sb("run_f", [1, H, U + 1])
        rowb = sb("row_b", [1, 2, H, U + 1])
        runb = sb("run_b", [1, H, U + 1])
        line = sb("line", [1, 2, H, U])
        col = sb("col", [128, 2])
        pT = sb("pT", [128, 128])
        fall = sb("fall", [1, H])
        fall2 = sb("fall2", [2, H])
        pair = sb("pair", [2, TT])
        sign = sb("sign", [2, 2])
        fac = sb("fac", [TT, H])
        one = sb("one_c", [1, 1])
        habs = sb("habs", [128, 4, TT])
        hot = sb("hot", [128, 8, TT])
        pv = sb("pv", [128, 4, H, VW])
        pq = [ps(f"pq{i}", [128, 512]) for i in range(3)]
        pc = ps("pchain", [128, 512])
        pp = ps("pp", [128, 512])
        pa = [ps(f"pa{i}", [TT, 512]) for i in range(3)]
        S = m.sem
        scT = pc[:, 0:128]
        loc_c = m.loc.rearrange("(k i) e -> k (i e)", i=U)
        ph = pp[:, 0:128].rearrange("p (h i) -> p h i", h=H)

        def rounds(eng, body):
            body(0, None, 1, 0, 0)
            body(1, 0, 2, 1, 0)
            with eng.Fori(1, CH // 2 - 1) as k:
                body(2 * k, 2 * k - 1, 2 * k + 1, 0, k)
                body(2 * k + 1, 2 * k, 2 * k + 2, 1, k)
            body(CH - 2, CH - 3, CH - 1, 0, CH // 2 - 1)
            body(CH - 1, CH - 2, None, 1, CH // 2 - 1)
            body(None, CH - 1, None, 0, CH // 2)

        def windows_of(chunk, steps, engines):
            return nc.values_load_multi_w_load_instructions(
                flat(m.win_of[0:1, bass.ds(chunk, 1), steps]), engines=engines, min_val=0, max_val=NT - 1,
                skip_runtime_bounds_check_because="edge_tables clamps the windows to 0 .. NT - 1")[1]

        with nc.Block() as block:
            @block.sync
            def _(sp):
                def body(n, c, nxt, par, turn):
                    if n is not None:
                        wait(sp, S.hotT_made, n)
                        sp.dma_start(locrow[:, :], loc_c[bass.ds(n, 1), :].to_broadcast([TT, U * 128])).then_inc(S.loc_in, 16)
                rounds(sp, body)

            @block.gpsimd
            def _(pool):
                pool.memset(one[:], 1.0).then_inc(S.at_const, 1)
                pool.memset(row[:], -RESET).then_inc(S.at_const, 1)
                pool.memset(rowb[:], -RESET).then_inc(S.at_const, 1)
                pool.memset(fall2[:], 1.0).then_inc(S.at_const, 1)
                pool.iota(sign[:, 0:1], pattern=[[0, 1]], base=1, channel_multiplier=-2, allow_small_or_imprecise_dtypes=True).then_inc(S.at_const, 1)
                pool.iota(sign[:, 1:2], pattern=[[0, 1]], base=0, channel_multiplier=1, allow_small_or_imprecise_dtypes=True).then_inc(S.at_const, 1)
                gather_chunk(pool, m, 1, slot[1])
                with pool.Fori(1, CH // 2) as k:
                    for par in range(2):
                        for u in range(U):
                            if u % 4 == 0:
                                pool.wait_ge(S.idx_ready, 8 * k + 4 * par + u // 4 - 7)
                                pool.nop(nofuse=True)
                                pool.wait_ge(S.pv_made, 2 * U * k + U * par + u + 4 - 2 * U)
                                pool.nop(nofuse=True)
                            pool.indirect_dma_start(slot[par][:, u, :], None, m.kv_d,
                                                    bass.IndirectOffsetOnAxis(ap=m.idx[:, par, u:u + 1].bitcast(U32), axis=0)).then_inc(S.arrived[par * 8 + u // 2], 16)

            @block.scalar
            def _(act):
                def stage(c, par, q):
                    r = slice(4 * q, 4 * q + 4)
                    act.wait_ge(S.pv_made, U * c + 4 * q + 4)
                    act.activation(m.idx[:, par, r], at(m.src_e, c + 2)[:, r], ACT.Copy).then_inc(S.idx_ready, 1)

                def hots(c, g):
                    wait(act, S.hot_made, 4 * c + g)
                    for u in range(4 * g, 4 * g + 4):
                        last = act.activation(habs[:, u % 4, :], m.iota_w[:, :], ACT.Abs, bias=at(m.nloc_e, c)[:, u:u + 1])
                    last.then_inc(S.hot_abs, 1)
                    act.wait_ge(S.hot_abs, 4 * c + g + 1)
                    wait(act, S.summed, U * c + 4 * g - 4)
                    act.activation(hot[:, 4 * (g % 2):4 * (g % 2) + 4, :], habs[:, :, :], ACT.Relu, bias=m.one_col[:, 0:1],
                                   scale=-1.0).then_inc(S.hot_made, 1)

                def body(n, c, nxt, par, turn):
                    if c is None:
                        return
                    act.activation(bst[:, :], at(m.edge_any, c), ACT.Copy)
                    act.activation(bwd[:, :], at(m.bwd, c), ACT.Copy).then_inc(S.chain_act, 1)
                    hots(c, 0)
                    act.wait_ge(S.chain_pe, CHAIN_PE * c + PE_ENDS)
                    act.activation(row[:, :, :, 1:U + 1], pc[0:1, 128:384].rearrange("p (a h i) -> p a h i", a=2, h=H), ACT.Copy).then_inc(S.chain_act, 1)
                    hots(c, 1)
                    act.wait_ge(S.chain_pe, CHAIN_PE * c + PE_ENDS_BACK)
                    act.activation(rowb[:, :, :, 0:U], pc[0:1, 128:384].rearrange("p (a h i) -> p a h i", a=2, h=H), ACT.Copy).then_inc(S.chain_act, 1)
                    act.wait_ge(S.chain, CHAIN * c + FALL_CAP)
                    act.activation(fall2[0:1, :], fall[:, :], ACT.Exp, scale=float(HD) ** -0.5).then_inc(S.chain_act, 1)
                    act.wait_ge(S.chain, CHAIN * c + SHIFT)
                    act.activation(pT[:, :], pT[:, :], ACT.Exp, scale=float(HD) ** -0.5).then_inc(S.chain_act, 1)
                    for q in range(4):
                        if n is not None:
                            stage(c, 1 - par, q)
                        if q < 2:
                            hots(c, q + 2)
                rounds(act, body)

            @block.vector
            def _(dve):
                def turned_hots(n):
                    dve.wait_ge(S.loc_in, 16 * n + 16)
                    wait(dve, S.q_spread, 8 * n)
                    dve.tensor_scalar(flat(hotT[:, :, :]), locrow[:, :], m.iota_p[0:TT, 0:1], None, ALU.is_equal).then_inc(S.hotT_made, 1)

                def reduce(n, j):
                    dve.wait_ge(S.prod_made, 8 * n + j + 1)
                    wait(dve, S.sc_made, n)
                    dve.tensor_reduce(sc[:, :, 2 * j:2 * j + 2].rearrange("p h i -> p i h"),
                                      prod[:, j % 2, :, :].rearrange("p i (h d) -> p i h d", h=H), X, ALU.add).then_inc(S.reduced, 1)

                def chain(c, piece):
                    def after(step):
                        dve.wait_ge(S.chain, CHAIN * c + step)

                    def turned(step):
                        dve.wait_ge(S.chain_pe, CHAIN_PE * c + step)

                    def then(ins):
                        ins.then_inc(S.chain, 1)
                    F = at(m.fwd, c)
                    if piece == (0, 0):
                        dve.wait_ge(S.sc_turned, c + 1)
                        then(dve.tensor_tensor_scan(fm[:, :], F, scT, -RESET, ALU.add, ALU.max))
                    elif piece == (2, 0):
                        dve.wait_ge(S.chain_act, CHAIN_ACT * c + ACT_ROWS)
                        then(dve.tensor_tensor_scan(run.rearrange("p h i -> p (h i)"), row[:, 1].rearrange("p h i -> p (h i)"),
                                                    row[:, 0].rearrange("p h i -> p (h i)"), -RESET, ALU.add, ALU.max))
                        after(CARRY)
                        then(dve.tensor_copy(line[:, 0, :, :], run[:, :, 0:U]))
                        then(dve.tensor_copy(row[:, 0, :, 0], run[:, :, U]))
                    elif piece == (3, 0):
                        turned(PE_CARRY)
                        then(dve.tensor_copy(col[:, 0:1], pc[:, 384:385]))
                    elif piece == (3, 1):
                        after(COLUMN)
                        then(dve.tensor_tensor_scan(fm[:, :], F, scT, col[:, 0:1], ALU.add, ALU.max))
                    elif piece == (4, 0):
                        dve.wait_ge(S.chain_act, CHAIN_ACT * c + ACT_BORDERS)
                        after(FORWARD)
                        then(dve.tensor_tensor_scan(bm[:, ::-1], bwd[:, ::-1], fm[:, ::-1], -RESET, ALU.add, ALU.max))
                    elif piece == (5, 1):
                        dve.wait_ge(S.chain_act, CHAIN_ACT * c + ACT_ROWS_BACK)
                        then(dve.tensor_tensor_scan(runb.rearrange("p h i -> p (h i)")[:, ::-1],
                                                    rowb[:, 1].rearrange("p h i -> p (h i)")[:, ::-1],
                                                    rowb[:, 0].rearrange("p h i -> p (h i)")[:, ::-1], -RESET, ALU.add, ALU.max))
                        after(CARRY_BACK)
                        then(dve.tensor_copy(line[:, 1, :, :], runb[:, :, 1:U + 1]))
                        then(dve.tensor_tensor(fall[:, :], run[:, :, 0], runb[:, :, 0], ALU.subtract))
                    elif piece == (6, 1):
                        turned(PE_CARRY_BACK)
                        then(dve.tensor_copy(col[:, 1:2], pc[:, 385:386]))
                        after(FALL)
                        then(dve.tensor_scalar(fall[:, :], fall[:, :], 0.0, None, ALU.min))
                    elif piece == (7, 0):
                        after(COLUMN_BACK)
                        then(dve.tensor_tensor_scan(bm[:, ::-1], bwd[:, ::-1], fm[:, ::-1], col[:, 1:2], ALU.add, ALU.max))
                    elif piece == (7, 1):
                        after(BACK)
                        then(dve.tensor_tensor(pT[:, :], scT, bm[:, :], ALU.subtract))
                        then(dve.tensor_scalar(pair[:, :], m.iota_w[0:2, :], at(m.first_loc.rearrange("p (k o) -> p k o", o=1), c), None, ALU.is_equal))
                    elif piece == (8, 0):
                        after(FIRST)
                        then(dve.tensor_scalar(pair[:, :], pair[:, :], sign[:, 0:1], sign[:, 1:2], ALU.mult, ALU.add))
                    elif piece == (8, 1):
                        turned(PE_TURNED)
                        then(dve.tensor_copy(fac[:, :], pc[0:TT, 386:386 + H]))

                def add(c, u, window):
                    dve.wait_ge(S.summed, U * c + u + 1)
                    wait(dve, S.added, U * c + u)
                    dst = at(m.agg, window)
                    dve.tensor_tensor(dst, dst, pa[u % 3][:, 0:H * VW].rearrange("p (h c) -> p h c", h=H), ALU.add).then_inc(S.added, 1)

                def body(n, c, nxt, par, turn):
                    for j in range(8):
                        if n is not None:
                            dve.wait_ge(S.arrived[par * 8 + j], 32 * turn + 32)
                            dve.wait_ge(S.q_spread, 8 * n + j + 1)
                            wait(dve, S.reduced, 8 * n + j - 1)
                            dve.tensor_tensor(prod[:, j % 2, :, :], pq[j % 3][:, :].rearrange("p (i d) -> p i d", i=2),
                                              slot[par][:, 2 * j:2 * j + 2, 0:D], ALU.mult).then_inc(S.prod_made, 1)
                        if c is not None and not (isinstance(c, int) and c == 0) and j < LATE:
                            if j == 0:
                                late = windows_of(c - 1, slice(U - LATE, U), DVE_ONLY)
                            add(c - 1, U - LATE + j, late[j])
                        if c is not None:
                            chain(c, (j, 0))
                        if n is not None and j:
                            reduce(n, j - 1)
                        if c is not None:
                            chain(c, (j, 1))
                    if n is not None:
                        reduce(n, 7)
                    if c is not None:
                        chain(c, (8, 0))
                    if n is not None:
                        if nxt is not None:
                            turned_hots(nxt)
                        dve.wait_ge(S.reduced, 8 * n + 8)
                        wait(dve, S.sc_turned, n)
                        dve.tensor_tensor(scp[:, :, :], sc[:, :, :], spread(at(m.pen_e, n), 1, H), ALU.add).then_inc(S.sc_made, 1)
                    if c is None:
                        return
                    wins = windows_of(c, slice(0, U), DVE_ONLY)
                    chain(c, (8, 1))
                    dve.wait_ge(S.chain, CHAIN * c + FACTOR)
                    wait(dve, S.added, U * c)
                    dst = at(m.agg, wins[0])
                    dve.tensor_tensor(dst, dst, spread(fac[:, :], 2, VW), ALU.mult).then_inc(S.rescaled, 1)
                    for u in range(U):
                        wait(dve, S.summed, U * c + u - 3)
                        dve.tensor_tensor(pv[:, u % 4, :, :], slot[1 - par][:, u, D:KV].rearrange("p (h c) -> p h c", h=H),
                                          spread(ph[:, :, u], 2, VW), ALU.mult).then_inc(S.pv_made, 1)
                        if u == LATE:
                            dve.wait_ge(S.rescaled, c + 1)
                        if u >= LATE:
                            add(c, u - LATE, wins[u - LATE])
                    if n is None:
                        for u in range(U - LATE, U):
                            add(c, u, wins[u])
                turned_hots(0)
                dve.memset(m.agg.rearrange("p t h c -> p (t h c)"), 0.0).then_inc(S.at_const, 1)
                dve.wait_ge(S.at_const, 7)
                rounds(dve, body)

            @block.tensor
            def _(pe):
                def spread_q(n, u, window):
                    j = u // 2
                    if u % 2 == 0 and j >= 3:
                        wait(pe, S.prod_made, 8 * n + j - 2)
                    for part in range(3):
                        mm = pe.matmul(pq[j % 3][:, (u % 2) * D:(u % 2 + 1) * D], hotT[:, u, :], at(m.q3, window)[:, part, :],
                                       start=(part == 0), stop=(part == 2))
                    if u % 2:
                        mm.then_inc(S.q_spread, 1)

                def chain(c, piece):
                    if piece in (0, 2):
                        back = piece // 2
                        pe.wait_ge(S.chain, CHAIN * c + (BACK_LOCAL if back else LOCAL))
                        pe.wait_ge(S.chain_act, CHAIN_ACT * c + ACT_BORDERS)
                        end = bm[:, 0:1] if back else fm[:, 127:128]
                        pe.transpose(pc[0:1, 128:256], end, m.ident[:, :])
                        pe.transpose(pc[0:1, 256:384], bst[:, back:back + 1], m.ident[:, :]).then_inc(S.chain_pe, 1)
                    elif piece in (1, 3):
                        back = piece // 2
                        pe.wait_ge(S.chain, CHAIN * c + (CARRY_BACK_FLAT if back else CARRY_FLAT))
                        pe.matmul(pc[:, 384 + back:385 + back], line[:, back].rearrange("p h i -> p (h i)"), one[:, :], start=True, stop=True).then_inc(S.chain_pe, 1)
                    else:
                        pe.wait_ge(S.chain_act, CHAIN_ACT * c + ACT_WEIGHTS)
                        pe.transpose(pp[:, 0:128], pT[:, :], m.ident[:, :])
                        pe.wait_ge(S.chain_act, CHAIN_ACT * c + ACT_FALL)
                        pe.wait_ge(S.chain, CHAIN * c + FIRST_PAIR)
                        pe.matmul(pc[0:TT, 386:386 + H], pair[:, :], fall2[:, :], start=True, stop=True).then_inc(S.chain_pe, 1)

                def body(n, c, nxt, par, turn):
                    if n is not None:
                        wins = windows_of(n, slice(AHEAD, U), PE_ONLY)
                    for j in range(8):
                        if n is not None and 2 * j >= AHEAD:
                            spread_q(n, 2 * j, wins[2 * j - AHEAD])
                            spread_q(n, 2 * j + 1, wins[2 * j + 1 - AHEAD])
                        if c is not None and j in (2, 4, 6, 7):
                            chain(c, (2, 4, 6, 7).index(j))
                    if c is not None:
                        chain(c, 4)
                    if nxt is not None:
                        ahead = windows_of(nxt, slice(0, AHEAD), PE_ONLY)
                    if n is not None:
                        pe.wait_ge(S.sc_made, n + 1)
                        if c is not None:
                            pe.wait_ge(S.chain, CHAIN * c + FACTOR)
                        pe.transpose(scT, scp[:, :, :].rearrange("p h i -> p (h i)"), m.ident[:, :]).then_inc(S.sc_turned, 1)
                    if c is None:
                        pe.wait_ge(S.hotT_made, nxt + 1)
                        for u in range(AHEAD):
                            spread_q(nxt, u, ahead[u])
                        return
                    for u in range(U):
                        if nxt is not None and u % 2 == 0 and u >= U - 2 * AHEAD:
                            if u == U - 2 * AHEAD:
                                pe.wait_ge(S.hotT_made, nxt + 1)
                            spread_q(nxt, u // 2 - (U // 2 - AHEAD), ahead[u // 2 - (U // 2 - AHEAD)])
                        wait(pe, S.added, U * c + u - 2)
                        wait(pe, S.hot_made, 4 * c + u // 4 + 1)
                        pe.wait_ge(S.pv_made, U * c + u + 1)
                        pe.matmul(pa[u % 3][:, 0:H * VW], hot[:, u % 8, :], pv[:, u % 4, :, :].rearrange("p h c -> p (h c)"),
                                  start=True, stop=True).then_inc(S.summed, 1)
                pe.wait_ge(S.at_const, 7)
                first = windows_of(0, slice(0, AHEAD), PE_ONLY)
                pe.wait_ge(S.hotT_made, 1)
                for u in range(AHEAD):
                    spread_q(0, u, first[u])
                rounds(pe, body)


def attention_out(nc, m, io):
    with ExitStack() as ctx:
        def sb(n, s, d=F32):
            return ctx.enter_context(nc.sbuf_tensor(n, s, d))
        rden = sb("rden", [TT, NT, H])
        an = sb("an", [TT, 2, D])
        hr = sb("hr", [TT, 2, D])
        anT = sb("anT", [128, 2, 2, TT])
        stats = sb("stats2", [TT, NT, 6])
        mean = sb("mean2", [TT, NT])
        tmp = sb("tmp2", [TT, NT])
        var = sb("var2", [TT, NT])
        gw = sb("gw", [128, 2, EX])
        gb = sb("gb", [TT, EX])
        pt = [ctx.enter_context(nc.psum_tensor(f"opt{i}", [128, 512], F32)) for i in range(2)]
        po = [ctx.enter_context(nc.psum_tensor(f"opo{i}", [TT, 512], F32)) for i in range(2)]
        pl = ctx.enter_context(nc.psum_tensor("opl", [TT, NT, EX], F32))
        S = m.sem

        def pairs(eng, body):
            for t in range(3):
                body(t, t % 2, True)
            with eng.Fori(2, 12) as k:
                body(2 * k - 1, 1, True)
                body(2 * k, 0, True)
            body(23, 1, False)
            body(24, 0, False)

        with nc.Block() as block:
            @block.sync
            def _(sp):
                sp.dma_start(gw[:, :, :], io.gate_w.rearrange("(c p) e -> p c e", p=128)).then_inc(S.gate_in, 16)
                sp.dma_start(gb[:, :], io.gate_b.partition_broadcast(TT)).then_inc(S.gate_in, 16)

            @block.vector
            def _(dve):
                st = m.dve_steps.on(dve)
                st.link(dve.tensor_scalar(rden[:, :, :], m.agg[:, :, :, HD], 0.5, None, ALU.max))
                st.link(dve.reciprocal(rden[:, :, :], rden[:, :, :]))

                def norm(t, par):
                    wait(dve, S.an_turned, t - 1)
                    dve.tensor_tensor(an[:, par, :].rearrange("p (h d) -> p h d", h=H),
                                      at(m.agg, t)[:, :, 0:HD],
                                      spread(at(rden, t), 2, HD), ALU.mult).then_inc(S.an_made, 1)

                def body(t, par, ahead):
                    if ahead:
                        norm(t + 2, par)
                    dve.wait_ge(S.out_prod, t + 1)
                    dve.tensor_tensor(at(m.base, t), at(m.base, t), po[par][:, 0:D], ALU.add).then_inc(S.x2_made, 1)
                    if isinstance(t, int) and t == 0:
                        return
                    dve.wait_ge(S.x2_made, t)
                    dve.bn_stats(at(stats, t - 1), at(m.base, t - 1)).then_inc(S.x2_stats, 1)
                norm(0, 0)
                norm(1, 1)
                pairs(dve, body)
                dve.wait_ge(S.x2_made, NT)
                dve.bn_stats(stats[:, NT - 1], m.base[:, NT - 1]).then_inc(S.x2_stats, 1)
                dve.wait_ge(S.x2_stats, NT)
                mean_and_var(dve, st, stats[:, :, :], mean[:, :], var[:, :], tmp[:, :]).then_inc(S.var2_made, 1)
                dve.wait_ge(S.std2_made, 1)
                st.link(dve.reciprocal(var[:, :], var[:, :]))
                with dve.Fori(0, NT) as t:
                    dve.tensor_scalar(at(m.h, t), at(m.base, t), at(mean.rearrange("p (t o) -> p t o", o=1), t), at(var.rearrange("p (t o) -> p t o", o=1), t),
                                      ALU.subtract, ALU.mult).then_inc(S.h_made, 1)
                dve.wait_ge(S.gate_in, 32)
                dve.wait_ge(S.logit_prod, NT)
                dve.tensor_tensor(m.logit[:, :, :], pl[:, :, :], spread(gb[:, :], 1, NT), ALU.add)

            @block.scalar
            def _(act):
                def turned(t, par, first, used):
                    act.wait_ge(S.an_turned, first + t + 1)
                    wait(act, used, t - 1)
                    act.activation(anT[:, par, :, :], pt[par][:, 0:2 * TT].rearrange("p (c n) -> p c n", c=2), ACT.Copy).then_inc(S.anT_made, 1)

                def stage(t, par):
                    act.wait_ge(S.h_made, t + 1)
                    wait(act, S.an_turned, NT + t - 1 if not isinstance(t, int) or t > 1 else 0)
                    act.activation(hr[:, par, :], at(m.h, t), ACT.Copy).then_inc(S.hr_made, 1)

                def rows(t, par, ahead):
                    turned(t, par, NT, S.logit_prod)
                    if ahead:
                        stage(t + 2, par)
                pairs(act, lambda t, par, ahead: turned(t, par, 0, S.out_prod))
                act.wait_ge(S.var2_made, 1)
                act.activation(var[:, :], var[:, :], ACT.Sqrt).then_inc(S.std2_made, 1)
                stage(0, 0)
                stage(1, 1)
                pairs(act, rows)

            @block.tensor
            def _(pe):
                def turn(t, par, src, ready, first):
                    pe.wait_ge(ready, t + 1)
                    wait(pe, S.anT_made, first + t - 1)
                    for c in range(2):
                        mm = pe.transpose(pt[par][:, c * TT:(c + 1) * TT], src[:, c * 128:(c + 1) * 128], m.ident[0:TT, 0:TT])
                    mm.then_inc(S.an_turned, 1)

                def body(t, par, ahead):
                    pe.wait_ge(S.anT_made, t + 1)
                    wait(pe, S.x2_made, t - 1)
                    for c in range(2):
                        mm = pe.matmul(po[par][:, 0:D], anT[:, par, c, :], m.woT[:, c, :], start=(c == 0), stop=(c == 1))
                    mm.then_inc(S.out_prod, 1)
                    if ahead:
                        turn(t + 2, par, an[:, par, :], S.an_made, 0)
                turn(0, 0, an[:, 0, :], S.an_made, 0)
                turn(1, 1, an[:, 1, :], S.an_made, 0)
                pairs(pe, body)

                def gate(t, par, ahead):
                    pe.wait_ge(S.anT_made, NT + t + 1)
                    for c in range(2):
                        mm = pe.matmul(at(pl, t), anT[:, par, c, :], gw[:, c, :], start=(c == 0), stop=(c == 1))
                    mm.then_inc(S.logit_prod, 1)
                    if ahead:
                        turn(t + 2, par, hr[:, par, :], S.hr_made, NT)
                turn(0, 0, hr[:, 0, :], S.hr_made, NT)
                turn(1, 1, hr[:, 1, :], S.hr_made, NT)
                pe.wait_ge(S.gate_in, 32)
                pairs(pe, gate)


def route(nc, m):
    with ExitStack() as ctx:
        def sb(n, s, d=F32):
            return ctx.enter_context(nc.sbuf_tensor(n, s, d))
        pr = sb("probs", [TT, NT, EX])
        e1 = sb("rt_e1", [TT, NT])
        e2 = sb("rt_e2", [TT, NT])
        pos = sb("rt_pos", [TT, NT])
        eid = sb("rt_eid", [TT, NT])
        slot = sb("rt_slot", [TT, NT])
        kept = sb("rt_kept", [TT, NT])
        node = sb("rt_node", [TT, NT])
        iota_e = sb("iota_e", [TT, EX])
        hot = sb("rt_hot", [TT, NT, EX])
        tmp = sb("rt_tmp", [TT, NT, EX])
        tri = sb("rt_tri", [TT, TT])
        ones = sb("rt_ones", [TT, TT])
        tot = sb("rt_tot", [TT, EX, NT])
        run = sb("rt_run", [TT, EX, NT])
        keep = sb("rt_keep", [TT, EX, NT])
        put = sb("rt_put", [TT, NT], I32)
        pi = ctx.enter_context(nc.psum_tensor("rt_pi", [TT, 512], F32))
        pj = ctx.enter_context(nc.psum_tensor("rt_pj", [TT, 512], F32))
        S = m.sem
        L = m.logit
        with nc.Block() as block:
            @block.gpsimd
            def _(pool):
                pool.memset(ones[:], 1.0).then_inc(S.rt_const, 1)
                pool.memset(tri[:], 1.0).then_inc(S.rt_c0, 1)
                pool.memset(keep[:], 1.0).then_inc(S.rt_c0, 1)
                pool.wait_ge(S.rt_c0, 2)
                pool.affine_select(out=tri[:, :], in_=tri[:, :], compare_op=ALU.is_ge, fill=0.0, base=0,
                                   pattern=[[1, TT]], channel_multiplier=-1).then_inc(S.rt_const, 1)
                pool.memset(keep[:, :, 0:1], 0.0).then_inc(S.rt_const, 1)
                pool.iota(iota_e[:, :], pattern=[[1, EX]], base=0, channel_multiplier=0, allow_small_or_imprecise_dtypes=True).then_inc(S.rt_const, 1)
                pool.iota(node[:, :], pattern=[[TT, NT]], base=EX * CAP, channel_multiplier=1, allow_small_or_imprecise_dtypes=True).then_inc(S.rt_const, 1)
                pool.wait_ge(S.slots_known, 1)
                for t in range(NT):
                    pool.indirect_dma_start(m.slots, bass.IndirectOffsetOnAxis(ap=put[:, t:t + 1].bitcast(U32), axis=0),
                                            m.h[:, t, :], None).then_inc(S.scattered, 16)
                pool.wait_ge(S.scattered, 16 * NT)

            @block.vector
            def _(dve):
                st = m.dve_steps.on(dve)
                st.link(dve.tensor_reduce(e1[:, :], L[:, :, :], X, ALU.max))
                st.link(dve.tensor_tensor(pr[:, :, :], L[:, :, :], spread(e1[:, :], 2, EX), ALU.subtract))
                dve.sem_inc(S.l_shifted, 1)
                dve.wait_ge(S.l_exp, 1)
                st.link(dve.tensor_reduce(e1[:, :], pr[:, :, :], X, ALU.add))
                st.link(dve.reciprocal(e1[:, :], e1[:, :]))
                st.link(dve.tensor_tensor(pr[:, :, :], pr[:, :, :], spread(e1[:, :], 2, EX), ALU.mult))
                st.link(dve.tensor_reduce(m.prb[:, :], pr[:, :, :], X, ALU.max))
                dve.wait_ge(S.rt_const, 5)
                st.link(dve.tensor_tensor(tmp[:, :, :], pr[:, :, :], spread(m.prb[:, :], 2, EX), ALU.is_equal))
                st.link(dve.tensor_scalar(tmp[:, :, :], tmp[:, :, :], -float(EX), float(EX), ALU.mult, ALU.add))
                st.link(dve.tensor_tensor(tmp[:, :, :], tmp[:, :, :], spread(iota_e[:, :], 1, NT), ALU.add))
                st.link(dve.tensor_reduce(eid[:, :], tmp[:, :, :], X, ALU.min))
                st.link(dve.tensor_tensor(hot[:, :, :], spread(iota_e[:, :], 1, NT), spread(eid[:, :], 2, EX), ALU.is_equal))
                dve.sem_inc(S.hot_ready, 1)
                dve.wait_ge(S.counted, 1)
                st.link(dve.tensor_copy(tot[:, :, :], pj[:, 0:NT * EX].rearrange("p (t e) -> p e t", e=EX)))
                st.link(dve.tensor_tensor_scan(run.rearrange("p e t -> p (e t)"), keep.rearrange("p e t -> p (e t)"),
                                               tot.rearrange("p e t -> p (e t)"), 0.0, ALU.mult, ALU.add))
                st.link(dve.tensor_tensor(run[:, :, :], run[:, :, :], tot[:, :, :], ALU.subtract))
                st.link(dve.tensor_tensor(tmp[:, :, :], run.rearrange("p e t -> p t e"), pi[:, 0:NT * EX].rearrange("p (t e) -> p t e", e=EX), ALU.add))
                st.link(dve.tensor_tensor(tmp[:, :, :], tmp[:, :, :], hot[:, :, :], ALU.mult))
                st.link(dve.tensor_reduce(pos[:, :], tmp[:, :, :], X, ALU.add))
                st.then(dve.tensor_scalar(kept[:, :], pos[:, :], float(CAP), None, ALU.is_le))
                st.link(dve.tensor_scalar(pos[:, :], pos[:, :], float(CAP), -1.0, ALU.min, ALU.add))
                st.link(dve.scalar_tensor_tensor(out=slot[:, :], in0=eid[:, :], scalar=float(CAP), in1=pos[:, :], op0=ALU.mult, op1=ALU.add))
                st.then(dve.tensor_copy(m.slot_i[:, :], slot[:, :]))
                st.then(dve.tensor_tensor(m.prb[:, :], m.prb[:, :], kept[:, :], ALU.mult))
                st.link(dve.tensor_tensor(e2[:, :], slot[:, :], node[:, :], ALU.subtract))
                st.link(dve.tensor_tensor(e2[:, :], e2[:, :], kept[:, :], ALU.mult))
                st.link(dve.tensor_tensor(e2[:, :], e2[:, :], node[:, :], ALU.add))
                st.link(dve.tensor_copy(put[:, :], e2[:, :]))
                dve.sem_inc(S.slots_known, 1)

            @block.scalar
            def _(act):
                act.wait_ge(S.l_shifted, 1)
                act.activation(pr[:, :, :], pr[:, :, :], ACT.Exp).then_inc(S.l_exp, 1)

            @block.tensor
            def _(pe):
                pe.wait_ge(S.rt_const, 5)
                pe.wait_ge(S.hot_ready, 1)
                pe.matmul(pi[:, 0:NT * EX], tri[:, :], flat(hot[:, :, :]), start=True, stop=True)
                pe.matmul(pj[:, 0:NT * EX], ones[:, :], flat(hot[:, :, :]), start=True, stop=True).then_inc(S.counted, 1)


def experts(nc, m, io):
    MT = -(-CAP // 128)
    sizes = [min(128, CAP - 128 * i) for i in range(MT)]
    FC = FF // 128
    with ExitStack() as ctx:
        def sb(n, s, d=F32):
            return ctx.enter_context(nc.sbuf_tensor(n, s, d))
        w1 = [sb(f"w1_{i}", [128, 2, FF]) for i in range(2)]
        w2 = [sb(f"w2_{i}", [128, FC, D]) for i in range(2)]
        b1n = sb("b1n", [EX * FC, 128])
        b1 = sb("b1", [128, EX, FC])
        b2 = [sb(f"b2_{i}", [128, D]) for i in range(2)]
        hb = [sb(f"hb_{i}", [128, MT, D]) for i in range(2)]
        hT = [sb(f"hT_{i}", [128, 2, 512]) for i in range(2)]
        hm = sb("hm", [128, FC, 512])
        yb = sb("yb", [128, MT, D])
        pt = [ctx.enter_context(nc.psum_tensor(f"xpt{i}", [128, 512], F32)) for i in range(2)]
        p1 = [ctx.enter_context(nc.psum_tensor(f"xp1{i}", [128, 512], F32)) for i in range(3)]
        p2 = [ctx.enter_context(nc.psum_tensor(f"xp2{i}", [128, 512], F32)) for i in range(3)]
        S = m.sem
        w1d = io.w1.rearrange("e (c p) f -> e p c f", p=128)
        w2d = io.w2.rearrange("e (c p) d -> e p c d", p=128)

        def rounds(eng, body, ends=False):
            for par in range(2):
                body(par, par, 0)
            with eng.Fori(1, EX // 2 - ends) as k:
                for par in range(2):
                    body(2 * k + par, par, k)
            if ends:
                for par in range(2):
                    body(EX - 2 + par, par, EX // 2 - 1)

        with nc.Block() as block:
            @block.sync
            def _(sp):
                def body(e, par, k):
                    wait(sp, S.y_stored, 64 * (e - 1) if not isinstance(e, int) else 0)
                    one = bass.ds(e, 1)
                    sp.dma_start(w1[par][:, :, :], w1d[one].squeeze(0)).then_inc(S.ex_in[par], 16)
                    sp.dma_start(hb[par][:, 0:MT - 1, :], m.slots[bass.ds(e * CAP, 128 * (MT - 1)), :].rearrange("(c p) d -> p c d", p=128)).then_inc(S.ex_in[par], 16)
                    sp.dma_start(hb[par][0:sizes[-1], MT - 1, :], m.slots[bass.ds(e * CAP + 128 * (MT - 1), sizes[-1]), :]).then_inc(S.ex_in[par], 16)
                    sp.dma_start(w2[par][:, :, :], w2d[one].squeeze(0)).then_inc(S.ex_in[par], 16)
                    sp.dma_start(b2[par][:, :], io.b2[one, :].to_broadcast([128, D])).then_inc(S.ex_in[par], 16)
                sp.dma_start(b1n[:, :], io.b1.rearrange("e (c p) -> (e c) p", p=128)).then_inc(S.b1_in, 16)
                rounds(sp, body)

            @block.scalar
            def _(act):
                act.wait_ge(S.b1_turned, 1)
                act.activation(b1.rearrange("p e c -> p (e c)"), p1[2][:, 0:EX * FC], ACT.Copy).then_inc(S.b1_made, 1)
                act.wait_ge(S.b1_made, 1)

                def turned(e, par):
                    for c in range(2):
                        act.wait_ge(S.hb_turned, 2 * e + c + 1)
                        act.activation(hT[par][:, c, 0:CAP], pt[c][:, 0:CAP], ACT.Copy).then_inc(S.hT_made, 1)
                turned(0, 0)

                def body(e, par, k):
                    for f in range(FC):
                        act.wait_ge(S.up_prod, FC * e + f + 1)
                        if f == 0:
                            wait(act, S.down_prod, MT * e)
                        act.activation(hm[:, f, 0:CAP], p1[f % 2][:, 0:CAP], ACT.Relu, bias=at(b1, e)[:, f:f + 1]).then_inc(S.hm_made, 1)
                    if not (isinstance(e, int) and e == EX - 1):
                        turned(e + 1, 1 - par)
                    for i in range(MT):
                        act.wait_ge(S.y_ready, MT * e + i + 1)
                        act.dma_start(m.y_d[bass.ds(e * CAP + 128 * i, sizes[i]), :], yb[0:sizes[i], i, :]).then_inc(S.y_stored, 16)
                rounds(act, body, True)
                act.wait_ge(S.y_stored, 16 * MT * EX)

            @block.vector
            def _(dve):
                def body(e, par, k):
                    wait(dve, S.y_stored, 16 * MT * e)
                    for i in range(MT):
                        dve.wait_ge(S.down_prod, MT * e + i + 1)
                        dve.tensor_tensor(yb[0:sizes[i], i, :], p2[i % 2][0:sizes[i], 0:D], b2[par][0:sizes[i], :], ALU.add).then_inc(S.y_ready, 1)
                rounds(dve, body)

            @block.tensor
            def _(pe):
                pe.wait_ge(S.b1_in, 16)
                pe.transpose(p1[2][:, 0:EX * FC], b1n[:, :], m.ident[0:EX * FC, 0:EX * FC]).then_inc(S.b1_turned, 1)

                def turn(e, par, k):
                    pe.wait_ge(S.ex_in[par], 80 * k + 80)
                    for c in range(2):
                        wait(pe, S.hT_made, 2 * e + c - 1)
                        for i in range(MT):
                            mm = pe.transpose(pt[c][:, 128 * i:128 * i + sizes[i]], hb[par][0:sizes[i], i, c * 128:(c + 1) * 128],
                                              m.ident[0:sizes[i], 0:sizes[i]])
                        mm.then_inc(S.hb_turned, 1)

                def body(e, par, k):
                    pe.wait_ge(S.hT_made, 2 * e + 2)
                    for f in range(FC):
                        wait(pe, S.hm_made, FC * e + f - 1)
                        for c in range(2):
                            mm = pe.matmul(p1[f % 2][:, 0:CAP], w1[par][:, c, f * 128:(f + 1) * 128], hT[par][:, c, 0:CAP], start=(c == 0), stop=(c == 1))
                        mm.then_inc(S.up_prod, 1)
                    if not (isinstance(e, int) and e == EX - 1):
                        turn(e + 1, 1 - par, k + par)
                    pe.wait_ge(S.hm_made, FC * e + FC)
                    for i in range(MT):
                        wait(pe, S.y_ready, MT * e + i - 1)
                        for f in range(FC):
                            mm = pe.matmul(p2[i % 2][0:sizes[i], 0:D], hm[:, f, 128 * i:128 * i + sizes[i]], w2[par][:, f, :],
                                           start=(f == 0), stop=(f == FC - 1))
                        mm.then_inc(S.down_prod, 1)
                turn(0, 0, 0)
                rounds(pe, body, True)


def combine(nc, m, out):
    size = 3
    groups = [range(a, min(a + size, NT)) for a in range(0, NT, size)]
    with ExitStack() as ctx:
        def sb(n, s, d=F32):
            return ctx.enter_context(nc.sbuf_tensor(n, s, d))
        y = sb("cb_y", [TT, NT, D])
        lo = [sb(f"cb_lo{i}", [TT, size, D]) for i in range(2)]
        hi = [sb(f"cb_hi{i}", [TT, size, D]) for i in range(2)]
        fin = [sb(f"cb_fin{i}", [TT, size, D], I32) for i in range(2)]
        S = m.sem
        with nc.Block() as block:
            @block.gpsimd
            def _(pool):
                for t in range(NT):
                    wait(pool, S.weighted, t - U + 1)
                    pool.indirect_dma_start(y[:, t, :], None, m.y_d,
                                            bass.IndirectOffsetOnAxis(ap=m.slot_i[:, t:t + 1].bitcast(U32), axis=0)).then_inc(S.arrived[t % U], 16)

            @block.scalar
            def _(act):
                for t in range(NT):
                    act.wait_ge(S.arrived[t % U], 16 * (CH + 1 + t // U))
                    act.activation(y[:, t, :], y[:, t, :], ACT.Copy, scale=m.prb[:, t:t + 1]).then_inc(S.weighted, 1)

            @block.vector
            def _(dve):
                st = m.dve_steps.on(dve)
                done = {}

                def step(g, k):
                    ts = groups[g]
                    r, n, p = slice(ts[0], ts[-1] + 1), len(ts), g % 2
                    l, h, f = lo[p][:, 0:n, :], hi[p][:, 0:n, :], fin[p][:, 0:n, :]
                    if k == 0:
                        dve.wait_ge(S.weighted, ts[-1] + 1)
                        wait(dve, S.out_made, g - 1)
                        st.then(dve.tensor_scalar(f, y[:, r, :], 0.0, 0.0, ALU.mult, ALU.is_equal))
                        st.then(dve.tensor_scalar(l, y[:, r, :], 0.0, -1.0e4, ALU.min, ALU.max))
                        st.then(dve.tensor_scalar(h, y[:, r, :], 0.0, 1.0e4, ALU.max, ALU.min))
                    elif k == 1:
                        dve.wait_ge(st.sem, done[g, 0])
                        st.then(dve.tensor_tensor(l, l, h, ALU.add))
                    elif k == 2:
                        dve.wait_ge(st.sem, done[g, 1])
                        st.then(dve.copy_predicated(l, f, y[:, r, :]))
                    else:
                        dve.wait_ge(st.sem, done[g, 2])
                        dve.tensor_tensor(m.base[:, r, :], m.base[:, r, :], l, ALU.add).then_inc(S.out_made, 1)
                    done[g, k] = st.c
                for g in range(len(groups) + 1):
                    for k in range(2):
                        if g < len(groups):
                            step(g, k)
                        if g:
                            step(g - 1, k + 2)

            @block.sync
            def _(sp):
                ot = out.rearrange("(t p) d -> p t d", p=TT)
                for g, ts in enumerate(groups):
                    r = slice(ts[0], ts[-1] + 1)
                    sp.wait_ge(S.out_made, g + 1)
                    sp.dma_start(ot[:, r, :], m.base[:, r, :]).then_inc(S.out_stored, 16)
                sp.wait_ge(S.out_stored, 16 * len(groups))


SEMS = """dve_step xr_made qr_made hr_made edges_in tbl_const last_in keys_out keys_made tbl_iota ident_zero ident_made
rows_known before_made rows_counted tbl_turned w_in b_in bo_in zero_made zero_out qkv_out mixv_one squared base_x
var_made std_made xn_made w_ready ss_made norm_made rms_made projected w_turned w_evac xn_turned xnT_made mix_out
mem_in la_const y_scaled kmax1 q_shifted kmax_turned kmax2 kmax_row kmax3 kmax_wide k_shifted mem_turned mem_ready
q_exp q_soft ctx_made cd_made cd_turned cdT_made wc_prod wc_made y_prod y_made y_squared yss_made ynorm_made yinv_made mk_exp
k_exp q_turned qT_made gate_in an_turned an_made out_prod x2_made x2_stats var2_made std2_made h_made logit_prod
anT_made rt_const rt_c0 slots_known scattered l_shifted l_exp b1_in b1_turned b1_made hot_ready counted
y_stored hb_turned up_prod hT_made down_prod hm_made y_ready weighted out_made out_stored first_in key_in q_whole q_rest
q_split borders_made costs_made loc_in hotT_made q_spread prod_made reduced sc_made sc_turned chain chain_pe chain_act
pv_made hot_abs hot_made summed added idx_ready at_const rescaled""".split()


class Signals:

    def __init__(self, names, new):
        (self.dve_step, self.xr_made, self.qr_made, self.hr_made, self.edges_in, self.tbl_const, self.last_in,
         self.keys_out, self.keys_made, self.tbl_iota, self.ident_zero, self.ident_made, self.rows_known,
         self.before_made, self.rows_counted, self.tbl_turned, self.w_in, self.b_in, self.bo_in, self.zero_made,
         self.zero_out, self.qkv_out, self.mixv_one, self.squared, self.base_x, self.var_made, self.std_made,
         self.xn_made, self.w_ready, self.ss_made, self.norm_made, self.rms_made, self.projected, self.w_turned,
         self.w_evac, self.xn_turned, self.xnT_made, self.mix_out, self.mem_in, self.la_const, self.y_scaled,
         self.kmax1, self.q_shifted, self.kmax_turned, self.kmax2, self.kmax_row, self.kmax3, self.kmax_wide,
         self.k_shifted, self.mem_turned, self.mem_ready, self.q_exp, self.q_soft, self.ctx_made, self.cd_made,
         self.cd_turned, self.cdT_made, self.wc_prod, self.wc_made, self.y_prod, self.y_made, self.y_squared,
         self.yss_made, self.ynorm_made, self.yinv_made, self.mk_exp, self.k_exp, self.q_turned, self.qT_made, self.gate_in,
         self.an_turned, self.an_made, self.out_prod, self.x2_made, self.x2_stats, self.var2_made, self.std2_made,
         self.h_made, self.logit_prod, self.anT_made, self.rt_const, self.rt_c0, self.slots_known,
         self.scattered, self.l_shifted, self.l_exp, self.b1_in, self.b1_turned, self.b1_made, self.hot_ready,
         self.counted, self.y_stored, self.hb_turned, self.up_prod, self.hT_made, self.down_prod, self.hm_made,
         self.y_ready, self.weighted, self.out_made, self.out_stored, self.first_in, self.key_in, self.q_whole, self.q_rest,
         self.q_split, self.borders_made, self.costs_made, self.loc_in, self.hotT_made, self.q_spread, self.prod_made, self.reduced,
         self.sc_made, self.sc_turned, self.chain, self.chain_pe, self.chain_act, self.pv_made,
         self.hot_abs, self.hot_made, self.summed, self.added, self.idx_ready, self.at_const, self.rescaled) = (new(n) for n in names)


class Inputs:
    def __init__(self, x, src, dst, Wq, bq, Wk, bk, Wv, bv, Wo, bo, w_qkv, mem_kv, w_out, b_out, g_out, g_pre, gate_w,
                 gate_b, w1, b1, w2, b2):
        self.x = x
        self.src = src
        self.dst = dst
        self.Wq = Wq
        self.bq = bq
        self.Wk = Wk
        self.bk = bk
        self.Wv = Wv
        self.bv = bv
        self.Wo = Wo
        self.bo = bo
        self.w_qkv = w_qkv
        self.mem_kv = mem_kv
        self.w_out = w_out
        self.b_out = b_out
        self.g_out = g_out
        self.g_pre = g_pre
        self.gate_w = gate_w
        self.gate_b = gate_b
        self.w1 = w1
        self.b1 = b1
        self.w2 = w2
        self.b2 = b2


class Mem:
    pass


def graph_layer(nc, io, out):
    m = Mem()

    def dram(n, s, d=F32):
        return nc.dram_tensor(n, s, d, kind="Internal").ap()
    m.edges = dram("edges_d", (EROWS, 256), I32)
    m.key = dram("key_d", (STEPS * 128 + 2,))
    m.loc = dram("loc_d", (STEPS, 128), BF16)
    m.kv_d = dram("kv_d", (N, KV))
    m.slots = dram("slots_d", (EX * CAP + N, D))
    m.y_d = dram("y_d", (EX * CAP, D))
    with ExitStack() as ctx:
        def sb(n, s, d=F32):
            return ctx.enter_context(nc.sbuf_tensor(n, s, d))

        def new(n):
            return ctx.enter_context(nc.semaphore(n))

        def several(n, count):
            return [new(f"{n}{i}") for i in range(count)]
        S = m.sem = Signals(SEMS, new)
        S.rows_in, S.x_in, S.kv_stored = several("rows_in", TG), several("x_in", 5), several("kv_stored", 2)
        S.arrived, S.ex_in = several("arrived", U), several("ex_in", 2)
        m.dve_steps = Steps(S.dve_step)
        m.base = sb("base", [TT, NT, D])
        m.ident = sb("ident", [128, 128])
        m.iota_w = sb("iota_w", [128, TT])
        m.iota_p = sb("iota_p", [128, 1])
        m.one_col = sb("one_col", [128, 1])
        m.pen_e = sb("pen_e", [128, CH, U])
        m.src_e = sb("src_e", [128, CH + 1, U], I32)
        m.win_of = sb("win_of", [1, CH, U], I32)
        m.idx = sb("idx", [128, 2, U], I32)
        m.nloc_e = sb("nloc_e", [128, CH, U])
        m.first_loc = sb("first_loc", [2, CH])
        m.edge_any = sb("edge_any", [128, CH, 2])
        m.woT = sb("woT", [128, 2, D])
        m.logit = sb("logit", [TT, NT, EX])
        m.prb = sb("prb", [TT, NT])
        m.slot_i = sb("slot_i", [TT, NT], I32)
        with ExitStack() as att:
            m.q3 = att.enter_context(nc.sbuf_tensor("q3", [TT, NT, 3, D], BF16))
            m.fwd = att.enter_context(nc.sbuf_tensor("fwd", [128, CH, 128], BF16))
            m.bwd = att.enter_context(nc.sbuf_tensor("bwd", [128, CH, 128], BF16))
            m.early = m.q3.rearrange("p t a d -> p (t a d)").bitcast(F32)
            m.slot0 = att.enter_context(nc.sbuf_tensor("slot0", [128, U, KV], F32))
            room = m.slot0.rearrange("p u c -> p (u c)")
            ends = np.cumsum([0, 2 * WALL, 3 * D, D, CH * 130, 4 * D])
            parts = [room[:, int(a):int(b)] for a, b in zip(ends, ends[1:])]
            m.wall = parts[0].rearrange("p (c n) -> p c n", c=2)
            m.bqkv, m.bo = parts[1][0:TT, :], parts[2][0:TT, :]
            m.keys = parts[3].rearrange("p (k e) -> p k e", k=CH)
            m.zero = parts[4]
            m.wnat = parts[3][:, 0:8 * D].rearrange("p (w c i) -> p w c i", w=4, c=2)
            m.sq = parts[3][0:TT, 8 * D:10 * D].rearrange("p (b d) -> p b d", b=2)
            with ExitStack() as mix:
                def keep(n, c):
                    return mix.enter_context(nc.sbuf_tensor(n, [TT, NT, c], F32))
                m.mixq, m.mixk, m.mixv, m.xn = keep("mixq", HID), keep("mixk", HID), keep("mixv", HID + 1), keep("xn", D)
                with ExitStack() as prep:
                    def ready(n, s):
                        return prep.enter_context(nc.sbuf_tensor(n, s, F32))
                    m.gpre, m.stats, m.rstd = ready("gpre", [128, 2]), ready("stats", [TT, NT, 6]), ready("rstd", [TT, NT])
                    m.mean, m.var, m.ss, m.rms = (ready(n, [TT, NT]) for n in ("mean", "var", "ss", "rms"))
                    edge_tables(nc, m, io)
                    project(nc, m)
                linear_attention(nc, m, io)
            m.agg = att.enter_context(nc.sbuf_tensor("agg", [TT, NT, H, VW], F32))
            attention(nc, m)
            m.h = m.q3.rearrange("p t a d -> p (t a d)")[:, 0:NT * 2 * D].bitcast(F32).rearrange("p (t d) -> p t d", t=NT)
            attention_out(nc, m, io)
            route(nc, m)
        experts(nc, m, io)
        combine(nc, m, out)


ARGS = {"x": "x", "src": "src", "dst": "dst", "Wq": "L0_gnn_Wq", "bq": "L0_gnn_bq", "Wk": "L0_gnn_Wk", "bk":
        "L0_gnn_bk", "Wv": "L0_gnn_Wv", "bv": "L0_gnn_bv", "Wo": "L0_gnn_Wo", "bo": "L0_gnn_bo", "w_qkv":
        "L0_mix_w_qkv", "mem_kv": "L0_mix_mem_kv", "w_out": "L0_mix_w_out", "b_out": "L0_mix_b_out", "g_out":
        "L0_mix_g_out", "g_pre": "L0_mix_g_pre", "gate_w": "L0_ffn_gate_w", "gate_b": "L0_ffn_gate_b", "w1":
        "L0_ffn_w1", "b1": "L0_ffn_b1", "w2": "L0_ffn_w2", "b2": "L0_ffn_b2"}


def kernel(**inputs):
    import concourse.bacc as _bacc
    from concourse.bass_utils import run_bass_kernel_spmd as _run

    nc = _bacc.Bacc("TRN2", target_bir_lowering=False, num_devices=1)
    arrays, params = {}, {}
    for short, name in ARGS.items():
        a = np.ascontiguousarray(inputs[name])
        arrays["in_" + short] = a
        params[short] = nc.dram_tensor("in_" + short, a.shape, mybir.dt.from_np(a.dtype), kind="ExternalInput").ap()
    out = nc.dram_tensor("out", (N, D), F32, kind="ExternalOutput").ap()
    graph_layer(nc, Inputs(**params), out)
    r = _run(nc, [arrays], core_ids=[0])
    return r.results[0]["out"]
```
